# Optimizing a Trainium2 kernel written in Bass

```python
import numpy as np
import jax
import jax.numpy as jnp

def _softmax(x, axis=-1):
    return jax.nn.softmax(x, axis=axis)
def _gelu(x):
    return jax.nn.gelu(x, approximate=True)
def _silu(x):
    return jax.nn.silu(x)
def _sigmoid(x):
    return jax.nn.sigmoid(x)
def _layernorm(x, axis=-1, eps=1e-5):
    m = jnp.mean(x, axis=axis, keepdims=True)
    v = jnp.var(x, axis=axis, keepdims=True)
    return (x - m) / jnp.sqrt(v + eps)
def _scatter_add(tgt, idx, src, axis=0):
    return tgt.at[idx].add(src)
def _segment_sum(src, seg, n):
    return jax.ops.segment_sum(src, seg, n)

kernel_name = 'mk_conv_preact_d2_conv_nchw192_114c9d'

def setup_inputs(seed: int = 0):
    np.random.seed(seed)
    _w = jnp.asarray
    def _rec_inputs():
        import jax
        import jax.numpy as jnp
        _gk = jax.random.key(seed)
        x = -0.0002221 + 1 * jax.random.normal(jax.random.fold_in(_gk, 1), (32, 192, 64, 64), jnp.float32)
        return x
    x = _rec_inputs()
    def _L0_conv_setup():
        import jax, jax.numpy as jnp
        import numpy as np
        BN_EPS = 1e-05
        key = jax.random.key(seed)
        ks = jax.random.split(key, 5)
        B, C, H, W = (32, 192, 64, 64)
        OC = 192
        x = jax.random.normal(ks[0], (B, C, H, W), dtype=jnp.float32)
        conv_w = jax.random.normal(ks[1], (OC, 2 * C), dtype=jnp.float32) * (1.0 / np.sqrt(2 * C))
        conv_b = jax.random.normal(ks[2], (OC,), dtype=jnp.float32) * 0.02
        bn_gamma = jnp.ones((OC,), dtype=jnp.float32)
        bn_beta = jnp.zeros((OC,), dtype=jnp.float32)
        return {'x': x, 'conv_w': conv_w, 'conv_b': conv_b, 'bn_gamma': bn_gamma, 'bn_beta': bn_beta, 'K': 8}
    _L0_conv_all = _L0_conv_setup()
    _L0_conv_in = {k: v for k, v in _L0_conv_all.items() if k in ('conv_w', 'conv_b', 'bn_gamma', 'bn_beta', )}
    del _L0_conv_all

    def _L1_conv_setup():
        import jax, jax.numpy as jnp
        import numpy as np
        import math
        C64 = jnp.complex64

        def _fftconv_full(a, kern):
            L = a.shape[-1] + kern.shape[0] - 1
            A = jnp.fft.fft(a, n=L, axis=-1)
            K = jnp.fft.fft(kern.astype(a.dtype), n=L)
            return jnp.fft.ifft(A * K, axis=-1)

        def _centered_ifft(f):
            N = f.shape[-1]
            shft = (np.arange(N) + int(np.fix(N / 2))) % N
            inv = np.argsort(shft)
            g = jnp.fft.ifft(f[..., shft], axis=-1) * math.sqrt(N)
            return g[..., inv].astype(f.dtype)

        def _sincinterp(f):
            N = f.shape[-1]
            y = jnp.zeros(f.shape[:-1] + (2 * N - 1,), f.dtype).at[..., ::2].set(f)
            kern = jnp.asarray(np.sinc(np.arange(-(2 * N - 3), 2 * N - 2) / 2.0).astype(np.complex64))
            return _fftconv_full(y, kern)[..., 2 * N - 3:4 * N - 4]

        def _frft_chirp(f, a):
            N = f.shape[-1]
            alpha = a * math.pi / 2
            tana2, sina = (math.tan(alpha / 2), math.sin(alpha))
            fi = _sincinterp(f)
            pad = jnp.zeros(f.shape[:-1] + (N - 1,), f.dtype)
            fp = jnp.concatenate([pad, fi, pad], axis=-1)
            n = np.arange(-2 * N + 2, 2 * N - 1).astype(np.float64)
            chrp = jnp.asarray(np.exp(-1j * math.pi / N * tana2 / 4 * n ** 2).astype(np.complex64))
            fp = chrp * fp
            c = math.pi / N / sina / 4
            m = np.arange(-(4 * N - 4), 4 * N - 3).astype(np.float64)
            kern = jnp.asarray(np.exp(1j * c * m ** 2).astype(np.complex64))
            ret = _fftconv_full(fp, kern)[..., 4 * N - 4:8 * N - 7] * math.sqrt(c / math.pi)
            ret = chrp * ret
            phase = np.complex64(np.exp(-1j * (1 - a) * math.pi / 4))
            return phase * ret[..., N - 1:3 * N - 2:2]

        def _frft_last(f, a):
            if a < 0.5:
                f = _centered_ifft(f)
                a = a + 1.0
            return _frft_chirp(f, a)

        def _frft2d(x, a):
            t = _frft_last(x, a)
            return jnp.swapaxes(_frft_last(jnp.swapaxes(t, -1, -2), a), -1, -2)

        def _c1x1(x, w, b=None):
            y = jnp.einsum('nchw,oc->nohw', x, w)
            return y if b is None else y + b[None, :, None, None]

        def _c3x3(x, w, b):
            y = jax.lax.conv_general_dilated(x, w, (1, 1), 'SAME', dimension_numbers=('NCHW', 'OIHW', 'NCHW'))
            return y + b[None, :, None, None]

        def _forward(x, conv1_w, mag_s_w, mag_s_b, mag_f_w, mag_f_b, mag_w, mag_b, pha_w, pha_b, conv_0_w, conv_0_b, conv_1_w, conv_1_b, conv2_w):
            angle = 0.5
            alpha = math.cos(angle * math.pi / 2)
            N, C, H, W = x.shape
            H1, W1 = (int(H * alpha), int(W * alpha))
            x1 = _c1x1(x, conv1_w)
            C1, C0 = (C // 4, C // 4 // 3)
            x_0, x_05, x_1 = (x1[:, :C0], x1[:, C0:C1 - C0], x1[:, C1 - C0:C1])
            h0, w0 = ((H - H1) // 2, (W - W1) // 2)
            mask1 = jnp.zeros((H, W), jnp.float32).at[h0:h0 + H1, w0:w0 + W1].set(1.0)
            mask2 = 1.0 - mask1
            Fre = _frft2d(x_05.astype(C64), angle)
            mag, pha = (jnp.abs(Fre), jnp.angle(Fre))
            mag_out = _c1x1(_c3x3(mag * mask1, mag_s_w, mag_s_b) * mask1 + _c1x1(mag * mask2, mag_f_w, mag_f_b) * mask2, mag_w, mag_b)
            pha_out = _c1x1(pha, pha_w, pha_b)
            Fre_out = jax.lax.complex(mag_out * jnp.cos(pha_out), mag_out * jnp.sin(pha_out))
            ifrft = jnp.abs(_frft2d(Fre_out, -angle))
            fre = jnp.fft.rfft2(x_1)
            fm, fp = (jnp.abs(fre), jnp.angle(fre))
            mo = _c1x1(fm, conv_1_w, conv_1_b)
            po = _c1x1(fp, conv_1_w, conv_1_b)
            x_1o = jnp.fft.irfft2(jax.lax.complex(mo * jnp.cos(po), mo * jnp.sin(po)), s=(H, W))
            x_0o = _c1x1(x_0, conv_0_w, conv_0_b)
            return _c1x1(jnp.concatenate([x_0o, ifrft, x_1o], axis=1), conv2_w)
        key = jax.random.key(seed)
        ks = jax.random.split(key, 16)
        N, C, H, W, Co = (4, 192, 128, 128, 192)
        C1, C0 = (C // 4, C // 4 // 3)
        Cm = C1 - 2 * C0
        s = 0.05
        r = lambda k, sh: jax.random.normal(k, sh, jnp.float32)
        return {'x': r(ks[0], (N, C, H, W)), 'conv1_w': r(ks[1], (C1, C)) * s, 'mag_s_w': r(ks[2], (Cm, Cm, 3, 3)) * s, 'mag_s_b': r(ks[3], (Cm,)) * s, 'mag_f_w': r(ks[4], (Cm, Cm)) * s, 'mag_f_b': r(ks[5], (Cm,)) * s, 'mag_w': r(ks[6], (Cm, Cm)) * s, 'mag_b': r(ks[7], (Cm,)) * s, 'pha_w': r(ks[8], (Cm, Cm)) * s, 'pha_b': r(ks[9], (Cm,)) * s, 'conv_0_w': r(ks[10], (C0, C0)) * s, 'conv_0_b': r(ks[11], (C0,)) * s, 'conv_1_w': r(ks[12], (C0, C0)) * s, 'conv_1_b': r(ks[13], (C0,)) * s, 'conv2_w': r(ks[14], (Co, C1)) * s}
    _L1_conv_all = _L1_conv_setup()
    _L1_conv_in = {k: v for k, v in _L1_conv_all.items() if k in ('conv1_w', 'mag_s_w', 'mag_s_b', 'mag_f_w', 'mag_f_b', 'mag_w', 'mag_b', 'pha_w', 'pha_b', 'conv_0_w', 'conv_0_b', 'conv_1_w', 'conv_1_b', 'conv2_w', )}
    del _L1_conv_all

    return {
        "x": x,
        "L0_conv_conv_w": _L0_conv_in["conv_w"],
        "L0_conv_conv_b": _L0_conv_in["conv_b"],
        "L0_conv_bn_gamma": _L0_conv_in["bn_gamma"],
        "L0_conv_bn_beta": _L0_conv_in["bn_beta"],
        "L1_conv_conv1_w": _L1_conv_in["conv1_w"],
        "L1_conv_mag_s_w": _L1_conv_in["mag_s_w"],
        "L1_conv_mag_s_b": _L1_conv_in["mag_s_b"],
        "L1_conv_mag_f_w": _L1_conv_in["mag_f_w"],
        "L1_conv_mag_f_b": _L1_conv_in["mag_f_b"],
        "L1_conv_mag_w": _L1_conv_in["mag_w"],
        "L1_conv_mag_b": _L1_conv_in["mag_b"],
        "L1_conv_pha_w": _L1_conv_in["pha_w"],
        "L1_conv_pha_b": _L1_conv_in["pha_b"],
        "L1_conv_conv_0_w": _L1_conv_in["conv_0_w"],
        "L1_conv_conv_0_b": _L1_conv_in["conv_0_b"],
        "L1_conv_conv_1_w": _L1_conv_in["conv_1_w"],
        "L1_conv_conv_1_b": _L1_conv_in["conv_1_b"],
        "L1_conv_conv2_w": _L1_conv_in["conv2_w"],
    }

def reference(x, L0_conv_conv_w, L0_conv_conv_b, L0_conv_bn_gamma, L0_conv_bn_beta, L1_conv_conv1_w, L1_conv_mag_s_w, L1_conv_mag_s_b, L1_conv_mag_f_w, L1_conv_mag_f_b, L1_conv_mag_w, L1_conv_mag_b, L1_conv_pha_w, L1_conv_pha_b, L1_conv_conv_0_w, L1_conv_conv_0_b, L1_conv_conv_1_w, L1_conv_conv_1_b, L1_conv_conv2_w):
    import jax
    import jax.numpy as jnp
    def _L0_conv_ref(x, conv_w, conv_b, bn_gamma, bn_beta, K):
        import jax, jax.numpy as jnp
        import numpy as np
        BN_EPS = 1e-05
        B, C, H, W = x.shape
        x_est = jnp.roll(x, shift=(-(H // 2), -(W // 2)), axis=(2, 3))
        norm = jnp.sum(jnp.abs(x - x_est), axis=1, keepdims=True)
        mean_dist = jnp.mean(norm, axis=(1, 2, 3), keepdims=True)
        std_dist = jnp.std(norm, axis=(1, 2, 3), keepdims=True, ddof=1)
        thresh = mean_dist - std_dist
        x_j = jnp.zeros_like(x)

        def accumulate(x_j, shift, axis):
            xr = jnp.roll(x, shift=-shift, axis=axis)
            dist = jnp.sum(jnp.abs(x - xr), axis=1, keepdims=True)
            mask = (dist < thresh).astype(x.dtype)
            return jnp.maximum(x_j, (xr - x) * mask)
        step = max(1, K)
        for i in range(step, H, step):
            x_j = accumulate(x_j, i, 2)
        for j in range(step, W, step):
            x_j = accumulate(x_j, j, 3)
        x_cat = jnp.concatenate([x, x_j], axis=1)
        y = jnp.einsum('bchw,oc->bohw', x_cat, conv_w) + conv_b[None, :, None, None]
        mu = jnp.mean(y, axis=(0, 2, 3), keepdims=True)
        var = jnp.var(y, axis=(0, 2, 3), keepdims=True)
        y_hat = (y - mu) * jax.lax.rsqrt(var + BN_EPS)
        y_bn = y_hat * bn_gamma[None, :, None, None] + bn_beta[None, :, None, None]
        return jax.nn.gelu(y_bn, approximate=False)

    def _L1_conv_ref(x, conv1_w, mag_s_w, mag_s_b, mag_f_w, mag_f_b, mag_w, mag_b, pha_w, pha_b, conv_0_w, conv_0_b, conv_1_w, conv_1_b, conv2_w):
        import jax, jax.numpy as jnp
        import numpy as np
        import math
        C64 = jnp.complex64

        def _fftconv_full(a, kern):
            L = a.shape[-1] + kern.shape[0] - 1
            A = jnp.fft.fft(a, n=L, axis=-1)
            K = jnp.fft.fft(kern.astype(a.dtype), n=L)
            return jnp.fft.ifft(A * K, axis=-1)

        def _centered_ifft(f):
            N = f.shape[-1]
            shft = (np.arange(N) + int(np.fix(N / 2))) % N
            inv = np.argsort(shft)
            g = jnp.fft.ifft(f[..., shft], axis=-1) * math.sqrt(N)
            return g[..., inv].astype(f.dtype)

        def _sincinterp(f):
            N = f.shape[-1]
            y = jnp.zeros(f.shape[:-1] + (2 * N - 1,), f.dtype).at[..., ::2].set(f)
            kern = jnp.asarray(np.sinc(np.arange(-(2 * N - 3), 2 * N - 2) / 2.0).astype(np.complex64))
            return _fftconv_full(y, kern)[..., 2 * N - 3:4 * N - 4]

        def _frft_chirp(f, a):
            N = f.shape[-1]
            alpha = a * math.pi / 2
            tana2, sina = (math.tan(alpha / 2), math.sin(alpha))
            fi = _sincinterp(f)
            pad = jnp.zeros(f.shape[:-1] + (N - 1,), f.dtype)
            fp = jnp.concatenate([pad, fi, pad], axis=-1)
            n = np.arange(-2 * N + 2, 2 * N - 1).astype(np.float64)
            chrp = jnp.asarray(np.exp(-1j * math.pi / N * tana2 / 4 * n ** 2).astype(np.complex64))
            fp = chrp * fp
            c = math.pi / N / sina / 4
            m = np.arange(-(4 * N - 4), 4 * N - 3).astype(np.float64)
            kern = jnp.asarray(np.exp(1j * c * m ** 2).astype(np.complex64))
            ret = _fftconv_full(fp, kern)[..., 4 * N - 4:8 * N - 7] * math.sqrt(c / math.pi)
            ret = chrp * ret
            phase = np.complex64(np.exp(-1j * (1 - a) * math.pi / 4))
            return phase * ret[..., N - 1:3 * N - 2:2]

        def _frft_last(f, a):
            if a < 0.5:
                f = _centered_ifft(f)
                a = a + 1.0
            return _frft_chirp(f, a)

        def _frft2d(x, a):
            t = _frft_last(x, a)
            return jnp.swapaxes(_frft_last(jnp.swapaxes(t, -1, -2), a), -1, -2)

        def _c1x1(x, w, b=None):
            y = jnp.einsum('nchw,oc->nohw', x, w)
            return y if b is None else y + b[None, :, None, None]

        def _c3x3(x, w, b):
            y = jax.lax.conv_general_dilated(x, w, (1, 1), 'SAME', dimension_numbers=('NCHW', 'OIHW', 'NCHW'))
            return y + b[None, :, None, None]

        def _forward(x, conv1_w, mag_s_w, mag_s_b, mag_f_w, mag_f_b, mag_w, mag_b, pha_w, pha_b, conv_0_w, conv_0_b, conv_1_w, conv_1_b, conv2_w):
            angle = 0.5
            alpha = math.cos(angle * math.pi / 2)
            N, C, H, W = x.shape
            H1, W1 = (int(H * alpha), int(W * alpha))
            x1 = _c1x1(x, conv1_w)
            C1, C0 = (C // 4, C // 4 // 3)
            x_0, x_05, x_1 = (x1[:, :C0], x1[:, C0:C1 - C0], x1[:, C1 - C0:C1])
            h0, w0 = ((H - H1) // 2, (W - W1) // 2)
            mask1 = jnp.zeros((H, W), jnp.float32).at[h0:h0 + H1, w0:w0 + W1].set(1.0)
            mask2 = 1.0 - mask1
            Fre = _frft2d(x_05.astype(C64), angle)
            mag, pha = (jnp.abs(Fre), jnp.angle(Fre))
            mag_out = _c1x1(_c3x3(mag * mask1, mag_s_w, mag_s_b) * mask1 + _c1x1(mag * mask2, mag_f_w, mag_f_b) * mask2, mag_w, mag_b)
            pha_out = _c1x1(pha, pha_w, pha_b)
            Fre_out = jax.lax.complex(mag_out * jnp.cos(pha_out), mag_out * jnp.sin(pha_out))
            ifrft = jnp.abs(_frft2d(Fre_out, -angle))
            fre = jnp.fft.rfft2(x_1)
            fm, fp = (jnp.abs(fre), jnp.angle(fre))
            mo = _c1x1(fm, conv_1_w, conv_1_b)
            po = _c1x1(fp, conv_1_w, conv_1_b)
            x_1o = jnp.fft.irfft2(jax.lax.complex(mo * jnp.cos(po), mo * jnp.sin(po)), s=(H, W))
            x_0o = _c1x1(x_0, conv_0_w, conv_0_b)
            return _c1x1(jnp.concatenate([x_0o, ifrft, x_1o], axis=1), conv2_w)
        return _forward(x, conv1_w, mag_s_w, mag_s_b, mag_f_w, mag_f_b, mag_w, mag_b, pha_w, pha_b, conv_0_w, conv_0_b, conv_1_w, conv_1_b, conv2_w)

    def _gn(v, G=32, eps=1e-5):
        B_, C_, H_, W_ = v.shape
        g = v.reshape(B_, G, C_ // G, H_, W_)
        m = jnp.mean(g, axis=(2, 3, 4), keepdims=True)
        s = jnp.var(g, axis=(2, 3, 4), keepdims=True)
        return ((g - m) / jnp.sqrt(s + eps)).reshape(v.shape)

    def _ln_c(v, eps=1e-6):
        m = jnp.mean(v, axis=1, keepdims=True)
        s = jnp.var(v, axis=1, keepdims=True)
        return (v - m) / jnp.sqrt(s + eps)

    def _ln_t(v, eps=1e-5):
        m = jnp.mean(v, axis=-1, keepdims=True)
        s = jnp.var(v, axis=-1, keepdims=True)
        return (v - m) / jnp.sqrt(s + eps)

    def _to_tokens(v):
        B_, C_, H_, W_ = v.shape
        return v.reshape(B_, C_, H_ * W_).transpose(0, 2, 1)
    def _from_tokens(t, like):
        B_, C_, H_, W_ = like.shape
        return t.transpose(0, 2, 1).reshape(B_, C_, H_, W_)

    x = x + _L0_conv_ref(_gn(x), L0_conv_conv_w, L0_conv_conv_b, L0_conv_bn_gamma, L0_conv_bn_beta, 8)
    x = x + _L1_conv_ref(_gn(x), L1_conv_conv1_w, L1_conv_mag_s_w, L1_conv_mag_s_b, L1_conv_mag_f_w, L1_conv_mag_f_b, L1_conv_mag_w, L1_conv_mag_b, L1_conv_pha_w, L1_conv_pha_b, L1_conv_conv_0_w, L1_conv_conv_0_b, L1_conv_conv_1_w, L1_conv_conv_1_b, L1_conv_conv2_w)
    return x


_drawn_inputs = setup_inputs


def setup_inputs(seed=0):
    import zlib

    import numpy as np

    out = dict(_drawn_inputs(seed))
    spreads = {'L0_conv_bn_gamma': (1.0, 0.2), 'L0_conv_bn_beta': (0.0, 0.1)}
    factors = {'L0_conv_conv_b': 64.0,
     'L1_conv_mag_s_w': 8.0,
     'L1_conv_mag_s_b': 8.0,
     'L1_conv_mag_f_w': 8.0,
     'L1_conv_mag_f_b': 8.0,
     'L1_conv_mag_w': 8.0,
     'L1_conv_mag_b': 8.0,
     'L1_conv_pha_w': 8.0,
     'L1_conv_pha_b': 64.0,
     'L1_conv_conv_0_b': 5.612,
     'L1_conv_conv_1_w': 2.708,
     'L1_conv_conv_1_b': 31.861,
     'L1_conv_conv_0_w': 2.789}
    for name, (base, spread) in spreads.items():
        noise = np.random.default_rng([zlib.crc32(name.encode()), seed]).standard_normal(out[name].shape)
        drawn = base * np.exp(spread * noise) if base else spread * noise
        out[name] = jnp.asarray(drawn.astype(out[name].dtype))
    for name, factor in factors.items():
        out[name] = (out[name] * factor).astype(out[name].dtype)
    return out
```

```python
import math

import numpy as np
import concourse.bass as bass
from concourse import mybir
from contextlib import ExitStack

F32 = mybir.dt.float32
ALU = mybir.AluOpType
ACT = mybir.ActivationFunctionType
AX = mybir.AxisListType

TP = 96
NT = 2
C = TP * NT
S = 64
HW = S * S
K = 8
NP = S // K
ROW = HW // NP
BIG = 1.0e30


def pairs_of_line():
    a = [(p, p + s) for s in (1, 2) for p in range(NP - s)]
    b = [(p, p + s) for s in range(3, NP) for p in range(NP - s)]
    return a, b


def layer0_conv(nc, sems, x, w0_d, b0_d, ident_d, group_d, imgsum_d, y_d, bn_d):
    B = x.shape[0]
    PAIRS = B // 2
    PA, PB = pairs_of_line()
    NA, NB = len(PA), len(PB)
    NL = 2 * NP
    xv = x.rearrange("b (t p) h w -> p b t (h w)", p=TP)
    yv = y_d.rearrange("b (t p) n -> p b t n", p=TP)

    with ExitStack() as ctx:
        def sb(name, shape):
            return ctx.enter_context(nc.sbuf_tensor(name, shape, F32))

        def ps(name, shape):
            return ctx.enter_context(nc.psum_tensor(name, shape, F32))

        def sem(name):
            return sems.enter_context(nc.semaphore(name))

        xraw = sb("xraw", [TP, NT, ROW])
        xc = sb("xc", [TP, NT, NP, NP, 2, K * K])
        xp = sb("xp", [128, NP * NP, C])
        best = sb("best", [128, NP * NP, C])
        diff = sb("diff", [128, NA + NB, C])
        xjc = sb("xjc", [TP, NT, NP, 2, S])
        ysb = sb("ysb", [TP, 2, NT, ROW])
        w0 = sb("w0", [TP, 4, C])
        b0 = sb("b0", [TP, NT])
        ident = sb("ident", [128, 128])
        group = sb("group", [TP, TP])
        imgsum = sb("imgsum", [128, 128])
        xst = sb("xst", [TP, 2 * NT, NP, 6])
        mv = sb("mv", [TP, 2 * NT, 2])
        gst = sb("gst", [TP, 2 * NT, 2])
        gtmp = sb("gtmp", [TP, 2 * NT])
        gstd = sb("gstd", [TP, 2 * NT])
        rstd = sb("rstd", [TP, 2 * NT])
        nbias = sb("nbias", [TP, 2 * NT])
        eps = sb("eps", [TP, 1])
        yst = xst[:, :, :, :].rearrange("p k a s -> p (k a s)").rearrange("p (o a s) -> p o a s", o=NT, s=6)
        ymv = sb("ymv", [TP, NT, 3])
        yagg = sb("yagg", [TP, NT, PAIRS, 3])
        ybn = sb("ybn", [TP, NT, 2])
        dist_e = sb("dist_e", [128, NP * NP // 2])
        esum = sb("esum", [128, 1])
        emean = sb("emean", [128, 1])
        esq = sb("esq", [128, 1])
        estd = sb("estd", [128, 1])
        thresh = sb("thresh", [128, 1])
        dist = sb("dist", [128, NA + NB])
        pen = sb("pen", [128, NA + NB])

        tps = [ps(f"tps{n}", [128, 2, 512]) for n in range(2)]
        yps = [ps(f"yps{n}", [TP, 512]) for n in range(2)]
        sps = ps("sps", [128, 16])

        const_loaded = sem("const_loaded")
        eps_set = sem("eps_set")
        x_loaded = sem("x_loaded")
        x_grouped = sem("x_grouped")
        xstat_done = sem("xstat_done")
        stat_step = sem("stat_step")
        chan_stats = sem("chan_stats")
        group_sums = sem("group_sums")
        group_var = sem("group_var")
        group_std = sem("group_std")
        norm_ready = sem("norm_ready")
        normed_dve = sem("normed_dve")
        normed_act = sem("normed_act")
        tp_filled = sem("tp_filled")
        evac_act = sem("evac_act")
        evac_dve = sem("evac_dve")
        edist_part = sem("edist_part")
        edist_mean = sem("edist_mean")
        edist_sq = sem("edist_sq")
        edist_var = sem("edist_var")
        edist_std = sem("edist_std")
        diff_a = sem("diff_a")
        diff_b = sem("diff_b")
        dist_a = sem("dist_a")
        dist_b = sem("dist_b")
        pen_a = sem("pen_a")
        pen_b = sem("pen_b")
        best_a = sem("best_a")
        best_b = sem("best_b")
        xj_done = sem("xj_done")
        y_filled = sem("y_filled")
        y_copied = sem("y_copied")
        y_counted = sem("y_counted")
        y_stored = sem("y_stored")
        bn_step = sem("bn_step")
        bn_ready = sem("bn_ready")
        bn_stored = sem("bn_stored")

        block = ctx.enter_context(nc.Block())

        def by_column(t):
            return t[:, :, :].rearrange("p (a b) c -> p a b c", b=NP)

        def line_of(t, along_rows, line, p0, n):
            v = by_column(t)
            if along_rows:
                return v[:, bass.ds(line, 1), p0:p0 + n, :].rearrange("p l n c -> p (l n) c")
            return v[:, p0:p0 + n, bass.ds(line, 1), :].rearrange("p n l c -> p n (l c)")

        STEPS = 5 + 3

        @block.sync
        def _(sp):
            def load_row(i, a):
                for img in range(2):
                    n, ni = sp.snap((i * NP + a) * 4 + 2 * img), sp.snap(2 * i + img)
                    sp.wait_ge(x_grouped, n)
                    sp.dma_start(xraw[:, :, :], xv[:, bass.ds(ni, 1), :, a * ROW:(a + 1) * ROW].rearrange("p b t n -> p (b t) n")
                                 ).then_inc(x_loaded, 16)

            def pair(i, more):
                for a in range(NP):
                    ni = sp.snap(2 * i)
                    sp.wait_ge(y_copied, i * (4 * NP) + 4 * (a + 1))
                    sp.dma_start(yv[:, bass.ds(ni, 2), :, a * ROW:(a + 1) * ROW], ysb[:, :, :, :]).then_inc(y_stored, 16)
                    if more:
                        load_row(i + 1, a)

            for dst, src in ((w0[:, :, :], w0_d), (b0[:, :], b0_d), (ident[:, :], ident_d),
                             (group[:, :], group_d), (imgsum[:, :], imgsum_d)):
                sp.dma_start(dst, src).then_inc(const_loaded, 16)
            for a in range(NP):
                load_row(0, a)
            if PAIRS > 1:
                with sp.Fori(0, PAIRS - 1) as i:
                    pair(i, True)
            pair(PAIRS - 1, False)
            sp.wait_ge(bn_ready, 1)
            sp.dma_start(bn_d, ybn[:, :, :]).then_inc(bn_stored, 16)
            sp.wait_ge(y_stored, 16 * NP * PAIRS)
            sp.wait_ge(bn_stored, 16)

        @block.gpsimd
        def _(pool):
            pool.memset(eps[:, :], 1e-5).then_inc(eps_set, 1)

            def line(i, along_rows, l):
                n = pool.snap(i * NL + (NP if along_rows else 0) + l)
                for half, s0, s1, ready, used, at in ((0, 1, 2, diff_a, dist_a, 0), (1, 3, 7, diff_b, dist_b, NA)):
                    pool.wait_ge(used, n)
                    for s in range(s0, s1 + 1):
                        m = NP - s
                        ins = pool.tensor_tensor(diff[:, at:at + m, :], line_of(xp, along_rows, l, s, m),
                                                 line_of(xp, along_rows, l, 0, m), ALU.subtract)
                        at += m
                    ins.then_inc(ready, 1)

            def finish(i, a):
                pool.wait_ge(best_b, (i * NL + NP + a + 1) * 2 * NB)
                r = best[:, :, :].rearrange("p (a b) c -> p a (b c)", b=NP)[:, bass.ds(a, 1), :].rearrange("p a n -> p (a n)")
                q = xp[:, :, :].rearrange("p (a b) c -> p a (b c)", b=NP)[:, bass.ds(a, 1), :].rearrange("p a n -> p (a n)")
                pool.tensor_tensor(r, r, q, ALU.subtract).then_inc(xj_done, 1)

            with pool.Fori(0, PAIRS) as i:
                pool.wait_ge(evac_act, i * (3 * NP) + NP)
                pool.wait_ge(evac_dve, i * NP + NP)
                line(i, False, 0)
                with pool.Fori(1, NP) as l:
                    line(i, False, l)
                for l in range(2):
                    line(i, True, l)
                with pool.Fori(2, NP) as l:
                    line(i, True, l)
                    finish(i, l - 2)
                for a in range(NP - 2, NP):
                    finish(i, a)

        @block.scalar
        def _(act):
            act.wait_ge(eps_set, 1)
            act.wait_ge(const_loaded, 16 * 5)

            def distances(i, along_rows, l):
                n = act.snap(i * NL + (NP if along_rows else 0) + l)
                for u0, m, ready, done, used in ((0, NA, diff_a, dist_a, pen_a), (NA, NB, diff_b, dist_b, pen_b)):
                    act.wait_ge(ready, n + 1)
                    act.wait_ge(used, n)
                    for u in range(u0, u0 + m):
                        ins = act.activation(diff[:, u, :], diff[:, u, :], ACT.Abs, accum_out=dist[:, u:u + 1])
                    ins.then_inc(done, 1)

            def finish(i, r, more):
                base = act.snap(i * (4 * NP) + 4 * r)
                fills = act.snap(i * (4 * NP) + 2 * NP + 2 * r)
                for t in range(NT):
                    act.wait_ge(tp_filled, fills + t + 1)
                    act.wait_ge(y_filled, base)
                    act.activation(xjc[:, t, :, :, :].rearrange("p b i n -> p (b i n)"),
                                   tps[t][0:TP, :, :].rearrange("p a n -> p (a n)"), ACT.Identity).then_inc(evac_act, 1)
                rows = act.snap(i * NP + r)
                act.wait_ge(y_stored, rows * 16)
                act.wait_ge(y_counted, base)
                for g in range(4):
                    img, o = divmod(g, NT)
                    act.wait_ge(y_filled, base + g + 1)
                    act.activation(ysb[:, img, o, :].rearrange("p (i b j) -> p b i j", i=K, b=NP),
                                   yps[g % 2][:, :].rearrange("p (b i j) -> p b i j", b=NP, i=K),
                                   ACT.Identity, bias=b0[:, o:o + 1]).then_inc(y_copied, 1)
                    if more and r > 0 and o == 0:
                        regroup(i + 1, r - 1, img)

            def regroup(i, a, img):
                act.wait_ge(x_loaded, (i * NP + a) * 32 + 16 * (img + 1))
                for t in range(NT):
                    act.activation(xc[:, t, a, :, img, :].rearrange("p b (i j) -> p b i j", i=K),
                                   xraw[:, t, :].rearrange("p (i b j) -> p b i j", i=K, b=NP),
                                   ACT.Identity).then_inc(x_grouped, 1)

            def pair(i, more):
                act.wait_ge(group_var, i + 1)
                act.activation(gstd[:, :], gst[:, :, 1], ACT.Sqrt, bias=eps[:, 0:1]).then_inc(group_std, 1)
                act.wait_ge(norm_ready, i + 1)
                for c in range(NP // 2):
                    for t in range(NT):
                        k = NT + t
                        px = xc[:, t, 2 * c:2 * c + 2, :, 1, :].rearrange("p a b n -> p (a b) n")
                        act.activation(px, px, ACT.Identity,
                                       scale=rstd[:, k:k + 1], bias=nbias[:, k:k + 1]).then_inc(normed_act, 1)
                for f in range(0, 2 * NP, 2):
                    act.wait_ge(tp_filled, i * (4 * NP) + f + 1)
                    if f == 0:
                        act.wait_ge(xj_done, i * NP)
                    act.activation(xp[:, 4 * f:4 * f + 4, :].rearrange("p (k g) c -> p k (g c)", k=2),
                                   tps[0][:, :, 0:2 * C], ACT.Identity).then_inc(evac_act, 1)
                distances(i, False, 0)
                act.wait_ge(edist_var, i + 1)
                act.activation(estd[:, :], sps[:, 9:10], ACT.Sqrt, scale=HW / (HW - 1)).then_inc(edist_std, 1)
                with act.Fori(1, NP) as l:
                    distances(i, False, l)
                for l in range(2):
                    distances(i, True, l)
                for l in range(2, NP):
                    distances(i, True, l)
                    finish(i, l - 2, more)
                for a in range(NP - 2, NP):
                    finish(i, a, more)
                if more:
                    for img in range(2):
                        regroup(i + 1, NP - 1, img)

            for a in range(NP):
                for img in range(2):
                    regroup(0, a, img)
            if PAIRS > 1:
                with act.Fori(0, PAIRS - 1) as i:
                    pair(i, True)
            pair(PAIRS - 1, False)

        @block.vector
        def _(dve):
            def line(i, along_rows, l):
                n = dve.snap(i * NL + (NP if along_rows else 0) + l)
                last = {}
                for half, us, off, made, done, known in ((0, PA, 0, pen_a, best_a, dist_a), (1, PB, NA, pen_b, best_b, dist_b)):
                    m = len(us)
                    dve.wait_ge(known, n + 1)
                    dve.wait_ge(done, n * 2 * m)
                    dve.tensor_scalar(pen[:, off:off + m], dist[:, off:off + m], thresh[:, 0:1], -BIG,
                                      ALU.is_ge, ALU.mult).then_inc(made, 1)
                    dve.wait_ge(made, n + 1)
                    at = dve.snap(n * 2 * m)
                    count = 0
                    todo = []
                    for s in sorted({q - p for p, q in us}):
                        todo += [(u, p, q) for u, (p, q) in enumerate(us) if q - p == s]
                        todo += [(u, q, p) for u, (p, q) in enumerate(us) if q - p == s]
                    for u, p, q in todo:
                        dst, cand = line_of(best, along_rows, l, p, 1), line_of(xp, along_rows, l, q, 1)
                        own = dst
                        if p in last:
                            sm, base, c = last[p]
                            dve.wait_ge(sm, base + c)
                        elif not along_rows:
                            own = line_of(xp, along_rows, l, p, 1)
                        dve.scalar_tensor_tensor(dst, cand, pen[:, off + u:off + u + 1], own,
                                                 ALU.add, ALU.max).then_inc(done, 1)
                        count += 1
                        last[p] = (done, at, count)

            def count_y(i, r):
                base = dve.snap(i * (4 * NP) + 4 * r)
                dve.wait_ge(y_copied, base + 4)
                for g in range(4):
                    img, o = divmod(g, NT)
                    dve.bn_stats(yst[:, o, bass.ds(2 * r + img, 1), :].rearrange("p a s -> p (a s)"),
                                 ysb[:, img, o, :]).then_inc(y_counted, 1)

            dve.wait_ge(const_loaded, 16 * 5)
            with dve.Fori(0, PAIRS) as i:
                steps = [0]

                def link(ins):
                    steps[0] += 1
                    ins.then_inc(stat_step, 1)
                    dve.wait_ge(stat_step, i * STEPS + steps[0])

                for a in range(NP):
                    dve.wait_ge(x_grouped, i * (4 * NP) + 4 * (a + 1))
                    for k in range(2 * NT):
                        dve.bn_stats(xst[:, k, a, :], xc[:, k % NT, a, :, k // NT, :]).then_inc(xstat_done, 1)
                dve.wait_ge(xstat_done, (i + 1) * (2 * NT * NP))
                dve.memset(gtmp[:, :], 0.0)
                for k in range(2 * NT):
                    ins = dve.bn_aggr(mv[:, k, :], xst[:, k, :, :].rearrange("p a s -> p (a s)"))
                link(ins)
                link(dve.tensor_tensor(gtmp[:, :], mv[:, :, 0], mv[:, :, 0], ALU.mult))
                dve.tensor_tensor(mv[:, :, 1], mv[:, :, 1], gtmp[:, :], ALU.add).then_inc(chan_stats, 1)
                dve.wait_ge(group_sums, i + 1)
                link(dve.tensor_copy(gst[:, :, :].rearrange("p k s -> p (k s)"), sps[0:TP, 0:4 * NT]))
                link(dve.tensor_tensor(gtmp[:, :], gst[:, :, 0], gst[:, :, 0], ALU.mult))
                dve.tensor_tensor(gst[:, :, 1], gst[:, :, 1], gtmp[:, :], ALU.subtract).then_inc(group_var, 1)
                dve.wait_ge(group_std, i + 1)
                link(dve.reciprocal(rstd[:, :], gstd[:, :]))
                dve.scalar_tensor_tensor(nbias[:, :], gst[:, :, 0], -1.0, rstd[:, :], ALU.mult, ALU.mult).then_inc(norm_ready, 1)
                for c in range(NP // 2):
                    for t in range(NT):
                        px = xc[:, t, 2 * c:2 * c + 2, :, 0, :].rearrange("p a b n -> p (a b) n")
                        dve.tensor_scalar(px, px, gst[:, t, 0:1], rstd[:, t:t + 1],
                                          ALU.subtract, ALU.mult).then_inc(normed_dve, 1)
                for f in range(1, 2 * NP, 2):
                    dve.wait_ge(tp_filled, i * (4 * NP) + f + 1)
                    if f == 1:
                        dve.wait_ge(xj_done, i * NP)
                    dve.tensor_copy(xp[:, 4 * f:4 * f + 4, :].rearrange("p (k g) c -> p k (g c)", k=2),
                                    tps[1][:, :, 0:2 * C]).then_inc(evac_dve, 1)
                dve.wait_ge(evac_act, i * (3 * NP) + NP)
                dve.wait_ge(evac_dve, i * NP + NP)
                h = NP // 2
                for a in range(h):
                    for b in (0, h):
                        ins = dve.tensor_tensor(best[:, a * NP + b:a * NP + b + h, :],
                                                xp[:, (a + h) * NP + h - b:(a + h) * NP + 2 * h - b, :],
                                                xp[:, a * NP + b:a * NP + b + h, :], ALU.subtract)
                link(ins)
                link(dve.tensor_reduce(dist_e[:, :], best[:, 0:NP * NP // 2, :], AX.X, ALU.add, apply_absolute_value=True))
                dve.tensor_reduce(esum[:, :], dist_e[:, :], AX.X, ALU.add).then_inc(edist_part, 1)
                dve.wait_ge(edist_mean, i + 1)
                link(dve.tensor_copy(emean[:, :], sps[:, 8:9]))
                dve.tensor_scalar(dist_e[:, :], dist_e[:, :], emean[:, 0:1], None, ALU.subtract).then_inc(edist_sq, 1)
                dve.wait_ge(edist_sq, i * 2 + 1)
                dve.tensor_tensor_reduce(out=dist_e[:, :], in0=dist_e[:, :], in1=dist_e[:, :], scale=1.0, scalar=0.0,
                                         op0=ALU.mult, op1=ALU.add, accum_out=esq[:, :]).then_inc(edist_sq, 1)
                dve.wait_ge(edist_std, i + 1)
                dve.tensor_tensor(thresh[:, :], emean[:, :], estd[:, :], ALU.subtract).then_inc(edist_part, 1)
                dve.wait_ge(edist_part, 2 * i + 2)
                assert steps[0] == STEPS, steps

                line(i, False, 0)
                with dve.Fori(1, NP) as l:
                    line(i, False, l)
                dve.wait_ge(best_b, (i * NL + NP) * 2 * NB)
                for l in range(2):
                    line(i, True, l)
                with dve.Fori(2, NP) as l:
                    line(i, True, l)
                    count_y(i, l - 2)
                for a in range(NP - 2, NP):
                    count_y(i, a)
                dve.wait_ge(y_counted, (i + 1) * (4 * NP))
                dve.memset(ymv[:, :, 0], float(2 * HW))
                for o in range(NT):
                    ins = dve.bn_aggr(ymv[:, o, 1:3], yst[:, o, :, :].rearrange("p a s -> p (a s)"))
                ins.then_inc(bn_step, 1)
                dve.wait_ge(bn_step, 1 + 2 * i)
                dve.tensor_copy(yagg[:, :, bass.ds(i, 1), 0:2].rearrange("p o a s -> p o (a s)"), ymv[:, :, 0:2])
                dve.tensor_scalar(yagg[:, :, bass.ds(i, 1), 2].rearrange("p o a -> p (o a)"), ymv[:, :, 2],
                                  float(2 * HW), None, ALU.mult).then_inc(bn_step, 1)
                dve.wait_ge(bn_step, 2 + 2 * i)
            for o in range(NT):
                ins = dve.bn_aggr(ybn[:, o, :], yagg[:, o, :, :].rearrange("p a s -> p (a s)"))
            ins.then_inc(bn_ready, 1)

        @block.tensor
        def _(pe):
            pe.wait_ge(const_loaded, 16 * 5)

            with pe.Fori(0, PAIRS) as i:
                pe.wait_ge(chan_stats, i + 1)
                pe.matmul(sps[0:TP, 0:4 * NT], group[:, :], mv[:, :, :].rearrange("p k s -> p (k s)"),
                          start=True, stop=True).then_inc(group_sums, 1)
                for f in range(2 * NP):
                    a = f // 2
                    if f % 4 == 0:
                        pe.wait_ge(normed_dve, i * NP + (f // 4 + 1) * NT)
                        pe.wait_ge(normed_act, i * NP + (f // 4 + 1) * NT)
                    if f % 2 == 0:
                        pe.wait_ge(evac_act, i * (3 * NP) + f // 2)
                    elif f > 1:
                        pe.wait_ge(evac_dve, i * NP + f // 2)
                    for g in range(4):
                        b = 4 * (f % 2) + g
                        for t in range(NT):
                            src = xc[:, t, a, b, :, :].rearrange("p k n -> p (k n)")
                            ins = pe.transpose(tps[f % 2][:, g // 2, (g % 2) * C + t * TP:(g % 2) * C + (t + 1) * TP],
                                               src, ident[0:TP, 0:TP])
                    ins.then_inc(tp_filled, 1)
                pe.wait_ge(edist_part, i * 2 + 1)
                pe.matmul(sps[:, 8:9], imgsum[:, :], esum[:, :], start=True, stop=True).then_inc(edist_mean, 1)
                pe.wait_ge(edist_sq, i * 2 + 2)
                pe.matmul(sps[:, 9:10], imgsum[:, :], esq[:, :], start=True, stop=True).then_inc(edist_var, 1)
                for a in range(NP):
                    pe.wait_ge(xj_done, i * NP + a + 1)
                    for t in range(NT):
                        if a == 0 and t == 1:
                            pe.wait_ge(evac_dve, i * NP + NP)
                        else:
                            pe.wait_ge(evac_act, i * (3 * NP) + NP + (2 * a - (1 - t) if a else 0))
                        for b in range(NP):
                            ins = pe.transpose(tps[t][0:TP, b // 4, (b % 4) * 128:(b % 4 + 1) * 128],
                                               best[:, a * NP + b, t * TP:(t + 1) * TP], ident[:, :])
                        ins.then_inc(tp_filled, 1)
                    for g in range(4):
                        img, o = divmod(g, NT)
                        n = 4 * a + g - 1
                        if n >= 0:
                            pe.wait_ge(y_copied, i * (4 * NP) + n)
                        else:
                            pe.wait_ge(y_copied, i * (4 * NP))
                        if g == 0:
                            pe.wait_ge(evac_act, i * (3 * NP) + NP + 2 * (a + 1))
                        for k in range(2 * NT):
                            t = k % NT
                            if k < NT:
                                rhs = xc[:, t, a, :, img, :]
                            else:
                                rhs = xjc[:, t, :, img, :]
                            ins = pe.matmul(yps[g % 2][:, :], w0[:, k, o * TP:(o + 1) * TP], rhs,
                                            start=(k == 0), stop=(k == 2 * NT - 1))
                        ins.then_inc(y_filled, 1)


CM = 16
C1 = 3 * CM
KW = S // 2 + 1
CH = HW // 8
NCH = HW // CH
H1 = int(S * math.cos(math.pi / 4))
H0 = (S - H1) // 2
FR = CM * S
RF = CM * KW
EW = FR + RF
BR = 8 * KW
BW = CH + BR
TWO_PI = 2 * math.pi
TWO_PI_HI = 6.28125
ROUND = 12582912.0
PIX = 2 * NT * NCH

FILLS = ([("s1f", c, "act" if c % 2 else "dve") for c in range(4)] + [("s1r", c, "act" if c % 2 else "dve") for c in range(4)]
         + [(n + p, c, e) for n in ("s2f", "s2r") for c in range(2) for p, e in (("_re", "act"), ("_im", "dve"))]
         + [(n, c, e) for c in range(2) for n, e in (("outer", "dve"), ("inner", "dve"), ("phase", "act"), ("rmod", "act"), ("rang", "act"), ("mod", "act"))]
         + [("s3f", c, "act" if c % 2 else "dve") for c in range(4)] + [("s3r", c, "act" if c % 2 else "dve") for c in range(4)]
         + [("s4f" + p, c, "act") for c in range(2) for p in ("_re", "_im")] + [("s4r", c, "dve") for c in range(2)])
NF = len(FILLS)
INDEX = {(n, c): k for k, (n, c, _) in enumerate(FILLS)}
TAKES = {e: sum(x == e for _, _, x in FILLS) for e in ("act", "dve")}
D_S1F, D_S1R, D_S2F, D_S2R, D_S3F, D_S3R, D_S4F, D_S4R, D_N = 0, 1, 2, 5, 8, 9, 10, 13, 15
M_TAP, M_UP, M_DOWN, M_OUTER, M_MOD, M_PHASE, M_REAL, M_N = 0, 9, 12, 15, 16, 17, 18, 19


def layer1(nc, sems, x, y_d, bn_d, affine_d, group_d, conv1_d, conv2_d, c0w_d, c0b_d, mix_d, bias_d, mask_d, dft_d, out,
           v_d, f_d, r_d, g_d, p_d, z_d):
    B = x.shape[0]
    PAIRS = B // 2
    xv = x.rearrange("b (t p) h w -> p b t (h w)", p=TP)
    ov = out.rearrange("b (t p) h w -> p b t (h w)", p=TP)
    yv = y_d.rearrange("b (t p) n -> p b t n", p=TP)

    with ExitStack() as ctx:
        def sb(name, shape):
            return ctx.enter_context(nc.sbuf_tensor(name, shape, F32))

        def ps(name, shape):
            return ctx.enter_context(nc.psum_tensor(name, shape, F32))

        def sem(name):
            return sems.enter_context(nc.semaphore("l1_" + name))

        x1 = [sb(f"x1_{n}", [TP, 2, NT, HW]) for n in range(2)]
        ych = [sb(f"ych{n}", [TP, CH]) for n in range(2)]
        vch = [sb(f"vch{n}", [C1, CH]) for n in range(2)]
        zch = [sb(f"zch{n}", [C1, CH]) for n in range(2)]
        ra, rb, rc = sb("ra", [128, 2 * EW]), sb("rb", [128, 6 * CH + 4 * BR]), sb("rc", [128, 2 * EW])
        xw = ra[:, 0:2 * FR].rearrange("p (c h) -> p c h", h=S)
        mod, ang = ra[:, 0:EW], ra[:, EW:2 * EW]
        mixu = ra[:, 0:2 * CH].rearrange("p (i r n) -> p i r n", i=2, r=8)
        mixt = ra[:, 2 * CH:2 * CH + 2 * 8 * H1].rearrange("p (i r n) -> p i r n", i=2, r=8)
        im2, re2 = ra[:, 0:2 * BW], ra[:, 2 * BW:4 * BW]
        zt = ra[:, 0:2 * FR].rearrange("p (c h) -> p c h", h=S)
        a1f = rb[:, 0:2 * FR].rearrange("p (c r n) -> p c r n", r=2, n=S)
        a1r = rb[:, 2 * FR:2 * FR + 2 * RF].rearrange("p (c r n) -> p c r n", r=2, n=KW)
        magb = rb[:, 0:2 * CH].rearrange("p (i n) -> p i n", i=2)
        magi = rb[:, 2 * CH:4 * CH].rearrange("p (i n) -> p i n", i=2)
        angb = rb[:, 4 * CH:6 * CH].rearrange("p (i n) -> p i n", i=2)
        rblk = rb[:, 6 * CH:6 * CH + 4 * BR].rearrange("p (i s n) -> p i s n", i=2, s=2)
        h1f = rb[:, 0:2 * FR].rearrange("p (c r n) -> p c r n", r=2, n=S)
        h1r = rb[:, 2 * FR:4 * FR].rearrange("p (c r n) -> p c r n", r=2, n=S)
        re, im = rc[:, 0:EW], rc[:, EW:2 * EW]
        mo = rc[:, 0:2 * BW].rearrange("p (i n) -> p i n", i=2)
        ph = rc[:, 2 * BW:4 * BW].rearrange("p (i n) -> p i n", i=2)
        gt = rc[:, 0:2 * FR].rearrange("p (i c n) -> p i c n", i=2, n=S)
        pt = rc[:, 2 * FR:2 * FR + 2 * RF].rearrange("p (i c n) -> p i c n", i=2, n=KW)
        sq = rc[:, 0:2 * FR].rearrange("p (r n) -> p r n", r=2)

        group = sb("l1_group", [TP, TP])
        conv1 = sb("conv1", [TP, NT, C1])
        conv1s = sb("conv1s", [TP, 2 * NT, C1])
        conv2 = sb("conv2", [C1, C])
        conv2a = sb("conv2a", [CM, C])
        c0w, c0b = sb("c0w", [CM, CM]), sb("c0b", [CM, 1])
        mix = sb("mix", [128, M_N, 128])
        bias = sb("bias", [128, 5])
        mask = sb("mask", [128, 2, 8, S])
        dft = sb("dft", [128, D_N, 128])
        bnp = sb("bnp", [TP, NT, 2])
        affine = sb("affine", [TP, 2, NT])
        bns = sb("bns", [TP, NT, 2])
        cbias = sb("cbias", [TP, NT])
        eps = sb("l1_eps", [TP, 1])
        half_pi = sb("half_pi", [128, 1])
        st = sb("st", [TP, 2 * NT, NCH, 6])
        mv = sb("l1_mv", [TP, 2 * NT, 2])
        gst = sb("l1_gst", [TP, 2 * NT, 2])
        gtmp = sb("l1_gtmp", [TP, 2 * NT])
        gstd = sb("l1_gstd", [TP, 2 * NT])
        rstd = sb("l1_rstd", [TP, 2 * NT])
        vbias = sb("vbias", [C1, 2])

        vps = [ps(f"vps{n}", [C1, CH]) for n in range(2)]
        ops = [ps(f"ops{n}", [TP, CH]) for n in range(2)]
        stage = [ps(f"stage{n}", [128, 512]) for n in range(3)]
        gps = ps("gps", [128, 512])

        const_loaded, eps_set, set_up, setup_sum = sem("const_loaded"), sem("eps_set"), sem("set_up"), sem("setup_sum")
        setup_step = sem("setup_step")
        x_loaded = sem("x_loaded")
        y_loaded = [sem(f"y_loaded{n}") for n in range(2)]
        gelu_done, x1_done, x1_counted, stat_step = sem("gelu_done"), sem("x1_done"), sem("x1_counted"), sem("stat_step")
        chan_stats, group_sums, group_var, group_std = sem("chan_stats"), sem("group_sums"), sem("group_var"), sem("group_std")
        w_scaled, vbias_sum, vbias_done = sem("w_scaled"), sem("vbias_sum"), sem("vbias_done")
        v_filled, v_copied = sem("v_filled"), sem("v_copied")
        v_stored = [sem(f"v_stored{n}") for n in range(2)]
        xw_loaded, filled = sem("xw_loaded"), sem("filled")
        taken = {"act": sem("taken_act"), "dve": sem("taken_dve")}
        squared, sq_summed, mod_done, ratio_done, atan_done = sem("squared"), sem("sq_summed"), sem("mod_done"), sem("ratio_done"), sem("atan_done")
        ew_step, ang_done, f_stored, f_loaded, masked = sem("ew_step"), sem("ang_done"), sem("f_stored"), sem("f_loaded"), sem("masked")
        mixed, turn_done, abs_done, sin_done, g_done = sem("mixed"), sem("turn_done"), sem("abs_done"), sem("sin_done"), sem("g_done")
        g_stored, g_loaded, z_squared, z_summed, z_abs, z_real = (sem("g_stored"), sem("g_loaded"), sem("z_squared"), sem("z_summed"),
                                                                  sem("z_abs"), sem("z_real"))
        z_stored = sem("z_stored")
        z_loaded = [sem(f"z_loaded{n}") for n in range(2)]
        o_filled, o_added, o_stored = sem("o_filled"), sem("o_added"), sem("o_stored")

        passed = {e: sem("passed_" + e) for e in ("sp", "pe")}

        block = ctx.enter_context(nc.Block())
        NCONST = 12

        def wait_fill(eng, i, k):
            eng.wait_ge(filled, i * NF + k + 1)

        def place(k):
            return k // (NT * NCH), (k // NCH) % NT, k % NCH

        def pairs_of(eng, body):
            if PAIRS > 2:
                with eng.Fori(0, PAIRS // 2 - 1) as j:
                    body(eng.snap(2 * j), 0, True)
                    body(eng.snap(2 * j + 1), 1, True)
            body(PAIRS - 2, 0, True)
            body(PAIRS - 1, 1, False)

        @block.sync
        def _(sp):
            def load_y(i, k0, k1):
                for k in range(k0, k1):
                    img, t, q = place(k)
                    ni, n = sp.snap(2 * i + img), sp.snap(i * PIX + max(k - 1, 0))
                    sp.wait_ge(x1_done, n)
                    sp.sem_inc(passed["sp"], 1)
                    sp.dma_start(ych[k % 2][:, :], yv[:, bass.ds(ni, 1), t, q * CH:(q + 1) * CH].rearrange("p b n -> p (b n)")
                                 ).then_inc(y_loaded[k % 2], 16)

            def load_x(i, slot):
                for img in range(2):
                    ni = sp.snap(2 * i + img)
                    sp.dma_start(x1[slot][:, img, :, :], xv[:, bass.ds(ni, 1), :, :].rearrange("p b t n -> p (b t) n")
                                 ).then_inc(x_loaded, 16)

            def chain(i, slot, more):
                b = [sp.snap(2 * i + img) for img in range(2)]
                rows = [slice(img * S, (img + 1) * S) for img in range(2)]
                n8, n1 = sp.snap(i * 128 + 128), sp.snap(i * 32)
                for n in range(2):
                    sp.wait_ge(v_stored[n], n8)
                    sp.sem_inc(passed["sp"], 1)
                sp.wait_ge(z_stored, n1)
                sp.sem_inc(passed["sp"], 1)
                for img in range(2):
                    sp.dma_start(xw[rows[img], :, :], v_d[bass.ds(b[img], 1), CM:C1, :].rearrange("b c (w h) -> w (b c) h", h=S)
                                 ).then_inc(xw_loaded, 16)
                if more:
                    sp.wait_ge(o_stored, n1)
                    sp.sem_inc(passed["sp"], 1)
                    load_x(i + 1, 1 - slot)
                    load_y(i + 1, 0, 2)
                done = sp.snap(i + 1)
                for s, part, ready in ((0, mod, mod_done), (1, ang, ang_done)):
                    sp.wait_ge(ready, done)
                    sp.sem_inc(passed["sp"], 1)
                    for img in range(2):
                        sp.dma_start(f_d[bass.ds(b[img], 1), s, :, :, :].rearrange("b c h w -> (b h) c w"),
                                     part[rows[img], 0:FR].rearrange("p (c n) -> p c n", n=S)).then_inc(f_stored, 16)
                        sp.dma_start(r_d[bass.ds(b[img], 1), s, :, :, :].rearrange("b c h w -> (b h) c w"),
                                     part[rows[img], FR:EW].rearrange("p (c n) -> p c n", n=KW)).then_inc(f_stored, 16)
                sp.wait_ge(f_stored, n8)
                sp.sem_inc(passed["sp"], 1)
                for img in range(2):
                    for s, dst in ((0, magb), (1, angb)):
                        sp.dma_start(dst[:, img, :], f_d[bass.ds(b[img], 1), s, :, :, :].rearrange("b c (k r) w -> (b c k) (r w)", r=8)
                                     ).then_inc(f_loaded, 16)
                        sp.dma_start(rblk[:, img, s, :], r_d[bass.ds(b[img], 1), s, :, :, :].rearrange("b c (k r) w -> (b c k) (r w)", r=8)
                                     ).then_inc(f_loaded, 16)
                if more:
                    load_y(i + 1, 2, 18)
                sp.wait_ge(g_done, done)
                sp.sem_inc(passed["sp"], 1)
                for img in range(2):
                    for ri, part in ((0, re2), (1, im2)):
                        sp.dma_start(g_d[bass.ds(b[img], 1), ri, :, :, :].rearrange("b c (k r) w -> (b c k) (r w)", r=8),
                                     part[:, img * BW:img * BW + CH]).then_inc(g_stored, 16)
                        sp.dma_start(p_d[bass.ds(b[img], 1), ri, :, :, :].rearrange("b c (k r) w -> (b c k) (r w)", r=8),
                                     part[:, img * BW + CH:(img + 1) * BW]).then_inc(g_stored, 16)
                sp.wait_ge(g_stored, n8)
                sp.sem_inc(passed["sp"], 1)
                for img in range(2):
                    for ri in range(2):
                        sp.dma_start(gt[rows[ri], img, :, :], g_d[bass.ds(b[img], 1), ri, :, :, :].rearrange("b c h w -> (b h) c w")
                                     ).then_inc(g_loaded, 16)
                        sp.dma_start(pt[rows[ri], img, :, :], p_d[bass.ds(b[img], 1), ri, :, :, :].rearrange("b c h w -> (b h) c w")
                                     ).then_inc(g_loaded, 16)
                if more:
                    load_y(i + 1, 18, PIX)
                sp.wait_ge(z_abs, done)
                sp.sem_inc(passed["sp"], 1)
                sp.wait_ge(z_real, done)
                sp.sem_inc(passed["sp"], 1)
                for img in range(2):
                    sp.dma_start(z_d[bass.ds(b[img], 1), :, :, :].rearrange("b c w h -> (b w) c h"), zt[rows[img], :, :]
                                 ).then_inc(z_stored, 16)
                n2 = sp.snap(i * 32 + 32)
                sp.wait_ge(z_stored, n2)
                sp.sem_inc(passed["sp"], 1)
                for j in range(2 * NCH):
                    img, q = divmod(j, NCH)
                    no = sp.snap(i * PIX + 2 * max(j - 1, 0))
                    sp.wait_ge(o_filled, no)
                    sp.sem_inc(passed["sp"], 1)
                    px = slice(q * CH, (q + 1) * CH)
                    sp.dma_start(zch[j % 2][0:CM, :], v_d[bass.ds(b[img], 1), 0:CM, px].rearrange("b c n -> (b c) n")
                                 ).then_inc(z_loaded[j % 2], 16)
                    sp.dma_start(zch[j % 2][CM:C1, :], z_d[bass.ds(b[img], 1), :, 8 * q:8 * q + 8, :].rearrange("b c w h -> (b c) (w h)")
                                 ).then_inc(z_loaded[j % 2], 16)
                for img in range(2):
                    na = sp.snap(i * PIX + 16 * (img + 1))
                    sp.wait_ge(o_added, na)
                    sp.sem_inc(passed["sp"], 1)
                    sp.dma_start(ov[:, bass.ds(b[img], 1), :, :].rearrange("p b t n -> p (b t) n"), x1[slot][:, img, :, :]
                                 ).then_inc(o_stored, 16)

            consts = [(group[:, :], group_d), (conv1[:, :, :], conv1_d), (conv2[:, :], conv2_d), (conv2a[:, :], conv2_d[0:CM, :]),
                      (c0w[:, :], c0w_d), (c0b[:, :], c0b_d), (mix[:, :, :], mix_d), (bias[:, :], bias_d),
                      (mask[:, :, :, :], mask_d), (dft[:, :, :], dft_d), (bnp[:, :, :], bn_d), (affine[:, :, :], affine_d)]
            for dst, src in consts:
                sp.dma_start(dst, src).then_inc(const_loaded, 16)
            assert len(consts) == NCONST
            load_x(0, 0)
            load_y(0, 0, PIX)
            pairs_of(sp, chain)
            sp.wait_ge(o_stored, 32 * PAIRS)

        @block.gpsimd
        def _(pool):
            pool.memset(eps[:, :], 1e-5).then_inc(eps_set, 1)
            pool.memset(half_pi[:, :], math.pi / 2).then_inc(eps_set, 1)

            def add(i, slot):
                pool.wait_ge(x_loaded, 32 * i + 32)
                for k in range(PIX):
                    img, t, q = place(k)
                    dst = x1[slot][:, img, t, q * CH:(q + 1) * CH]
                    pool.wait_ge(gelu_done, i * PIX + k + 1)
                    pool.tensor_tensor(dst, dst, ych[k % 2][:, :], ALU.add).then_inc(x1_done, 1)

            def chain(i, slot, more):
                if more:
                    add(i + 1, 1 - slot)

            add(0, 0)
            pairs_of(pool, chain)

        @block.scalar
        def _(act):
            def take(i, k, out_ap, in_ap, func=ACT.Identity, **kw):
                wait_fill(act, i, k)
                act.activation(out_ap, in_ap, func, **kw).then_inc(taken["act"], 1)

            def gelu(i, k0, k1):
                for k in range(k0, k1):
                    img, t, q = place(k)
                    act.wait_ge(y_loaded[k % 2], i * (8 * PIX) + 16 * (k // 2 + 1))
                    act.activation(ych[k % 2][:, :], ych[k % 2][:, :], ACT.Gelu, scale=bns[:, t, 0:1], bias=bns[:, t, 1:2]
                                   ).then_inc(gelu_done, 1)

            def copy_v(i):
                act.wait_ge(vbias_done, i + 1)
                for k in range(2 * NCH):
                    img, q = divmod(k, NCH)
                    act.wait_ge(v_filled, i * (2 * NCH) + k + 1)
                    act.wait_ge(v_stored[k % 2], i * 128 + 16 * (k // 2))
                    act.activation(vch[k % 2][:, :], vps[k % 2][:, :], ACT.Identity, bias=vbias[:, img:img + 1]).then_inc(v_copied, 1)
                    ni, n = act.snap(2 * i + img), act.snap(i * (2 * NCH) + k + 1)
                    act.wait_ge(v_copied, n)
                    act.dma_start(v_d[bass.ds(ni, 1), :, q * CH:(q + 1) * CH].rearrange("b c n -> (b c) n"), vch[k % 2][:, :]
                                  ).then_inc(v_stored[k % 2], 16)

            def group_root(i):
                act.wait_ge(group_var, i + 1)
                act.activation(gstd[:, :], gst[:, :, 1], ACT.Sqrt, bias=eps[:, 0:1]).then_inc(group_std, 1)

            def chain(i, slot, more):
                for n, dst, w in (("s1f", a1f, 512), ("s1r", a1r, 8 * KW)):
                    for c in (1, 3):
                        k = INDEX[n, c]
                        take(i, k, dst[:, 4 * c:4 * c + 4, :, :].rearrange("p c r n -> p (c r n)"), stage[k % 3][:, 0:w])
                for n, off, w in (("s2f", 0, 512), ("s2r", FR, 8 * KW)):
                    for c in range(2):
                        k = INDEX[n + "_re", c]
                        take(i, k, re[:, off + c * w:off + (c + 1) * w], stage[k % 3][:, 0:w])
                act.wait_ge(taken["act"], i * TAKES["act"] + 8)
                act.activation(mod, re, ACT.Square).then_inc(squared, 1)
                act.wait_ge(taken["dve"], i * TAKES["dve"] + 8)
                act.activation(ang, im, ACT.Square).then_inc(squared, 1)
                act.wait_ge(sq_summed, i + 1)
                act.activation(ang, re, ACT.Abs)
                act.activation(mod, mod, ACT.Sqrt).then_inc(mod_done, 1)
                act.wait_ge(ratio_done, i + 1)
                act.activation(ang, ang, ACT.Arctan).then_inc(atan_done, 1)
                if more:
                    gelu(i + 1, 0, 16)
                for img in range(2):
                    for n, dst, w, kw in (("phase", ph[:, img, 0:CH], CH, dict(scale=2.0, bias=bias[:, 3:4])),
                                          ("rmod", mo[:, img, CH:BW], BR, dict(bias=bias[:, 4:5])),
                                          ("rang", ph[:, img, CH:BW], BR, dict(scale=2.0, bias=bias[:, 4:5])),
                                          ("mod", mo[:, img, 0:CH], CH, dict(bias=bias[:, 2:3]))):
                        k = INDEX[n, img]
                        take(i, k, dst, stage[k % 3][:, 0:w], **kw)
                act.wait_ge(turn_done, i + 1)
                act.activation(re2, im2, ACT.Abs).then_inc(abs_done, 1)
                act.wait_ge(abs_done, 2 * i + 1)
                act.activation(re2, re2, ACT.Sin, scale=-1.0, bias=half_pi[:, 0:1]).then_inc(sin_done, 1)
                act.activation(im2, im2, ACT.Sin).then_inc(sin_done, 1)
                act.wait_ge(sin_done, 2 * i + 2)
                act.activation(eps[:, 0:1], eps[:, 0:1], ACT.Identity).then_inc(abs_done, 1)
                if more:
                    gelu(i + 1, 16, PIX)
                for n, dst, p in (("s3f", h1f, 128), ("s3r", h1r, KW)):
                    for c in (1, 3):
                        k = INDEX[n, c]
                        wait_fill(act, i, k)
                        if p == 128:
                            act.activation(dst[:, 4 * c:4 * c + 4, :, :].rearrange("p c r n -> p (c r n)"), stage[k % 3][:, :],
                                           ACT.Identity).then_inc(taken["act"], 1)
                        else:
                            for img in range(2):
                                rows = slice(img * S, img * S + KW)
                                ins = act.activation(dst[rows, 4 * c:4 * c + 4, :, :].rearrange("p c r n -> p (c r n)"),
                                                     stage[k % 3][rows, :], ACT.Identity)
                            ins.then_inc(taken["act"], 1)
                for c in range(2):
                    for r, n in enumerate(("s4f_re", "s4f_im")):
                        k = INDEX[n, c]
                        take(i, k, sq[:, r, c * 512:(c + 1) * 512], stage[k % 3][:, :], ACT.Square)
                act.wait_ge(z_summed, i + 1)
                act.activation(zt[:, 0:CM, :].rearrange("p c n -> p (c n)"), sq[:, 0, :], ACT.Sqrt).then_inc(z_abs, 1)
                if more:
                    group_root(i + 1)
                    copy_v(i + 1)

            act.wait_ge(eps_set, 2)
            act.wait_ge(const_loaded, 16 * NCONST)
            act.activation(bns[:, :, 0], bnp[:, :, 1], ACT.Sqrt, bias=eps[:, 0:1]).then_inc(set_up, 1)
            act.wait_ge(set_up, 3)
            gelu(0, 0, PIX)
            group_root(0)
            copy_v(0)
            pairs_of(act, chain)

        @block.vector
        def _(dve):
            count = {"ew": 0, "stat": 0}
            EW_STEPS, STAT_STEPS = 10, 6

            def link(ins, i, what):
                count[what] += 1
                s, n = (ew_step, EW_STEPS) if what == "ew" else (stat_step, STAT_STEPS)
                ins.then_inc(s, 1)
                dve.wait_ge(s, i * n + count[what])

            def take(i, k, out_ap, in_ap):
                wait_fill(dve, i, k)
                dve.tensor_copy(out_ap, in_ap).then_inc(taken["dve"], 1)

            def stats(i, slot, k0, k1):
                for k in range(k0, k1):
                    img, t, q = place(k)
                    dve.wait_ge(x1_done, i * PIX + k + 1)
                    dve.bn_stats(st[:, img * NT + t, q, :], x1[slot][:, img, t, q * CH:(q + 1) * CH]).then_inc(x1_counted, 1)

            def group_stats(i):
                count["stat"] = 0
                dve.wait_ge(x1_counted, (i + 1) * PIX)
                dve.memset(gtmp[:, :], 0.0)
                for k in range(2 * NT):
                    ins = dve.bn_aggr(mv[:, k, :], st[:, k, :, :].rearrange("p a s -> p (a s)"))
                link(ins, i, "stat")
                link(dve.tensor_tensor(gtmp[:, :], mv[:, :, 0], mv[:, :, 0], ALU.mult), i, "stat")
                dve.tensor_tensor(mv[:, :, 1], mv[:, :, 1], gtmp[:, :], ALU.add).then_inc(chan_stats, 1)
                dve.wait_ge(group_sums, i + 1)
                link(dve.tensor_copy(gst[:, :, :].rearrange("p k s -> p (k s)"), gps[0:TP, 0:4 * NT]), i, "stat")
                link(dve.tensor_tensor(gtmp[:, :], gst[:, :, 0], gst[:, :, 0], ALU.mult), i, "stat")
                dve.tensor_tensor(gst[:, :, 1], gst[:, :, 1], gtmp[:, :], ALU.subtract).then_inc(group_var, 1)
                dve.wait_ge(group_std, i + 1)
                link(dve.reciprocal(rstd[:, :], gstd[:, :]), i, "stat")
                for k in range(2 * NT):
                    ins = dve.tensor_scalar(conv1s[:, k, :], conv1[:, k % NT, :], rstd[:, k:k + 1], None, ALU.mult)
                ins.then_inc(w_scaled, 1)
                dve.wait_ge(vbias_sum, i + 1)
                link(dve.tensor_scalar(vbias[:, :], gps[0:C1, 16:18], -1.0, None, ALU.mult), i, "stat")
                dve.tensor_copy(gtmp[:, 0:1], rstd[:, 0:1]).then_inc(vbias_done, 1)
                assert count["stat"] == STAT_STEPS

            def chain(i, slot, more):
                count["ew"] = 0
                for n, dst, w in (("s1f", a1f, 512), ("s1r", a1r, 8 * KW)):
                    for c in (0, 2):
                        k = INDEX[n, c]
                        take(i, k, dst[:, 4 * c:4 * c + 4, :, :].rearrange("p c r n -> p (c r n)"), stage[k % 3][:, 0:w])
                for n, off, w in (("s2f", 0, 512), ("s2r", FR, 8 * KW)):
                    for c in range(2):
                        k = INDEX[n + "_im", c]
                        take(i, k, im[:, off + c * w:off + (c + 1) * w], stage[k % 3][:, 0:w])
                dve.wait_ge(squared, 2 * i + 2)
                dve.tensor_tensor(mod, mod, ang, ALU.add).then_inc(sq_summed, 1)
                dve.wait_ge(mod_done, i + 1)
                link(dve.scalar_tensor_tensor(ang, ang, 1e-30, mod, ALU.max, ALU.add), i, "ew")
                link(dve.reciprocal(ang, ang), i, "ew")
                dve.tensor_tensor(ang, im, ang, ALU.mult).then_inc(ratio_done, 1)
                dve.wait_ge(ratio_done, i + 1)
                link(dve.tensor_scalar(im, im, 0.0, -0.5, ALU.is_ge, ALU.add), i, "ew")
                dve.wait_ge(atan_done, i + 1)
                link(dve.scalar_tensor_tensor(im, ang, -2.0 / math.pi, im, ALU.mult, ALU.add), i, "ew")
                link(dve.scalar_tensor_tensor(re, re, 0.0, im, ALU.is_lt, ALU.mult), i, "ew")
                dve.scalar_tensor_tensor(ang, re, math.pi, ang, ALU.mult, ALU.add).then_inc(ang_done, 1)
                dve.wait_ge(f_loaded, (i + 1) * 128)
                for img in range(2):
                    ins = dve.tensor_tensor(magi[:, img, :], magb[:, img, :], mask[:, 0, :, :].rearrange("p r n -> p (r n)"), ALU.mult)
                link(ins, i, "ew")
                for img in range(2):
                    ins = dve.tensor_tensor(magb[:, img, :], magb[:, img, :], mask[:, 1, :, :].rearrange("p r n -> p (r n)"), ALU.mult)
                ins.then_inc(masked, 1)
                inner = slice(H0, H0 + H1)
                for img in range(2):
                    k = INDEX["outer", img]
                    wait_fill(dve, i, k)
                    dve.scalar_tensor_tensor(mixu[:, img, :, :].rearrange("p r n -> p (r n)"), stage[k % 3][:, :], bias[:, 1:2],
                                             mask[:, 1, :, :].rearrange("p r n -> p (r n)"), ALU.add, ALU.mult).then_inc(taken["dve"], 1)
                    k = INDEX["inner", img]
                    wait_fill(dve, i, k)
                    dve.scalar_tensor_tensor(mixt[:, img, :, :], stage[k % 3][:, 0:8 * H1].rearrange("p (r n) -> p r n", n=H1),
                                             bias[:, 0:1], mask[:, 0, :, inner], ALU.add, ALU.mult).then_inc(taken["dve"], 1)
                    dve.wait_ge(taken["dve"], i * TAKES["dve"] + 8 + 2 * (img + 1))
                    dve.tensor_tensor(mixu[:, img, :, inner], mixu[:, img, :, inner], mixt[:, img, :, :], ALU.add).then_inc(mixed, 1)
                if more:
                    stats(i + 1, 1 - slot, 0, 16)
                dve.wait_ge(taken["act"], i * TAKES["act"] + 16)
                phf, mof = ph[:, :, :].rearrange("p i n -> p (i n)"), mo[:, :, :].rearrange("p i n -> p (i n)")
                link(dve.tensor_scalar(im2, phf, 1.0 / TWO_PI, ROUND, ALU.mult, ALU.add), i, "ew")
                link(dve.tensor_scalar(im2, im2, ROUND, None, ALU.subtract), i, "ew")
                link(dve.scalar_tensor_tensor(re2, im2, -TWO_PI_HI, phf, ALU.mult, ALU.add), i, "ew")
                link(dve.scalar_tensor_tensor(im2, im2, -(TWO_PI - TWO_PI_HI), re2, ALU.mult, ALU.add), i, "ew")
                dve.tensor_scalar(im2, im2, 3.1415925, -3.1415925, ALU.min, ALU.max).then_inc(turn_done, 1)
                dve.wait_ge(sin_done, 2 * i + 2)
                dve.tensor_tensor(re2, re2, mof, ALU.mult)
                dve.tensor_tensor(im2, im2, mof, ALU.mult).then_inc(g_done, 1)
                for n, dst, p in (("s3f", h1f, 128), ("s3r", h1r, KW)):
                    for c in (0, 2):
                        k = INDEX[n, c]
                        wait_fill(dve, i, k)
                        if p == 128:
                            dve.tensor_copy(dst[:, 4 * c:4 * c + 4, :, :].rearrange("p c r n -> p (c r n)"), stage[k % 3][:, :]
                                            ).then_inc(taken["dve"], 1)
                        else:
                            for img in range(2):
                                rows = slice(img * S, img * S + KW)
                                ins = dve.tensor_copy(dst[rows, 4 * c:4 * c + 4, :, :].rearrange("p c r n -> p (c r n)"),
                                                      stage[k % 3][rows, :])
                            ins.then_inc(taken["dve"], 1)
                for c in range(2):
                    k = INDEX["s4r", c]
                    wait_fill(dve, i, k)
                    dve.tensor_copy(zt[:, CM + 8 * c:CM + 8 * c + 8, :].rearrange("p c n -> p (c n)"), stage[k % 3][:, :]
                                    ).then_inc(taken["dve"], 1)
                dve.wait_ge(taken["dve"], (i + 1) * TAKES["dve"])
                dve.tensor_copy(gtmp[:, 0:1], rstd[:, 0:1]).then_inc(z_real, 1)
                dve.wait_ge(taken["act"], (i + 1) * TAKES["act"])
                dve.tensor_tensor(sq[:, 0, :], sq[:, 0, :], sq[:, 1, :], ALU.add).then_inc(z_summed, 1)
                if more:
                    stats(i + 1, 1 - slot, 16, PIX)
                    group_stats(i + 1)
                for j in range(2 * NCH):
                    img, q = divmod(j, NCH)
                    for t in range(NT):
                        dve.wait_ge(o_filled, i * PIX + 2 * j + t + 1)
                        dst = x1[slot][:, img, t, :].rearrange("p (h w) -> p w h", w=S)[:, 8 * q:8 * q + 8, :]
                        dve.scalar_tensor_tensor(dst, ops[t][:, :].rearrange("p (w h) -> p w h", h=S), cbias[:, t:t + 1], dst,
                                                 ALU.add, ALU.add).then_inc(o_added, 1)
                print("ew steps", count["ew"]) if count["ew"] != EW_STEPS else None

            dve.wait_ge(set_up, 1)
            dve.reciprocal(bns[:, :, 0], bns[:, :, 0]).then_inc(setup_step, 1)
            dve.wait_ge(setup_step, 1)
            dve.tensor_tensor(bns[:, :, 0], bns[:, :, 0], affine[:, 0, :], ALU.mult).then_inc(setup_step, 1)
            dve.wait_ge(setup_step, 2)
            dve.tensor_tensor(bns[:, :, 1], bns[:, :, 0], bnp[:, :, 0], ALU.mult).then_inc(setup_step, 1)
            dve.wait_ge(setup_step, 3)
            dve.tensor_tensor(bns[:, :, 1], affine[:, 1, :], bns[:, :, 1], ALU.subtract).then_inc(set_up, 1)
            dve.wait_ge(setup_sum, 1)
            dve.tensor_copy(conv2[0:CM, :], gps[0:CM, 32:32 + C])
            dve.tensor_copy(cbias[:, :], gps[0:TP, 20:22]).then_inc(set_up, 1)
            stats(0, 0, 0, PIX)
            group_stats(0)
            pairs_of(dve, chain)

        @block.tensor
        def _(pe):
            def fill(i, k, products):
                before = k - 3
                if before >= 0:
                    e = FILLS[before][2]
                    pe.wait_ge(taken[e], i * TAKES[e] + sum(x == e for _, _, x in FILLS[:before + 1]))
                else:
                    e = FILLS[before][2]
                    pe.wait_ge(taken[e], i * TAKES[e])
                if products[0][1].shape[0] <= S and products[0][0].shape[0] <= S:
                    pe.sem_inc(passed["pe"], 1)
                for args in products:
                    ins = pe.matmul(*args[:3], start=args[3], stop=args[4])
                ins.then_inc(filled, 1)

            def conv_first(i, slot):
                pe.wait_ge(chan_stats, i + 1)
                pe.matmul(gps[0:TP, 0:4 * NT], group[:, :], mv[:, :, :].rearrange("p k s -> p (k s)"), start=True, stop=True
                          ).then_inc(group_sums, 1)
                pe.wait_ge(w_scaled, i + 1)
                for img in range(2):
                    for t in range(NT):
                        ins = pe.matmul(gps[0:C1, 16 + img:17 + img], conv1s[:, img * NT + t, :], gst[:, img * NT + t, 0:1],
                                        start=(t == 0), stop=(t == NT - 1))
                ins.then_inc(vbias_sum, 1)
                for k in range(2 * NCH):
                    img, q = divmod(k, NCH)
                    pe.wait_ge(v_copied, i * (2 * NCH) + max(k - 1, 0))
                    for t in range(NT):
                        rhs = x1[slot][:, img, t, :].rearrange("p (h w) -> p w h", w=S)[:, 8 * q:8 * q + 8, :]
                        ins = pe.matmul(vps[k % 2][:, :], conv1s[:, img * NT + t, :], rhs, start=(t == 0), stop=(t == NT - 1))
                    ins.then_inc(v_filled, 1)

            def chain(i, slot, more):
                pe.wait_ge(xw_loaded, 32 * i + 32)
                for name, w, c0, d in (("s1f", 128, 0, D_S1F), ("s1r", 2 * KW, CM, D_S1R)):
                    for c in range(4):
                        k = INDEX[name, c]
                        fill(i, k, [(stage[k % 3][img * S:(img + 1) * S, w * g:w * (g + 1)], xw[img * S:(img + 1) * S, c0 + 4 * c + g, :],
                                     dft[img * S:(img + 1) * S, d, 0:w], True, True) for g in range(4) for img in range(2)])
                pe.wait_ge(taken["act"], i * TAKES["act"] + 4)
                pe.wait_ge(taken["dve"], i * TAKES["dve"] + 4)
                for name, src, d, w in (("s2f", a1f, D_S2F, S), ("s2r", a1r, D_S2R, KW)):
                    for c in range(2):
                        r, m = src[:, 8 * c:8 * c + 8, 0, :], src[:, 8 * c:8 * c + 8, 1, :]
                        for part, terms in (("_re", ((d, r), (d + 2, m))), ("_im", ((d + 1, r), (d, m)))):
                            k = INDEX[name + part, c]
                            fill(i, k, [(stage[k % 3][:, 0:8 * w], dft[:, dd, :], rhs, n == 0, n == 1) for n, (dd, rhs) in enumerate(terms)])
                pe.wait_ge(masked, i + 1)
                for img in range(2):
                    k = INDEX["outer", img]
                    fill(i, k, [(stage[k % 3][:, :], mix[:, M_OUTER, :], magb[:, img, :], True, True)])
                    k = INDEX["inner", img]
                    o = stage[k % 3][:, 0:8 * H1].rearrange("p (r n) -> p r n", n=H1)
                    src = magi[:, img, :].rearrange("p (r n) -> p r n", n=S)

                    def cols(dx):
                        return slice(H0 + dx - 1, H0 + dx - 1 + H1)

                    prods = [(o, mix[:, M_TAP + 3 + dx, :], src[:, :, cols(dx)], dx == 0, False) for dx in range(3)]
                    prods += [(o[:, 1:8, :], mix[:, M_TAP + dx, :], src[:, 0:7, cols(dx)], False, False) for dx in range(3)]
                    prods += [(o[:, 0:7, :], mix[:, M_TAP + 6 + dx, :], src[:, 1:8, cols(dx)], False, False) for dx in range(3)]
                    prods += [(o[:, 0, :], mix[:, M_UP + dx, :], src[:, 7, cols(dx)], False, False) for dx in range(3)]
                    prods += [(o[:, 7, :], mix[:, M_DOWN + dx, :], src[:, 0, cols(dx)], False, dx == 2) for dx in range(3)]
                    fill(i, k, prods)
                    for name, m, rhs, w in (("phase", M_PHASE, angb[:, img, :], CH), ("rmod", M_REAL, rblk[:, img, 0, :], BR),
                                            ("rang", M_REAL, rblk[:, img, 1, :], BR)):
                        k = INDEX[name, img]
                        fill(i, k, [(stage[k % 3][:, 0:w], mix[:, m, :], rhs, True, True)])
                    k = INDEX["mod", img]
                    pe.wait_ge(mixed, 2 * i + img + 1)
                    fill(i, k, [(stage[k % 3][:, :], mix[:, M_MOD, :], mixu[:, img, :, :].rearrange("p r n -> p (r n)"), True, True)])
                pe.wait_ge(g_loaded, (i + 1) * 128)
                for name, src, n, d in (("s3f", gt, S, D_S3F), ("s3r", pt, KW, D_S3R)):
                    for c in range(4):
                        k = INDEX[name, c]
                        fill(i, k, [(stage[k % 3][img * S:img * S + n, 128 * g:128 * (g + 1)], src[:, img, 4 * c + g, :], dft[:, d, :], True, True)
                                    for g in range(4) for img in range(2)])
                n3 = 16 + 4
                pe.wait_ge(taken["act"], i * TAKES["act"] + n3)
                pe.wait_ge(taken["dve"], i * TAKES["dve"] + 12 + 4)
                for c in range(2):
                    r, m = h1f[:, 8 * c:8 * c + 8, 0, :], h1f[:, 8 * c:8 * c + 8, 1, :]
                    for part, terms in (("_re", ((D_S4F, r), (D_S4F + 2, m))), ("_im", ((D_S4F + 1, r), (D_S4F, m)))):
                        k = INDEX["s4f" + part, c]
                        fill(i, k, [(stage[k % 3][:, :], dft[:, dd, :], rhs, n == 0, n == 1) for n, (dd, rhs) in enumerate(terms)])
                for c in range(2):
                    k = INDEX["s4r", c]
                    fill(i, k, [(stage[k % 3][img * S:(img + 1) * S, :], dft[img * S:img * S + KW, D_S4R + r, 0:S],
                                 h1r[img * S:img * S + KW, 8 * c:8 * c + 8, r, :], r == 0, r == 1) for img in range(2) for r in range(2)])
                if more:
                    conv_first(i + 1, 1 - slot)
                for j in range(2 * NCH):
                    img, q = divmod(j, NCH)
                    pe.wait_ge(z_loaded[j % 2], i * 256 + 32 * (j // 2 + 1))
                    for t in range(NT):
                        pe.wait_ge(o_added, i * PIX + max(2 * j + t - 1, 0))
                        pe.matmul(ops[t][:, :], conv2[:, t * TP:(t + 1) * TP], zch[j % 2][:, :], start=True, stop=True).then_inc(o_filled, 1)

            pe.wait_ge(const_loaded, 16 * NCONST)
            pe.matmul(gps[0:CM, 32:32 + C], c0w[:, :], conv2a[:, :], start=True, stop=True)
            for t in range(NT):
                ins = pe.matmul(gps[0:TP, 20 + t:21 + t], conv2a[:, t * TP:(t + 1) * TP], c0b[:, :], start=True, stop=True)
            ins.then_inc(setup_sum, 1)
            conv_first(0, 0)
            pairs_of(pe, chain)


def frft_matrix(N, a):
    shift = None
    if a < 0.5:
        shft = (np.arange(N) + int(np.fix(N / 2))) % N
        inv = np.argsort(shft)
        W = np.exp(2j * np.pi * np.outer(np.arange(N), np.arange(N)) / N) / math.sqrt(N)
        shift = W[inv, :][:, inv]
        a = a + 1.0
    alpha = a * math.pi / 2
    tana2, sina = math.tan(alpha / 2), math.sin(alpha)
    up = np.zeros((2 * N - 1, N))
    up[::2] = np.eye(N)
    kern = np.sinc(np.arange(-(2 * N - 3), 2 * N - 2) / 2.0)
    fi = np.stack([np.convolve(up[:, k], kern)[2 * N - 3:4 * N - 4] for k in range(N)], 1)
    fp = np.concatenate([np.zeros((N - 1, N)), fi, np.zeros((N - 1, N))], 0).astype(complex)
    n = np.arange(-2 * N + 2, 2 * N - 1).astype(float)
    chrp = np.exp(-1j * math.pi / N * tana2 / 4 * n ** 2)
    fp = chrp[:, None] * fp
    c = math.pi / N / sina / 4
    m = np.arange(-(4 * N - 4), 4 * N - 3).astype(float)
    kern = np.exp(1j * c * m ** 2)
    ret = np.stack([np.convolve(fp[:, k], kern)[4 * N - 4:8 * N - 7] for k in range(N)], 1) * math.sqrt(c / math.pi)
    ret = chrp[:, None] * ret
    M = np.exp(-1j * (1 - a) * math.pi / 4) * ret[N - 1:3 * N - 2:2]
    return M @ shift if shift is not None else M


def transforms():
    T, U = frft_matrix(S, 0.5), frft_matrix(S, -0.5)
    k = np.arange(S)
    turn = (np.outer(k, k) % S)
    cos, sin = np.round(np.cos(2 * np.pi * turn / S), 15), np.round(np.sin(2 * np.pi * turn / S), 15)
    d = np.zeros((128, D_N, 128))
    for img in range(2):
        r = slice(img * S, (img + 1) * S)
        d[r, D_S1F, :] = np.concatenate([T.real.T, T.imag.T], 1)
        d[r, D_S1R, 0:2 * KW] = np.concatenate([cos[:, 0:KW], -sin[:, 0:KW]], 1)
        for slot, a, b in ((D_S2F, T.real, T.imag), (D_S2R, cos, -sin), (D_S4F, U.real, U.imag)):
            d[r, slot, r], d[r, slot + 1, r], d[r, slot + 2, r] = a.T, b.T, -b.T
        c = np.full((KW, 1), 2.0 / S)
        c[0] = c[-1] = 1.0 / S
        d[img * S:img * S + KW, D_S4R, 0:S] = c * cos[0:KW]
        d[img * S:img * S + KW, D_S4R + 1, 0:S] = -c * sin[0:KW]
    for slot, a, b in ((D_S3F, U.real, U.imag), (D_S3R, cos / S, sin / S)):
        d[:, slot, :] = np.block([[a.T, b.T], [-b.T, a.T]])
    return (d + 0.0).astype(np.float32)


def masks():
    m = np.zeros((S, S), np.float32)
    m[H0:H0 + H1, H0:H0 + H1] = 1.0
    m = np.tile(m.reshape(8, 8, S), (CM, 1, 1))
    return np.stack([m, 1 - m], 1)


def spread(w, shift=0):
    m = np.zeros((CM, 8, CM, 8), w.dtype)
    for b in range(8):
        if 0 <= b + shift < 8:
            m[:, b, :, b + shift] = w.T
    return m.reshape(128, 128)


def mixing(mag_s_w, mag_f_w, mag_w, pha_w, conv_1_w):
    taps = [spread(mag_s_w[:, :, dy, dx]) for dy in range(3) for dx in range(3)]
    up = [spread(mag_s_w[:, :, 0, dx], 1) for dx in range(3)]
    down = [spread(mag_s_w[:, :, 2, dx], -1) for dx in range(3)]
    return np.ascontiguousarray(np.stack(taps + up + down + [spread(mag_f_w), spread(mag_w), spread(pha_w), spread(conv_1_w)], 1))


def biases(*b):
    return np.stack([np.repeat(x, 8) for x in b], 1)


def two_layers(nc, x, w0, b0, ident, group, imgsum, affine, conv1, conv2, c0w, c0b, mix, bias, mask, dft, out):
    B = x.shape[0]

    def scratch(name, shape):
        return nc.dram_tensor(name, shape, F32, kind="Internal").ap()

    y_d, bn_d = scratch("y_d", [B, C, HW]), scratch("bn_d", [TP, NT, 2])
    with ExitStack() as sems:
        layer0_conv(nc, sems, x, w0, b0, ident, group, imgsum, y_d, bn_d)
        layer1(nc, sems, x, y_d, bn_d, affine, group, conv1, conv2, c0w, c0b, mix, bias, mask, dft, out,
               scratch("v_d", [B, C1, HW]), scratch("f_d", [B, 2, CM, S, S]), scratch("r_d", [B, 2, CM, S, KW]),
               scratch("g_d", [B, 2, CM, S, S]), scratch("p_d", [B, 2, CM, S, KW]), scratch("z_d", [B, 2 * CM, S, S]))


def kernel(**inputs):
    import concourse.bacc as _bacc
    from concourse.bass_utils import run_bass_kernel_spmd as _run

    a = {k.replace("L0_conv_", "").replace("L1_conv_", ""): np.asarray(v) for k, v in inputs.items()}

    def by_tile(v):
        return v.reshape(NT, TP).T

    ins = {
        "x": a["x"],
        "w0": a["conv_w"].T.reshape(2 * NT, TP, C).transpose(1, 0, 2),
        "b0": by_tile(a["conv_b"]),
        "ident": np.eye(128, dtype=np.float32),
        "group": np.kron(np.eye(TP // 6), np.full((6, 6), 1 / 6)).astype(np.float32),
        "imgsum": np.kron(np.eye(2), np.full((S, S), 2.0 / HW)).astype(np.float32),
        "affine": np.stack([by_tile(a["bn_gamma"]), by_tile(a["bn_beta"])], 1),
        "conv1": a["conv1_w"].T.reshape(NT, TP, C1).transpose(1, 0, 2),
        "conv2": a["conv2_w"].T,
        "c0w": a["conv_0_w"],
        "c0b": a["conv_0_b"][:, None],
        "mix": mixing(a["mag_s_w"], a["mag_f_w"], a["mag_w"], a["pha_w"], a["conv_1_w"]),
        "bias": biases(a["mag_s_b"], a["mag_f_b"], a["mag_b"], a["pha_b"], a["conv_1_b"]),
        "mask": masks(),
        "dft": transforms(),
    }
    nc = _bacc.Bacc("TRN2", target_bir_lowering=False, num_devices=1)
    arrays, args = {}, []
    for name, v in ins.items():
        arrays[f"in_{name}_dram"] = np.ascontiguousarray(v)
        args.append(nc.dram_tensor(f"in_{name}_dram", v.shape, mybir.dt.from_np(v.dtype), kind="ExternalInput").ap())
    args.append(nc.dram_tensor("out_0_dram", a["x"].shape, F32, kind="ExternalOutput").ap())
    two_layers(nc, *args)
    r = _run(nc, [arrays], core_ids=[0])
    return r.results[0]["out_0_dram"]
```

```python
import math

import numpy as np
import concourse.bass as bass
from concourse import mybir
from contextlib import ExitStack

F32 = mybir.dt.float32
ALU = mybir.AluOpType
ACT = mybir.ActivationFunctionType
AX = mybir.AxisListType

TP = 96
NT = 2
C = TP * NT
S = 64
HW = S * S
K = 8
NP = S // K
ROW = HW // NP
BIG = 1.0e30


def pairs_of_line():
    a = [(p, p + s) for s in (1, 2) for p in range(NP - s)]
    b = [(p, p + s) for s in range(3, NP) for p in range(NP - s)]
    return a, b


def layer0_conv(nc, sems, x, w0_d, b0_d, ident_d, group_d, imgsum_d, y_d, bn_d):
    B = x.shape[0]
    PAIRS = B // 2
    PA, PB = pairs_of_line()
    NA, NB = len(PA), len(PB)
    NL = 2 * NP
    xv = x.rearrange("b (t p) h w -> p b t (h w)", p=TP)
    yv = y_d.rearrange("b (t p) n -> p b t n", p=TP)

    with ExitStack() as ctx:
        def sb(name, shape):
            return ctx.enter_context(nc.sbuf_tensor(name, shape, F32))

        def ps(name, shape):
            return ctx.enter_context(nc.psum_tensor(name, shape, F32))

        def sem(name):
            return sems.enter_context(nc.semaphore(name))

        xraw = sb("xraw", [TP, NT, ROW])
        xc = sb("xc", [TP, NT, NP, NP, 2, K * K])
        xp = sb("xp", [128, NP * NP, C])
        best = sb("best", [128, NP * NP, C])
        diff = sb("diff", [128, NA + NB, C])
        xjc = sb("xjc", [TP, NT, NP, 2, S])
        ysb = sb("ysb", [TP, 2, NT, ROW])
        xlast = diff[0:TP, :, :].rearrange("p u c -> p (u c)")[:, 0:2 * NT * ROW].rearrange("p (i t n) -> p i t n", i=2, t=NT)
        w0 = sb("w0", [TP, 4, C])
        b0 = sb("b0", [TP, NT])
        ident = sb("ident", [128, 128])
        group = sb("group", [TP, TP])
        imgsum = sb("imgsum", [128, 128])
        xst = sb("xst", [TP, 2 * NT, NP, 6])
        mv = sb("mv", [TP, 2 * NT, 2])
        gst = sb("gst", [TP, 2 * NT, 2])
        gtmp = sb("gtmp", [TP, 2 * NT])
        gstd = sb("gstd", [TP, 2 * NT])
        rstd = sb("rstd", [TP, 2 * NT])
        nbias = sb("nbias", [TP, 2 * NT])
        eps = sb("eps", [TP, 1])
        yst = xst[:, :, :, :].rearrange("p k a s -> p (k a s)").rearrange("p (o a s) -> p o a s", o=NT, s=6)
        ymv = sb("ymv", [TP, NT, 3])
        yagg = sb("yagg", [TP, NT, PAIRS, 3])
        ybn = sb("ybn", [TP, NT, 2])
        dist_e = sb("dist_e", [128, NP * NP // 2])
        esum = sb("esum", [128, 1])
        emean = sb("emean", [128, 1])
        esq = sb("esq", [128, 1])
        estd = sb("estd", [128, 1])
        thresh = sb("thresh", [128, 1])
        dist = sb("dist", [128, NA + NB])
        pen = sb("pen", [128, NA + NB])

        tps = [ps(f"tps{n}", [128, 2, 512]) for n in range(2)]
        YB = 3
        yps = [ps(f"yps{n}", [TP, 512]) for n in range(YB)]
        sps = ps("sps", [128, 16])

        const_loaded = sem("const_loaded")
        eps_set = sem("eps_set")
        stat_loaded = sem("stat_loaded")
        x_loaded = sem("x_loaded")
        xlast_loaded = sem("xlast_loaded")
        x_grouped = sem("x_grouped")
        xstat_done = sem("xstat_done")
        stat_step = sem("stat_step")
        chan_stats = sem("chan_stats")
        group_sums = sem("group_sums")
        group_var = sem("group_var")
        group_std = sem("group_std")
        norm_ready = sem("norm_ready")
        tp_filled = sem("tp_filled")
        evac_act = sem("evac_act")
        edist_part = sem("edist_part")
        edist_mean = sem("edist_mean")
        edist_sq = sem("edist_sq")
        edist_diff = sem("edist_diff")
        edist_step = sem("edist_step")
        edist_var = sem("edist_var")
        edist_std = sem("edist_std")
        diff_a = sem("diff_a")
        diff_b = sem("diff_b")
        dist_a = sem("dist_a")
        dist_b = sem("dist_b")
        pen_a = sem("pen_a")
        pen_b = sem("pen_b")
        best_a = sem("best_a")
        best_b = sem("best_b")
        xj_done = sem("xj_done")
        y_filled = sem("y_filled")
        y_copied = sem("y_copied")
        y_counted = sem("y_counted")
        y_stored = [sem(f"y_stored{n}") for n in range(2)]
        bn_step = sem("bn_step")
        bn_ready = sem("bn_ready")
        bn_stored = sem("bn_stored")
        passed = sem("passed_rows")

        block = ctx.enter_context(nc.Block())

        def by_column(t):
            return t[:, :, :].rearrange("p (a b) c -> p a b c", b=NP)

        def line_of(t, along_rows, line, p0, n):
            v = by_column(t)
            if along_rows:
                return v[:, bass.ds(line, 1), p0:p0 + n, :].rearrange("p l n c -> p (l n) c")
            return v[:, p0:p0 + n, bass.ds(line, 1), :].rearrange("p n l c -> p n (l c)")

        GSTEPS, ESTEPS = 5, 3
        FILLS = 4 * NP

        def first_fill(i):
            return i * FILLS + 2 * NP

        def fill_back(r, more):
            return 4 * r - 2 if more and r else 2 * r

        def fill_next(r):
            return 4 * r + 4 if r < NP - 1 else FILLS - 2

        def pairs_of(eng, body):
            if PAIRS > 1:
                body(0, True)
            if PAIRS > 2:
                with eng.Fori(1, PAIRS - 1) as i:
                    body(i, True)
            body(PAIRS - 1, False)

        @block.sync
        def _(sp):
            def load_stat(i, a):
                n, ny = sp.snap((i * NP + a) * 2 * NT), sp.snap(2 * i)
                sp.wait_ge(xstat_done, n)
                sp.dma_start(ysb[:, :, :, :], xv[:, bass.ds(ny, 2), :, a * ROW:(a + 1) * ROW]).then_inc(stat_loaded, 16)

            def load_row(i, a, img):
                n, ni = sp.snap((i * NP + a) * 4 + 2 * img), sp.snap(2 * i + img)
                src = xv[:, bass.ds(ni, 1), :, a * ROW:(a + 1) * ROW].rearrange("p b t n -> p (b t) n")
                if a < NP - 1:
                    sp.wait_ge(x_grouped, n)
                    sp.dma_start(xraw[:, :, :], src).then_inc(x_loaded, 16)
                else:
                    sp.dma_start(xlast[:, img, :, :], src).then_inc(xlast_loaded, 16)

            def pair(i, more):
                if more:
                    stored, counted = sp.snap(i * (16 * NP)), sp.snap(i * (4 * NP))
                    for s, n in ((y_stored[0], stored), (y_stored[1], stored), (y_counted, counted)):
                        sp.wait_ge(s, n)
                        sp.sem_inc(passed, 1)
                    for a in range(NP):
                        load_stat(i + 1, a)
                    load_row(i + 1, 0, 0)
                for a in range(NP):
                    for img in range(2):
                        ni = sp.snap(2 * i + img)
                        sp.wait_ge(y_copied, i * (4 * NP) + 4 * a + 2 * (img + 1))
                        sp.dma_start(yv[:, bass.ds(ni, 1), :, a * ROW:(a + 1) * ROW].rearrange("p b t n -> p (b t) n"),
                                     ysb[:, img, :, :]).then_inc(y_stored[img], 16)
                    if more and a < NP - 1:
                        load_row(i + 1, a, 1)
                        if a < NP - 2:
                            load_row(i + 1, a + 1, 0)
                        if a == NP - 3:
                            nd = sp.snap(i * NL + NL)
                            sp.wait_ge(dist_b, nd)
                            sp.sem_inc(passed, 1)
                            for img in range(2):
                                load_row(i + 1, NP - 1, img)

            for dst, src in ((w0[:, :, :], w0_d), (b0[:, :], b0_d), (ident[:, :], ident_d),
                             (group[:, :], group_d), (imgsum[:, :], imgsum_d)):
                sp.dma_start(dst, src).then_inc(const_loaded, 16)
            for a in range(NP):
                load_stat(0, a)
            for a in range(NP):
                for img in range(2):
                    load_row(0, a, img)
            pairs_of(sp, pair)
            sp.wait_ge(bn_ready, 1)
            sp.dma_start(bn_d, ybn[:, :, :]).then_inc(bn_stored, 16)
            for n in range(2):
                sp.wait_ge(y_stored[n], 16 * NP * PAIRS)
            sp.wait_ge(bn_stored, 16)

        @block.gpsimd
        def _(pool):
            pool.memset(eps[:, :], 1e-5).then_inc(eps_set, 1)

            def line(i, along_rows, l):
                n = pool.snap(i * NL + (NP if along_rows else 0) + l)
                for half, s0, s1, ready, used, at in ((0, 1, 2, diff_a, dist_a, 0), (1, 3, 7, diff_b, dist_b, NA)):
                    pool.wait_ge(used, n)
                    for s in range(s0, s1 + 1):
                        m = NP - s
                        ins = pool.tensor_tensor(diff[:, at:at + m, :], line_of(xp, along_rows, l, s, m),
                                                 line_of(xp, along_rows, l, 0, m), ALU.subtract)
                        at += m
                    ins.then_inc(ready, 1)

            def finish(i, a):
                pool.wait_ge(best_b, (i * NL + NP + a + 1) * 2 * NB)
                r = best[:, :, :].rearrange("p (a b) c -> p a (b c)", b=NP)[:, bass.ds(a, 1), :].rearrange("p a n -> p (a n)")
                q = xp[:, :, :].rearrange("p (a b) c -> p a (b c)", b=NP)[:, bass.ds(a, 1), :].rearrange("p a n -> p (a n)")
                pool.tensor_tensor(r, r, q, ALU.subtract).then_inc(xj_done, 1)

            def pair(i, more):
                pool.wait_ge(evac_act, first_fill(i))
                line(i, False, 0)
                with pool.Fori(1, NP) as l:
                    line(i, False, l)
                line(i, True, 0)
                with pool.Fori(1, NP) as l:
                    line(i, True, l)
                    finish(i, l - 1)
                finish(i, NP - 1)

            pairs_of(pool, pair)

        @block.scalar
        def _(act):
            act.wait_ge(eps_set, 1)
            act.wait_ge(const_loaded, 16 * 5)

            def distances(i, along_rows, l, halves=(0, 1)):
                n = act.snap(i * NL + (NP if along_rows else 0) + l)
                for half in halves:
                    u0, m, ready, done, used = ((0, NA, diff_a, dist_a, pen_a), (NA, NB, diff_b, dist_b, pen_b))[half]
                    act.wait_ge(ready, n + 1)
                    act.wait_ge(used, n)
                    for u in range(u0, u0 + m):
                        ins = act.activation(diff[:, u, :], diff[:, u, :], ACT.Abs, accum_out=dist[:, u:u + 1])
                    ins.then_inc(done, 1)

            def row(i, r, more):
                base = act.snap(i * (4 * NP) + 4 * r)
                for t in range(NT):
                    act.wait_ge(tp_filled, first_fill(i) + fill_back(r, more) + t + 1)
                    act.wait_ge(y_filled, base)
                    act.activation(xjc[:, t, :, :, :].rearrange("p b i n -> p (b i n)"),
                                   tps[t][0:TP, :, :].rearrange("p a n -> p (a n)"), ACT.Identity).then_inc(evac_act, 1)
                if r + 2 < NP:
                    distances(i, True, r + 2, (0,))
                if more and r > 0:
                    regroup(i + 1, r - 1, 1)
                rows = act.snap(i * NP + r)
                for g in range(4):
                    img, o = divmod(g, NT)
                    if more and r > 0 and g == 2:
                        fill_xp(first_fill(i) + fill_next(r - 1), r - 1)
                    if g == 3 and r + 2 < NP:
                        distances(i, True, r + 2, (1,))
                    if o == 0:
                        act.wait_ge(y_stored[img], rows * 16)
                        act.wait_ge(y_counted, base + (g - 2 if r else 0))
                    if more and r == 0 and g == 0:
                        act.wait_ge(xstat_done, (i + 2) * (2 * NT * NP))
                    act.wait_ge(y_filled, base + g + 1)
                    act.activation(ysb[:, img, o, :].rearrange("p (i b j) -> p b i j", i=K, b=NP),
                                   yps[(4 * r + g) % YB][:, :].rearrange("p (b i j) -> p b i j", b=NP, i=K),
                                   ACT.Identity, bias=b0[:, o:o + 1]).then_inc(y_copied, 1)
                if more:
                    if r == 0:
                        act.wait_ge(norm_ready, i + 2)
                    regroup(i + 1, r, 0)

            def fill_xp(at, r):
                for n in range(2):
                    act.wait_ge(tp_filled, at + n + 1)
                    act.activation(xp[:, NP * r + 4 * n:NP * r + 4 * n + 4, :].rearrange("p (k g) c -> p k (g c)", k=2),
                                   tps[n][:, :, 0:2 * C], ACT.Identity).then_inc(evac_act, 1)

            def regroup(i, a, img):
                if a < NP - 1:
                    act.wait_ge(x_loaded, (i * (NP - 1) + a) * 32 + 16 * (img + 1))
                else:
                    act.wait_ge(xlast_loaded, i * 32 + 32)
                for t in range(NT):
                    k = img * NT + t
                    src = xraw[:, t, :] if a < NP - 1 else xlast[:, img, t, :]
                    act.activation(xc[:, t, a, :, img, :].rearrange("p b (i j) -> p b i j", i=K),
                                   src.rearrange("p (i b j) -> p b i j", i=K, b=NP),
                                   ACT.Identity, scale=rstd[:, k:k + 1], bias=nbias[:, k:k + 1]).then_inc(x_grouped, 1)

            def group_root(i):
                act.wait_ge(group_var, i + 1)
                act.activation(gstd[:, :], gst[:, :, 1], ACT.Sqrt, bias=eps[:, 0:1]).then_inc(group_std, 1)

            def pair(i, more):
                distances(i, False, 0)
                act.wait_ge(edist_var, i + 1)
                act.activation(estd[:, :], sps[:, 9:10], ACT.Sqrt, scale=HW / (HW - 1)).then_inc(edist_std, 1)
                with act.Fori(1, NP) as l:
                    distances(i, False, l)
                distances(i, True, 0)
                distances(i, True, 1, (0,))
                if more:
                    group_root(i + 1)
                distances(i, True, 1, (1,))
                for r in range(NP):
                    row(i, r, more)
                if more:
                    regroup(i + 1, NP - 1, 1)
                    fill_xp(first_fill(i) + fill_next(NP - 1), NP - 1)

            group_root(0)
            act.wait_ge(norm_ready, 1)
            for a in range(NP):
                for img in range(2):
                    regroup(0, a, img)
                if a > 0:
                    fill_xp(2 * (a - 1), a - 1)
            fill_xp(2 * (NP - 1), NP - 1)
            pairs_of(act, pair)

        @block.vector
        def _(dve):
            def line(i, along_rows, l, between=None):
                n = dve.snap(i * NL + (NP if along_rows else 0) + l)
                last = {}
                for half, us, off, made, done, known in ((0, PA, 0, pen_a, best_a, dist_a), (1, PB, NA, pen_b, best_b, dist_b)):
                    m = len(us)
                    if half == 1 and between:
                        between()
                    dve.wait_ge(known, n + 1)
                    dve.wait_ge(done, n * 2 * m)
                    dve.tensor_scalar(pen[:, off:off + m], dist[:, off:off + m], thresh[:, 0:1], -BIG,
                                      ALU.is_ge, ALU.mult).then_inc(made, 1)
                    dve.wait_ge(made, n + 1)
                    at = dve.snap(n * 2 * m)
                    count = 0
                    todo = []
                    for s in sorted({q - p for p, q in us}):
                        todo += [(u, p, q) for u, (p, q) in enumerate(us) if q - p == s]
                        todo += [(u, q, p) for u, (p, q) in enumerate(us) if q - p == s]
                    for u, p, q in todo:
                        dst, cand = line_of(best, along_rows, l, p, 1), line_of(xp, along_rows, l, q, 1)
                        own = dst
                        if p in last:
                            sm, base, c = last[p]
                            dve.wait_ge(sm, base + c)
                        elif not along_rows:
                            own = line_of(xp, along_rows, l, p, 1)
                        dve.scalar_tensor_tensor(dst, cand, pen[:, off + u:off + u + 1], own,
                                                 ALU.add, ALU.max).then_inc(done, 1)
                        count += 1
                        last[p] = (done, at, count)

            def count_y(i, r, img):
                base = dve.snap(i * (4 * NP) + 4 * r)
                dve.wait_ge(y_copied, base + 2 * (img + 1))
                for o in range(NT):
                    dve.bn_stats(yst[:, o, bass.ds(2 * r + img, 1), :].rearrange("p a s -> p (a s)"),
                                 ysb[:, img, o, :]).then_inc(y_counted, 1)

            def link(ins, s, value):
                ins.then_inc(s, 1)
                dve.wait_ge(s, value)

            def count_x(i, row):
                dve.wait_ge(stat_loaded, (i * NP + row) * 16 + 16)
                for k in range(2 * NT):
                    dve.bn_stats(xst[:, k, bass.ds(row, 1), :].rearrange("p a s -> p (a s)"), ysb[:, k // NT, k % NT, :]
                                 ).then_inc(xstat_done, 1)

            def channel_stats(i):
                dve.wait_ge(xstat_done, (i + 1) * (2 * NT * NP))
                dve.memset(gtmp[:, :], 0.0)
                for k in range(2 * NT):
                    ins = dve.bn_aggr(mv[:, k, :], xst[:, k, :, :].rearrange("p a s -> p (a s)"))
                link(ins, stat_step, i * GSTEPS + 1)
                link(dve.tensor_tensor(gtmp[:, :], mv[:, :, 0], mv[:, :, 0], ALU.mult), stat_step, i * GSTEPS + 2)
                dve.tensor_tensor(mv[:, :, 1], mv[:, :, 1], gtmp[:, :], ALU.add).then_inc(chan_stats, 1)

            def group_variance(i, first=False):
                dve.wait_ge(group_sums, i + 1)
                if not first:
                    dve.wait_ge(x_grouped, i * (4 * NP))
                link(dve.tensor_copy(gst[:, :, :].rearrange("p k s -> p (k s)"), sps[0:TP, 0:4 * NT]), stat_step, i * GSTEPS + 3)
                link(dve.tensor_tensor(gtmp[:, :], gst[:, :, 0], gst[:, :, 0], ALU.mult), stat_step, i * GSTEPS + 4)
                dve.tensor_tensor(gst[:, :, 1], gst[:, :, 1], gtmp[:, :], ALU.subtract).then_inc(group_var, 1)

            def group_scale(i):
                dve.wait_ge(group_std, i + 1)
                link(dve.reciprocal(rstd[:, :], gstd[:, :]), stat_step, i * GSTEPS + 5)
                dve.scalar_tensor_tensor(nbias[:, :], gst[:, :, 0], -1.0, rstd[:, :], ALU.mult, ALU.mult).then_inc(norm_ready, 1)

            def half_roll(i, a):
                h = NP // 2
                dve.wait_ge(evac_act, first_fill(i) - FILLS + fill_next(a + h) + 2)
                for b in (0, h):
                    ins = dve.tensor_tensor(best[:, a * NP + b:a * NP + b + h, :],
                                            xp[:, (a + h) * NP + h - b:(a + h) * NP + 2 * h - b, :],
                                            xp[:, a * NP + b:a * NP + b + h, :], ALU.subtract)
                link(ins, edist_diff, i * h + a + 1)
                return dve.tensor_reduce(dist_e[:, a * NP:(a + 1) * NP], best[:, a * NP:(a + 1) * NP, :], AX.X, ALU.add,
                                         apply_absolute_value=True)

            def threshold(i):
                ins = half_roll(i, NP // 2 - 1)
                link(ins, edist_step, i * ESTEPS + 1)
                dve.tensor_reduce(esum[:, :], dist_e[:, :], AX.X, ALU.add).then_inc(edist_part, 1)
                dve.wait_ge(edist_mean, i + 1)
                link(dve.tensor_copy(emean[:, :], sps[:, 8:9]), edist_step, i * ESTEPS + 2)
                link(dve.tensor_scalar(dist_e[:, :], dist_e[:, :], emean[:, 0:1], None, ALU.subtract), edist_step, i * ESTEPS + 3)
                dve.tensor_tensor_reduce(out=dist_e[:, :], in0=dist_e[:, :], in1=dist_e[:, :], scale=1.0, scalar=0.0,
                                         op0=ALU.mult, op1=ALU.add, accum_out=esq[:, :]).then_inc(edist_sq, 1)
                dve.wait_ge(edist_std, i + 1)
                dve.tensor_tensor(thresh[:, :], emean[:, :], estd[:, :], ALU.subtract).then_inc(edist_part, 1)
                dve.wait_ge(edist_part, 2 * i + 2)

            def pair(i, more):
                threshold(i)
                line(i, False, 0)
                if more:
                    count_x(i + 1, 0)
                with dve.Fori(1, NP) as l:
                    line(i, False, l)
                    if more:
                        count_x(i + 1, l)
                dve.wait_ge(best_b, (i * NL + NP) * 2 * NB)
                if more:
                    channel_stats(i + 1)
                line(i, True, 0, (lambda: group_variance(i + 1)) if more else None)
                if more:
                    group_scale(i + 1)
                line(i, True, 1)
                count_y(i, 0, 0)
                with dve.Fori(2, NP) as l:
                    line(i, True, l, lambda: count_y(i, l - 2, 1))
                    count_y(i, l - 1, 0)
                if more:
                    half_roll(i + 1, 0)
                count_y(i, NP - 2, 1)
                if more:
                    half_roll(i + 1, 1)
                for img in range(2):
                    count_y(i, NP - 1, img)
                if more:
                    half_roll(i + 1, 2)
                dve.wait_ge(y_counted, (i + 1) * (4 * NP))
                dve.memset(ymv[:, :, 0], float(2 * HW))
                for o in range(NT):
                    ins = dve.bn_aggr(ymv[:, o, 1:3], yst[:, o, :, :].rearrange("p a s -> p (a s)"))
                ins.then_inc(bn_step, 1)
                dve.wait_ge(bn_step, 1 + 2 * i)
                dve.tensor_copy(yagg[:, :, bass.ds(i, 1), 0:2].rearrange("p o a s -> p o (a s)"), ymv[:, :, 0:2])
                dve.tensor_scalar(yagg[:, :, bass.ds(i, 1), 2].rearrange("p o a -> p (o a)"), ymv[:, :, 2],
                                  float(2 * HW), None, ALU.mult).then_inc(bn_step, 1)
                dve.wait_ge(bn_step, 2 + 2 * i)
            dve.wait_ge(const_loaded, 16 * 5)
            for a in range(NP):
                count_x(0, a)
            channel_stats(0)
            group_variance(0, True)
            group_scale(0)
            dve.wait_ge(evac_act, 2 * NP)
            for a in range(3):
                half_roll(0, a)
            pairs_of(dve, pair)
            for o in range(NT):
                ins = dve.bn_aggr(ybn[:, o, :], yagg[:, o, :, :].rearrange("p a s -> p (a s)"))
            ins.then_inc(bn_ready, 1)

        @block.tensor
        def _(pe):
            pe.wait_ge(const_loaded, 16 * 5)

            def group_average(i):
                pe.wait_ge(chan_stats, i + 1)
                pe.matmul(sps[0:TP, 0:4 * NT], group[:, :], mv[:, :, :].rearrange("p k s -> p (k s)"),
                          start=True, stop=True).then_inc(group_sums, 1)

            def to_pixels(at, i, a):
                pe.wait_ge(x_grouped, (i * NP + a) * 4 + 4)
                for n in range(2):
                    if not isinstance(at, int) or at + n > 1:
                        pe.wait_ge(evac_act, at + n - 1)
                    for g in range(4):
                        for t in range(NT):
                            src = xc[:, t, a, 4 * n + g, :, :].rearrange("p k n -> p (k n)")
                            ins = pe.transpose(tps[n][:, g // 2, (g % 2) * C + t * TP:(g % 2) * C + (t + 1) * TP],
                                               src, ident[0:TP, 0:TP])
                    ins.then_inc(tp_filled, 1)

            def pair(i, more):
                pe.wait_ge(edist_part, i * 2 + 1)
                pe.matmul(sps[:, 8:9], imgsum[:, :], esum[:, :], start=True, stop=True).then_inc(edist_mean, 1)
                pe.wait_ge(edist_sq, i + 1)
                pe.matmul(sps[:, 9:10], imgsum[:, :], esq[:, :], start=True, stop=True).then_inc(edist_var, 1)
                if more:
                    group_average(i + 1)
                for a in range(NP):
                    pe.wait_ge(xj_done, i * NP + a + 1)
                    for t in range(NT):
                        pe.wait_ge(evac_act, first_fill(i) + fill_back(a, more) + t - 1)
                        for b in range(NP):
                            ins = pe.transpose(tps[t][0:TP, b // 4, (b % 4) * 128:(b % 4 + 1) * 128],
                                               best[:, a * NP + b, t * TP:(t + 1) * TP], ident[:, :])
                        ins.then_inc(tp_filled, 1)
                    for g in range(4):
                        img, o = divmod(g, NT)
                        if more and a > 0 and g == 2:
                            to_pixels(first_fill(i) + fill_next(a - 1), i + 1, a - 1)
                        n = 4 * a + g
                        pe.wait_ge(y_copied, i * (4 * NP) + (n + 1 - YB if n >= YB else 0))
                        if g == 0:
                            pe.wait_ge(evac_act, first_fill(i) + fill_back(a, more) + 2)
                        for k in range(2 * NT):
                            t = k % NT
                            if k < NT:
                                rhs = xc[:, t, a, :, img, :]
                            else:
                                rhs = xjc[:, t, :, img, :]
                            ins = pe.matmul(yps[n % YB][:, :], w0[:, k, o * TP:(o + 1) * TP], rhs,
                                            start=(k == 0), stop=(k == 2 * NT - 1))
                        ins.then_inc(y_filled, 1)
                if more:
                    to_pixels(first_fill(i) + fill_next(NP - 1), i + 1, NP - 1)

            group_average(0)
            for a in range(NP):
                to_pixels(2 * a, 0, a)
            pairs_of(pe, pair)


CM = 16
C1 = 3 * CM
KW = S // 2 + 1
CH = HW // 8
NCH = HW // CH
H1 = int(S * math.cos(math.pi / 4))
H0 = (S - H1) // 2
FR = CM * S
RF = CM * KW
EW = FR + RF
BR = 8 * KW
BW = CH + BR
TWO_PI = 2 * math.pi
TWO_PI_HI = 6.28125
ROUND = 12582912.0
PIX = 2 * NT * NCH

FILLS = ([("s1f", c, "act" if c % 2 else "dve") for c in range(4)] + [("s1r", c, "act" if c % 2 else "dve") for c in range(4)]
         + [(n + p, c, e) for n in ("s2f", "s2r") for c in range(2) for p, e in (("_re", "act"), ("_im", "dve"))]
         + [(n, c, e) for c in range(2) for n, e in (("outer", "dve"), ("inner", "dve"), ("phase", "act"), ("rmod", "act"), ("rang", "act"), ("mod", "act"))]
         + [("s3f", c, "act" if c % 2 else "dve") for c in range(4)] + [("s3r", c, "act" if c % 2 else "dve") for c in range(4)]
         + [("s4f" + p, c, "act") for c in range(2) for p in ("_re", "_im")] + [("s4r", c, "dve") for c in range(2)])
NF = len(FILLS)
INDEX = {(n, c): k for k, (n, c, _) in enumerate(FILLS)}
TAKES = {e: sum(x == e for _, _, x in FILLS) for e in ("act", "dve")}
D_S1F, D_S1R, D_S2F, D_S2R, D_S3F, D_S3R, D_S4F, D_S4R, D_N = 0, 1, 2, 5, 8, 9, 10, 13, 15
M_TAP, M_UP, M_DOWN, M_OUTER, M_MOD, M_PHASE, M_REAL, M_N = 0, 9, 12, 15, 16, 17, 18, 19


def layer1(nc, sems, x, y_d, bn_d, affine_d, group_d, conv1_d, conv2_d, c0w_d, c0b_d, mix_d, bias_d, mask_d, dft_d, out,
           v_d, f_d, r_d, g_d, p_d, z_d):
    B = x.shape[0]
    PAIRS = B // 2
    xv = x.rearrange("b (t p) h w -> p b t (h w)", p=TP)
    ov = out.rearrange("b (t p) h w -> p b t (h w)", p=TP)
    yv = y_d.rearrange("b (t p) n -> p b t n", p=TP)

    with ExitStack() as ctx:
        def sb(name, shape):
            return ctx.enter_context(nc.sbuf_tensor(name, shape, F32))

        def ps(name, shape):
            return ctx.enter_context(nc.psum_tensor(name, shape, F32))

        def sem(name):
            return sems.enter_context(nc.semaphore("l1_" + name))

        x1 = [sb(f"x1_{n}", [TP, 2, NT, HW]) for n in range(2)]
        ych = [sb(f"ych{n}", [TP, CH]) for n in range(2)]
        vch = [sb(f"vch{n}", [C1, CH]) for n in range(2)]
        zch = [sb(f"zch{n}", [C1, CH]) for n in range(2)]
        ra, rb, rc = sb("ra", [128, 2 * EW]), sb("rb", [128, 6 * CH + 4 * BR]), sb("rc", [128, 2 * EW])
        xw = ra[:, 0:2 * FR].rearrange("p (c h) -> p c h", h=S)
        mod, ang = ra[:, 0:EW], ra[:, EW:2 * EW]
        mixu = ra[:, 0:2 * CH].rearrange("p (i r n) -> p i r n", i=2, r=8)
        mixt = ra[:, 2 * CH:2 * CH + 2 * 8 * H1].rearrange("p (i r n) -> p i r n", i=2, r=8)
        im2, re2 = ra[:, 0:2 * BW], ra[:, 2 * BW:4 * BW]
        zt = ra[:, 0:2 * FR].rearrange("p (c h) -> p c h", h=S)
        a1f = rb[:, 0:2 * FR].rearrange("p (c r n) -> p c r n", r=2, n=S)
        a1r = rb[:, 2 * FR:2 * FR + 2 * RF].rearrange("p (c r n) -> p c r n", r=2, n=KW)
        magb = rb[:, 0:2 * CH].rearrange("p (i n) -> p i n", i=2)
        magi = rb[:, 2 * CH:4 * CH].rearrange("p (i n) -> p i n", i=2)
        angb = rb[:, 4 * CH:6 * CH].rearrange("p (i n) -> p i n", i=2)
        rblk = rb[:, 6 * CH:6 * CH + 4 * BR].rearrange("p (i s n) -> p i s n", i=2, s=2)
        h1f = rb[:, 0:2 * FR].rearrange("p (c r n) -> p c r n", r=2, n=S)
        h1r = rb[:, 2 * FR:4 * FR].rearrange("p (c r n) -> p c r n", r=2, n=S)
        re, im = rc[:, 0:EW], rc[:, EW:2 * EW]
        mo = rc[:, 0:2 * BW].rearrange("p (i n) -> p i n", i=2)
        ph = rc[:, 2 * BW:4 * BW].rearrange("p (i n) -> p i n", i=2)
        gt = rc[:, 0:2 * FR].rearrange("p (i c n) -> p i c n", i=2, n=S)
        pt = rc[:, 2 * FR:2 * FR + 2 * RF].rearrange("p (i c n) -> p i c n", i=2, n=KW)
        sq = rc[:, 0:2 * FR].rearrange("p (r n) -> p r n", r=2)

        group = sb("l1_group", [TP, TP])
        conv1 = sb("conv1", [TP, NT, C1])
        conv1s = sb("conv1s", [TP, 2 * NT, C1])
        conv2 = sb("conv2", [C1, C])
        conv2a = sb("conv2a", [CM, C])
        c0w, c0b = sb("c0w", [CM, CM]), sb("c0b", [CM, 1])
        mix = sb("mix", [128, M_N, 128])
        bias = sb("bias", [128, 5])
        mask = sb("mask", [128, 2, 8, S])
        dft = sb("dft", [128, D_N, 128])
        bnp = sb("bnp", [TP, NT, 2])
        affine = sb("affine", [TP, 2, NT])
        bns = sb("bns", [TP, NT, 2])
        cbias = sb("cbias", [TP, NT])
        eps = sb("l1_eps", [TP, 1])
        half_pi = sb("half_pi", [128, 1])
        st = sb("st", [TP, 2 * NT, NCH, 6])
        mv = sb("l1_mv", [TP, 2 * NT, 2])
        gst = sb("l1_gst", [TP, 2 * NT, 2])
        gtmp = sb("l1_gtmp", [TP, 2 * NT])
        gstd = sb("l1_gstd", [TP, 2 * NT])
        rstd = sb("l1_rstd", [TP, 2 * NT])
        vbias = sb("vbias", [C1, 2])

        vps = [ps(f"vps{n}", [C1, CH]) for n in range(2)]
        ops = [ps(f"ops{n}", [TP, CH]) for n in range(2)]
        stage = [ps(f"stage{n}", [128, 512]) for n in range(3)]
        gps = ps("gps", [128, 512])

        const_loaded, eps_set, set_up, setup_sum = sem("const_loaded"), sem("eps_set"), sem("set_up"), sem("setup_sum")
        setup_step = sem("setup_step")
        x_loaded = sem("x_loaded")
        y_loaded = [sem(f"y_loaded{n}") for n in range(2)]
        gelu_done, x1_done, x1_counted, stat_step = sem("gelu_done"), sem("x1_done"), sem("x1_counted"), sem("stat_step")
        chan_stats, group_sums, group_var, group_std = sem("chan_stats"), sem("group_sums"), sem("group_var"), sem("group_std")
        w_scaled, vbias_sum, vbias_done = sem("w_scaled"), sem("vbias_sum"), sem("vbias_done")
        v_filled, v_copied = sem("v_filled"), sem("v_copied")
        v_stored = [sem(f"v_stored{n}") for n in range(2)]
        xw_loaded, filled = sem("xw_loaded"), sem("filled")
        taken = {"act": sem("taken_act"), "dve": sem("taken_dve")}
        squared, sq_summed, mod_done, ratio_done, atan_done = sem("squared"), sem("sq_summed"), sem("mod_done"), sem("ratio_done"), sem("atan_done")
        ew_step, ang_done, f_stored, f_loaded, masked = sem("ew_step"), sem("ang_done"), sem("f_stored"), sem("f_loaded"), sem("masked")
        mixed, turn_done, abs_done, sin_done, g_done = sem("mixed"), sem("turn_done"), sem("abs_done"), sem("sin_done"), sem("g_done")
        g_stored, g_loaded, z_squared, z_summed, z_abs, z_real = (sem("g_stored"), sem("g_loaded"), sem("z_squared"), sem("z_summed"),
                                                                  sem("z_abs"), sem("z_real"))
        z_stored = sem("z_stored")
        z_loaded = [sem(f"z_loaded{n}") for n in range(2)]
        o_filled, o_added, o_stored = sem("o_filled"), sem("o_added"), sem("o_stored")

        passed = {e: sem("passed_" + e) for e in ("sp", "pe")}

        block = ctx.enter_context(nc.Block())
        NCONST = 12

        def wait_fill(eng, i, k):
            eng.wait_ge(filled, i * NF + k + 1)

        def place(k):
            return k // (NT * NCH), (k // NCH) % NT, k % NCH

        def pairs_of(eng, body):
            if PAIRS > 2:
                body(0, 0, True)
                body(1, 1, True)
            if PAIRS > 4:
                with eng.Fori(1, PAIRS // 2 - 1) as j:
                    body(eng.snap(2 * j), 0, True)
                    body(eng.snap(2 * j + 1), 1, True)
            body(PAIRS - 2, 0, True)
            body(PAIRS - 1, 1, False)

        @block.sync
        def _(sp):
            def load_y(i, k0, k1):
                for k in range(k0, k1):
                    img, t, q = place(k)
                    ni, n = sp.snap(2 * i + img), sp.snap(i * PIX + max(k - 1, 0))
                    sp.wait_ge(x1_done, n)
                    sp.sem_inc(passed["sp"], 1)
                    sp.dma_start(ych[k % 2][:, :], yv[:, bass.ds(ni, 1), t, q * CH:(q + 1) * CH].rearrange("p b n -> p (b n)")
                                 ).then_inc(y_loaded[k % 2], 16)

            def load_x(i, slot):
                for img in range(2):
                    ni = sp.snap(2 * i + img)
                    sp.dma_start(x1[slot][:, img, :, :], xv[:, bass.ds(ni, 1), :, :].rearrange("p b t n -> p (b t) n")
                                 ).then_inc(x_loaded, 16)

            def chain(i, slot, more):
                b = [sp.snap(2 * i + img) for img in range(2)]
                rows = [slice(img * S, (img + 1) * S) for img in range(2)]
                n8, n1 = sp.snap(i * 128 + 128), sp.snap(i * 32)
                for n in range(2):
                    sp.wait_ge(v_stored[n], n8)
                    sp.sem_inc(passed["sp"], 1)
                sp.wait_ge(z_stored, n1)
                sp.sem_inc(passed["sp"], 1)
                for img in range(2):
                    sp.dma_start(xw[rows[img], :, :], v_d[bass.ds(b[img], 1), CM:C1, :].rearrange("b c (w h) -> w (b c) h", h=S)
                                 ).then_inc(xw_loaded, 16)
                if more:
                    sp.wait_ge(o_stored, n1)
                    sp.sem_inc(passed["sp"], 1)
                    load_x(i + 1, 1 - slot)
                    load_y(i + 1, 0, 2)
                done = sp.snap(i + 1)
                for s, part, ready in ((0, mod, mod_done), (1, ang, ang_done)):
                    sp.wait_ge(ready, done)
                    sp.sem_inc(passed["sp"], 1)
                    for img in range(2):
                        sp.dma_start(f_d[bass.ds(b[img], 1), s, :, :, :].rearrange("b c h w -> (b h) c w"),
                                     part[rows[img], 0:FR].rearrange("p (c n) -> p c n", n=S)).then_inc(f_stored, 16)
                        sp.dma_start(r_d[bass.ds(b[img], 1), s, :, :, :].rearrange("b c h w -> (b h) c w"),
                                     part[rows[img], FR:EW].rearrange("p (c n) -> p c n", n=KW)).then_inc(f_stored, 16)
                sp.wait_ge(f_stored, n8)
                sp.sem_inc(passed["sp"], 1)
                for img in range(2):
                    for s, dst in ((0, magb), (1, angb)):
                        sp.dma_start(dst[:, img, :], f_d[bass.ds(b[img], 1), s, :, :, :].rearrange("b c (k r) w -> (b c k) (r w)", r=8)
                                     ).then_inc(f_loaded, 16)
                        sp.dma_start(rblk[:, img, s, :], r_d[bass.ds(b[img], 1), s, :, :, :].rearrange("b c (k r) w -> (b c k) (r w)", r=8)
                                     ).then_inc(f_loaded, 16)
                if more:
                    load_y(i + 1, 2, 18)
                sp.wait_ge(g_done, done)
                sp.sem_inc(passed["sp"], 1)
                for img in range(2):
                    for ri, part in ((0, re2), (1, im2)):
                        sp.dma_start(g_d[bass.ds(b[img], 1), ri, :, :, :].rearrange("b c (k r) w -> (b c k) (r w)", r=8),
                                     part[:, img * BW:img * BW + CH]).then_inc(g_stored, 16)
                        sp.dma_start(p_d[bass.ds(b[img], 1), ri, :, :, :].rearrange("b c (k r) w -> (b c k) (r w)", r=8),
                                     part[:, img * BW + CH:(img + 1) * BW]).then_inc(g_stored, 16)
                sp.wait_ge(g_stored, n8)
                sp.sem_inc(passed["sp"], 1)
                for img in range(2):
                    for ri in range(2):
                        sp.dma_start(gt[rows[ri], img, :, :], g_d[bass.ds(b[img], 1), ri, :, :, :].rearrange("b c h w -> (b h) c w")
                                     ).then_inc(g_loaded, 16)
                        sp.dma_start(pt[rows[ri], img, :, :], p_d[bass.ds(b[img], 1), ri, :, :, :].rearrange("b c h w -> (b h) c w")
                                     ).then_inc(g_loaded, 16)
                if more:
                    load_y(i + 1, 18, PIX)
                sp.wait_ge(z_abs, done)
                sp.sem_inc(passed["sp"], 1)
                sp.wait_ge(z_real, done)
                sp.sem_inc(passed["sp"], 1)
                for img in range(2):
                    sp.dma_start(z_d[bass.ds(b[img], 1), :, :, :].rearrange("b c w h -> (b w) c h"), zt[rows[img], :, :]
                                 ).then_inc(z_stored, 16)
                n2 = sp.snap(i * 32 + 32)
                sp.wait_ge(z_stored, n2)
                sp.sem_inc(passed["sp"], 1)
                for j in range(2 * NCH):
                    img, q = divmod(j, NCH)
                    no = sp.snap(i * PIX + 2 * max(j - 1, 0))
                    sp.wait_ge(o_filled, no)
                    sp.sem_inc(passed["sp"], 1)
                    px = slice(q * CH, (q + 1) * CH)
                    sp.dma_start(zch[j % 2][0:CM, :], v_d[bass.ds(b[img], 1), 0:CM, px].rearrange("b c n -> (b c) n")
                                 ).then_inc(z_loaded[j % 2], 16)
                    sp.dma_start(zch[j % 2][CM:C1, :], z_d[bass.ds(b[img], 1), :, 8 * q:8 * q + 8, :].rearrange("b c w h -> (b c) (w h)")
                                 ).then_inc(z_loaded[j % 2], 16)
                for img in range(2):
                    na = sp.snap(i * PIX + 16 * (img + 1))
                    sp.wait_ge(o_added, na)
                    sp.sem_inc(passed["sp"], 1)
                    sp.dma_start(ov[:, bass.ds(b[img], 1), :, :].rearrange("p b t n -> p (b t) n"), x1[slot][:, img, :, :]
                                 ).then_inc(o_stored, 16)

            consts = [(group[:, :], group_d), (conv1[:, :, :], conv1_d), (conv2[:, :], conv2_d), (conv2a[:, :], conv2_d[0:CM, :]),
                      (c0w[:, :], c0w_d), (c0b[:, :], c0b_d), (mix[:, :, :], mix_d), (bias[:, :], bias_d),
                      (mask[:, :, :, :], mask_d), (dft[:, :, :], dft_d), (bnp[:, :, :], bn_d), (affine[:, :, :], affine_d)]
            for dst, src in consts:
                sp.dma_start(dst, src).then_inc(const_loaded, 16)
            assert len(consts) == NCONST
            load_x(0, 0)
            load_y(0, 0, PIX)
            pairs_of(sp, chain)
            sp.wait_ge(o_stored, 32 * PAIRS)

        @block.gpsimd
        def _(pool):
            pool.memset(eps[:, :], 1e-5).then_inc(eps_set, 1)
            pool.memset(half_pi[:, :], math.pi / 2).then_inc(eps_set, 1)

            def add(i, slot):
                pool.wait_ge(x_loaded, 32 * i + 32)
                for k in range(PIX):
                    img, t, q = place(k)
                    dst = x1[slot][:, img, t, q * CH:(q + 1) * CH]
                    pool.wait_ge(gelu_done, i * PIX + k + 1)
                    pool.tensor_tensor(dst, dst, ych[k % 2][:, :], ALU.add).then_inc(x1_done, 1)

            def chain(i, slot, more):
                if more:
                    add(i + 1, 1 - slot)

            add(0, 0)
            pairs_of(pool, chain)

        @block.scalar
        def _(act):
            def take(i, k, out_ap, in_ap, func=ACT.Identity, **kw):
                wait_fill(act, i, k)
                act.activation(out_ap, in_ap, func, **kw).then_inc(taken["act"], 1)

            def gelu(i, k0, k1):
                for k in range(k0, k1):
                    img, t, q = place(k)
                    act.wait_ge(y_loaded[k % 2], i * (8 * PIX) + 16 * (k // 2 + 1))
                    act.activation(ych[k % 2][:, :], ych[k % 2][:, :], ACT.Gelu, scale=bns[:, t, 0:1], bias=bns[:, t, 1:2]
                                   ).then_inc(gelu_done, 1)

            def copy_v(i):
                act.wait_ge(vbias_done, i + 1)
                for k in range(2 * NCH):
                    img, q = divmod(k, NCH)
                    act.wait_ge(v_filled, i * (2 * NCH) + k + 1)
                    act.wait_ge(v_stored[k % 2], i * 128 + 16 * (k // 2))
                    act.activation(vch[k % 2][:, :], vps[k % 2][:, :], ACT.Identity, bias=vbias[:, img:img + 1]).then_inc(v_copied, 1)
                    ni, n = act.snap(2 * i + img), act.snap(i * (2 * NCH) + k + 1)
                    act.wait_ge(v_copied, n)
                    act.dma_start(v_d[bass.ds(ni, 1), :, q * CH:(q + 1) * CH].rearrange("b c n -> (b c) n"), vch[k % 2][:, :]
                                  ).then_inc(v_stored[k % 2], 16)

            def group_root(i):
                act.wait_ge(group_var, i + 1)
                act.activation(gstd[:, :], gst[:, :, 1], ACT.Sqrt, bias=eps[:, 0:1]).then_inc(group_std, 1)

            def chain(i, slot, more):
                for n, dst, w in (("s1f", a1f, 512), ("s1r", a1r, 8 * KW)):
                    for c in (1, 3):
                        k = INDEX[n, c]
                        take(i, k, dst[:, 4 * c:4 * c + 4, :, :].rearrange("p c r n -> p (c r n)"), stage[k % 3][:, 0:w])
                for n, off, w in (("s2f", 0, 512), ("s2r", FR, 8 * KW)):
                    for c in range(2):
                        k = INDEX[n + "_re", c]
                        take(i, k, re[:, off + c * w:off + (c + 1) * w], stage[k % 3][:, 0:w])
                act.wait_ge(taken["act"], i * TAKES["act"] + 8)
                act.activation(mod, re, ACT.Square).then_inc(squared, 1)
                act.wait_ge(taken["dve"], i * TAKES["dve"] + 8)
                act.activation(ang, im, ACT.Square).then_inc(squared, 1)
                act.wait_ge(sq_summed, i + 1)
                act.activation(ang, re, ACT.Abs)
                act.activation(mod, mod, ACT.Sqrt).then_inc(mod_done, 1)
                act.wait_ge(ratio_done, i + 1)
                act.activation(ang, ang, ACT.Arctan).then_inc(atan_done, 1)
                if more:
                    gelu(i + 1, 0, 16)
                for img in range(2):
                    for n, dst, w, kw in (("phase", ph[:, img, 0:CH], CH, dict(scale=2.0, bias=bias[:, 3:4])),
                                          ("rmod", mo[:, img, CH:BW], BR, dict(bias=bias[:, 4:5])),
                                          ("rang", ph[:, img, CH:BW], BR, dict(scale=2.0, bias=bias[:, 4:5])),
                                          ("mod", mo[:, img, 0:CH], CH, dict(bias=bias[:, 2:3]))):
                        k = INDEX[n, img]
                        take(i, k, dst, stage[k % 3][:, 0:w], **kw)
                act.wait_ge(turn_done, i + 1)
                act.activation(re2, im2, ACT.Abs).then_inc(abs_done, 1)
                act.wait_ge(abs_done, 2 * i + 1)
                act.activation(re2, re2, ACT.Sin, scale=-1.0, bias=half_pi[:, 0:1]).then_inc(sin_done, 1)
                act.activation(im2, im2, ACT.Sin).then_inc(sin_done, 1)
                act.wait_ge(sin_done, 2 * i + 2)
                act.activation(eps[:, 0:1], eps[:, 0:1], ACT.Identity).then_inc(abs_done, 1)
                if more:
                    gelu(i + 1, 16, PIX)
                for n, dst, p in (("s3f", h1f, 128), ("s3r", h1r, KW)):
                    for c in (1, 3):
                        k = INDEX[n, c]
                        wait_fill(act, i, k)
                        if p == 128:
                            act.activation(dst[:, 4 * c:4 * c + 4, :, :].rearrange("p c r n -> p (c r n)"), stage[k % 3][:, :],
                                           ACT.Identity).then_inc(taken["act"], 1)
                        else:
                            for img in range(2):
                                rows = slice(img * S, img * S + KW)
                                ins = act.activation(dst[rows, 4 * c:4 * c + 4, :, :].rearrange("p c r n -> p (c r n)"),
                                                     stage[k % 3][rows, :], ACT.Identity)
                            ins.then_inc(taken["act"], 1)
                for c in range(2):
                    for r, n in enumerate(("s4f_re", "s4f_im")):
                        k = INDEX[n, c]
                        take(i, k, sq[:, r, c * 512:(c + 1) * 512], stage[k % 3][:, :], ACT.Square)
                act.wait_ge(z_summed, i + 1)
                act.activation(zt[:, 0:CM, :].rearrange("p c n -> p (c n)"), sq[:, 0, :], ACT.Sqrt).then_inc(z_abs, 1)
                if more:
                    group_root(i + 1)
                    copy_v(i + 1)

            act.wait_ge(eps_set, 2)
            act.wait_ge(const_loaded, 16 * NCONST)
            act.activation(bns[:, :, 0], bnp[:, :, 1], ACT.Sqrt, bias=eps[:, 0:1]).then_inc(set_up, 1)
            act.wait_ge(set_up, 3)
            gelu(0, 0, PIX)
            group_root(0)
            copy_v(0)
            pairs_of(act, chain)

        @block.vector
        def _(dve):
            count = {"ew": 0, "stat": 0}
            EW_STEPS, STAT_STEPS = 10, 6

            def link(ins, i, what):
                count[what] += 1
                s, n = (ew_step, EW_STEPS) if what == "ew" else (stat_step, STAT_STEPS)
                ins.then_inc(s, 1)
                dve.wait_ge(s, i * n + count[what])

            def take(i, k, out_ap, in_ap):
                wait_fill(dve, i, k)
                dve.tensor_copy(out_ap, in_ap).then_inc(taken["dve"], 1)

            def stats(i, slot, k0, k1):
                for k in range(k0, k1):
                    img, t, q = place(k)
                    dve.wait_ge(x1_done, i * PIX + k + 1)
                    dve.bn_stats(st[:, img * NT + t, q, :], x1[slot][:, img, t, q * CH:(q + 1) * CH]).then_inc(x1_counted, 1)

            def group_stats(i):
                count["stat"] = 0
                dve.wait_ge(x1_counted, (i + 1) * PIX)
                dve.memset(gtmp[:, :], 0.0)
                for k in range(2 * NT):
                    ins = dve.bn_aggr(mv[:, k, :], st[:, k, :, :].rearrange("p a s -> p (a s)"))
                link(ins, i, "stat")
                link(dve.tensor_tensor(gtmp[:, :], mv[:, :, 0], mv[:, :, 0], ALU.mult), i, "stat")
                dve.tensor_tensor(mv[:, :, 1], mv[:, :, 1], gtmp[:, :], ALU.add).then_inc(chan_stats, 1)
                dve.wait_ge(group_sums, i + 1)
                link(dve.tensor_copy(gst[:, :, :].rearrange("p k s -> p (k s)"), gps[0:TP, 0:4 * NT]), i, "stat")
                link(dve.tensor_tensor(gtmp[:, :], gst[:, :, 0], gst[:, :, 0], ALU.mult), i, "stat")
                dve.tensor_tensor(gst[:, :, 1], gst[:, :, 1], gtmp[:, :], ALU.subtract).then_inc(group_var, 1)
                dve.wait_ge(group_std, i + 1)
                link(dve.reciprocal(rstd[:, :], gstd[:, :]), i, "stat")
                for k in range(2 * NT):
                    ins = dve.tensor_scalar(conv1s[:, k, :], conv1[:, k % NT, :], rstd[:, k:k + 1], None, ALU.mult)
                ins.then_inc(w_scaled, 1)
                dve.wait_ge(vbias_sum, i + 1)
                link(dve.tensor_scalar(vbias[:, :], gps[0:C1, 16:18], -1.0, None, ALU.mult), i, "stat")
                dve.tensor_copy(gtmp[:, 0:1], rstd[:, 0:1]).then_inc(vbias_done, 1)
                assert count["stat"] == STAT_STEPS

            def chain(i, slot, more):
                count["ew"] = 0
                for n, dst, w in (("s1f", a1f, 512), ("s1r", a1r, 8 * KW)):
                    for c in (0, 2):
                        k = INDEX[n, c]
                        take(i, k, dst[:, 4 * c:4 * c + 4, :, :].rearrange("p c r n -> p (c r n)"), stage[k % 3][:, 0:w])
                for n, off, w in (("s2f", 0, 512), ("s2r", FR, 8 * KW)):
                    for c in range(2):
                        k = INDEX[n + "_im", c]
                        take(i, k, im[:, off + c * w:off + (c + 1) * w], stage[k % 3][:, 0:w])
                dve.wait_ge(squared, 2 * i + 2)
                dve.tensor_tensor(mod, mod, ang, ALU.add).then_inc(sq_summed, 1)
                dve.wait_ge(mod_done, i + 1)
                link(dve.scalar_tensor_tensor(ang, ang, 1e-30, mod, ALU.max, ALU.add), i, "ew")
                link(dve.reciprocal(ang, ang), i, "ew")
                dve.tensor_tensor(ang, im, ang, ALU.mult).then_inc(ratio_done, 1)
                dve.wait_ge(ratio_done, i + 1)
                link(dve.tensor_scalar(im, im, 0.0, -0.5, ALU.is_ge, ALU.add), i, "ew")
                dve.wait_ge(atan_done, i + 1)
                link(dve.scalar_tensor_tensor(im, ang, -2.0 / math.pi, im, ALU.mult, ALU.add), i, "ew")
                link(dve.scalar_tensor_tensor(re, re, 0.0, im, ALU.is_lt, ALU.mult), i, "ew")
                dve.scalar_tensor_tensor(ang, re, math.pi, ang, ALU.mult, ALU.add).then_inc(ang_done, 1)
                dve.wait_ge(f_loaded, (i + 1) * 128)
                for img in range(2):
                    ins = dve.tensor_tensor(magi[:, img, :], magb[:, img, :], mask[:, 0, :, :].rearrange("p r n -> p (r n)"), ALU.mult)
                link(ins, i, "ew")
                for img in range(2):
                    ins = dve.tensor_tensor(magb[:, img, :], magb[:, img, :], mask[:, 1, :, :].rearrange("p r n -> p (r n)"), ALU.mult)
                ins.then_inc(masked, 1)
                inner = slice(H0, H0 + H1)
                for img in range(2):
                    k = INDEX["outer", img]
                    wait_fill(dve, i, k)
                    dve.scalar_tensor_tensor(mixu[:, img, :, :].rearrange("p r n -> p (r n)"), stage[k % 3][:, :], bias[:, 1:2],
                                             mask[:, 1, :, :].rearrange("p r n -> p (r n)"), ALU.add, ALU.mult).then_inc(taken["dve"], 1)
                    k = INDEX["inner", img]
                    wait_fill(dve, i, k)
                    dve.scalar_tensor_tensor(mixt[:, img, :, :], stage[k % 3][:, 0:8 * H1].rearrange("p (r n) -> p r n", n=H1),
                                             bias[:, 0:1], mask[:, 0, :, inner], ALU.add, ALU.mult).then_inc(taken["dve"], 1)
                    dve.wait_ge(taken["dve"], i * TAKES["dve"] + 8 + 2 * (img + 1))
                    dve.tensor_tensor(mixu[:, img, :, inner], mixu[:, img, :, inner], mixt[:, img, :, :], ALU.add).then_inc(mixed, 1)
                if more:
                    stats(i + 1, 1 - slot, 0, 16)
                dve.wait_ge(taken["act"], i * TAKES["act"] + 16)
                phf, mof = ph[:, :, :].rearrange("p i n -> p (i n)"), mo[:, :, :].rearrange("p i n -> p (i n)")
                link(dve.tensor_scalar(im2, phf, 1.0 / TWO_PI, ROUND, ALU.mult, ALU.add), i, "ew")
                link(dve.tensor_scalar(im2, im2, ROUND, None, ALU.subtract), i, "ew")
                link(dve.scalar_tensor_tensor(re2, im2, -TWO_PI_HI, phf, ALU.mult, ALU.add), i, "ew")
                link(dve.scalar_tensor_tensor(im2, im2, -(TWO_PI - TWO_PI_HI), re2, ALU.mult, ALU.add), i, "ew")
                dve.tensor_scalar(im2, im2, 3.1415925, -3.1415925, ALU.min, ALU.max).then_inc(turn_done, 1)
                dve.wait_ge(sin_done, 2 * i + 2)
                dve.tensor_tensor(re2, re2, mof, ALU.mult)
                dve.tensor_tensor(im2, im2, mof, ALU.mult).then_inc(g_done, 1)
                for n, dst, p in (("s3f", h1f, 128), ("s3r", h1r, KW)):
                    for c in (0, 2):
                        k = INDEX[n, c]
                        wait_fill(dve, i, k)
                        if p == 128:
                            dve.tensor_copy(dst[:, 4 * c:4 * c + 4, :, :].rearrange("p c r n -> p (c r n)"), stage[k % 3][:, :]
                                            ).then_inc(taken["dve"], 1)
                        else:
                            for img in range(2):
                                rows = slice(img * S, img * S + KW)
                                ins = dve.tensor_copy(dst[rows, 4 * c:4 * c + 4, :, :].rearrange("p c r n -> p (c r n)"),
                                                      stage[k % 3][rows, :])
                            ins.then_inc(taken["dve"], 1)
                for c in range(2):
                    k = INDEX["s4r", c]
                    wait_fill(dve, i, k)
                    dve.tensor_copy(zt[:, CM + 8 * c:CM + 8 * c + 8, :].rearrange("p c n -> p (c n)"), stage[k % 3][:, :]
                                    ).then_inc(taken["dve"], 1)
                dve.wait_ge(taken["dve"], (i + 1) * TAKES["dve"])
                dve.tensor_copy(gtmp[:, 0:1], rstd[:, 0:1]).then_inc(z_real, 1)
                dve.wait_ge(taken["act"], (i + 1) * TAKES["act"])
                dve.tensor_tensor(sq[:, 0, :], sq[:, 0, :], sq[:, 1, :], ALU.add).then_inc(z_summed, 1)
                if more:
                    stats(i + 1, 1 - slot, 16, PIX)
                    group_stats(i + 1)
                for j in range(2 * NCH):
                    img, q = divmod(j, NCH)
                    for t in range(NT):
                        dve.wait_ge(o_filled, i * PIX + 2 * j + t + 1)
                        dst = x1[slot][:, img, t, :].rearrange("p (h w) -> p w h", w=S)[:, 8 * q:8 * q + 8, :]
                        dve.scalar_tensor_tensor(dst, ops[t][:, :].rearrange("p (w h) -> p w h", h=S), cbias[:, t:t + 1], dst,
                                                 ALU.add, ALU.add).then_inc(o_added, 1)
                print("ew steps", count["ew"]) if count["ew"] != EW_STEPS else None

            dve.wait_ge(set_up, 1)
            dve.reciprocal(bns[:, :, 0], bns[:, :, 0]).then_inc(setup_step, 1)
            dve.wait_ge(setup_step, 1)
            dve.tensor_tensor(bns[:, :, 0], bns[:, :, 0], affine[:, 0, :], ALU.mult).then_inc(setup_step, 1)
            dve.wait_ge(setup_step, 2)
            dve.tensor_tensor(bns[:, :, 1], bns[:, :, 0], bnp[:, :, 0], ALU.mult).then_inc(setup_step, 1)
            dve.wait_ge(setup_step, 3)
            dve.tensor_tensor(bns[:, :, 1], affine[:, 1, :], bns[:, :, 1], ALU.subtract).then_inc(set_up, 1)
            dve.wait_ge(setup_sum, 1)
            dve.tensor_copy(conv2[0:CM, :], gps[0:CM, 32:32 + C])
            dve.tensor_copy(cbias[:, :], gps[0:TP, 20:22]).then_inc(set_up, 1)
            stats(0, 0, 0, PIX)
            group_stats(0)
            pairs_of(dve, chain)

        @block.tensor
        def _(pe):
            def fill(i, k, products):
                before = k - 3
                if before >= 0:
                    e = FILLS[before][2]
                    pe.wait_ge(taken[e], i * TAKES[e] + sum(x == e for _, _, x in FILLS[:before + 1]))
                else:
                    e = FILLS[before][2]
                    pe.wait_ge(taken[e], i * TAKES[e])
                if products[0][1].shape[0] <= S and products[0][0].shape[0] <= S:
                    pe.sem_inc(passed["pe"], 1)
                for args in products:
                    ins = pe.matmul(*args[:3], start=args[3], stop=args[4])
                ins.then_inc(filled, 1)

            def conv_first(i, slot):
                pe.wait_ge(chan_stats, i + 1)
                pe.matmul(gps[0:TP, 0:4 * NT], group[:, :], mv[:, :, :].rearrange("p k s -> p (k s)"), start=True, stop=True
                          ).then_inc(group_sums, 1)
                pe.wait_ge(w_scaled, i + 1)
                for img in range(2):
                    for t in range(NT):
                        ins = pe.matmul(gps[0:C1, 16 + img:17 + img], conv1s[:, img * NT + t, :], gst[:, img * NT + t, 0:1],
                                        start=(t == 0), stop=(t == NT - 1))
                ins.then_inc(vbias_sum, 1)
                for k in range(2 * NCH):
                    img, q = divmod(k, NCH)
                    pe.wait_ge(v_copied, i * (2 * NCH) + max(k - 1, 0))
                    for t in range(NT):
                        rhs = x1[slot][:, img, t, :].rearrange("p (h w) -> p w h", w=S)[:, 8 * q:8 * q + 8, :]
                        ins = pe.matmul(vps[k % 2][:, :], conv1s[:, img * NT + t, :], rhs, start=(t == 0), stop=(t == NT - 1))
                    ins.then_inc(v_filled, 1)

            def chain(i, slot, more):
                pe.wait_ge(xw_loaded, 32 * i + 32)
                for name, w, c0, d in (("s1f", 128, 0, D_S1F), ("s1r", 2 * KW, CM, D_S1R)):
                    for c in range(4):
                        k = INDEX[name, c]
                        fill(i, k, [(stage[k % 3][img * S:(img + 1) * S, w * g:w * (g + 1)], xw[img * S:(img + 1) * S, c0 + 4 * c + g, :],
                                     dft[img * S:(img + 1) * S, d, 0:w], True, True) for g in range(4) for img in range(2)])
                pe.wait_ge(taken["act"], i * TAKES["act"] + 4)
                pe.wait_ge(taken["dve"], i * TAKES["dve"] + 4)
                for name, src, d, w in (("s2f", a1f, D_S2F, S), ("s2r", a1r, D_S2R, KW)):
                    for c in range(2):
                        r, m = src[:, 8 * c:8 * c + 8, 0, :], src[:, 8 * c:8 * c + 8, 1, :]
                        for part, terms in (("_re", ((d, r), (d + 2, m))), ("_im", ((d + 1, r), (d, m)))):
                            k = INDEX[name + part, c]
                            fill(i, k, [(stage[k % 3][:, 0:8 * w], dft[:, dd, :], rhs, n == 0, n == 1) for n, (dd, rhs) in enumerate(terms)])
                pe.wait_ge(masked, i + 1)
                for img in range(2):
                    k = INDEX["outer", img]
                    fill(i, k, [(stage[k % 3][:, :], mix[:, M_OUTER, :], magb[:, img, :], True, True)])
                    k = INDEX["inner", img]
                    o = stage[k % 3][:, 0:8 * H1].rearrange("p (r n) -> p r n", n=H1)
                    src = magi[:, img, :].rearrange("p (r n) -> p r n", n=S)

                    def cols(dx):
                        return slice(H0 + dx - 1, H0 + dx - 1 + H1)

                    prods = [(o, mix[:, M_TAP + 3 + dx, :], src[:, :, cols(dx)], dx == 0, False) for dx in range(3)]
                    prods += [(o[:, 1:8, :], mix[:, M_TAP + dx, :], src[:, 0:7, cols(dx)], False, False) for dx in range(3)]
                    prods += [(o[:, 0:7, :], mix[:, M_TAP + 6 + dx, :], src[:, 1:8, cols(dx)], False, False) for dx in range(3)]
                    prods += [(o[:, 0, :], mix[:, M_UP + dx, :], src[:, 7, cols(dx)], False, False) for dx in range(3)]
                    prods += [(o[:, 7, :], mix[:, M_DOWN + dx, :], src[:, 0, cols(dx)], False, dx == 2) for dx in range(3)]
                    fill(i, k, prods)
                    for name, m, rhs, w in (("phase", M_PHASE, angb[:, img, :], CH), ("rmod", M_REAL, rblk[:, img, 0, :], BR),
                                            ("rang", M_REAL, rblk[:, img, 1, :], BR)):
                        k = INDEX[name, img]
                        fill(i, k, [(stage[k % 3][:, 0:w], mix[:, m, :], rhs, True, True)])
                    k = INDEX["mod", img]
                    pe.wait_ge(mixed, 2 * i + img + 1)
                    fill(i, k, [(stage[k % 3][:, :], mix[:, M_MOD, :], mixu[:, img, :, :].rearrange("p r n -> p (r n)"), True, True)])
                pe.wait_ge(g_loaded, (i + 1) * 128)
                for name, src, n, d in (("s3f", gt, S, D_S3F), ("s3r", pt, KW, D_S3R)):
                    for c in range(4):
                        k = INDEX[name, c]
                        fill(i, k, [(stage[k % 3][img * S:img * S + n, 128 * g:128 * (g + 1)], src[:, img, 4 * c + g, :], dft[:, d, :], True, True)
                                    for g in range(4) for img in range(2)])
                n3 = 16 + 4
                pe.wait_ge(taken["act"], i * TAKES["act"] + n3)
                pe.wait_ge(taken["dve"], i * TAKES["dve"] + 12 + 4)
                for c in range(2):
                    r, m = h1f[:, 8 * c:8 * c + 8, 0, :], h1f[:, 8 * c:8 * c + 8, 1, :]
                    for part, terms in (("_re", ((D_S4F, r), (D_S4F + 2, m))), ("_im", ((D_S4F + 1, r), (D_S4F, m)))):
                        k = INDEX["s4f" + part, c]
                        fill(i, k, [(stage[k % 3][:, :], dft[:, dd, :], rhs, n == 0, n == 1) for n, (dd, rhs) in enumerate(terms)])
                for c in range(2):
                    k = INDEX["s4r", c]
                    fill(i, k, [(stage[k % 3][img * S:(img + 1) * S, :], dft[img * S:img * S + KW, D_S4R + r, 0:S],
                                 h1r[img * S:img * S + KW, 8 * c:8 * c + 8, r, :], r == 0, r == 1) for img in range(2) for r in range(2)])
                if more:
                    conv_first(i + 1, 1 - slot)
                for j in range(2 * NCH):
                    img, q = divmod(j, NCH)
                    pe.wait_ge(z_loaded[j % 2], i * 256 + 32 * (j // 2 + 1))
                    for t in range(NT):
                        pe.wait_ge(o_added, i * PIX + max(2 * j + t - 1, 0))
                        pe.matmul(ops[t][:, :], conv2[:, t * TP:(t + 1) * TP], zch[j % 2][:, :], start=True, stop=True).then_inc(o_filled, 1)

            pe.wait_ge(const_loaded, 16 * NCONST)
            pe.matmul(gps[0:CM, 32:32 + C], c0w[:, :], conv2a[:, :], start=True, stop=True)
            for t in range(NT):
                ins = pe.matmul(gps[0:TP, 20 + t:21 + t], conv2a[:, t * TP:(t + 1) * TP], c0b[:, :], start=True, stop=True)
            ins.then_inc(setup_sum, 1)
            conv_first(0, 0)
            pairs_of(pe, chain)


def frft_matrix(N, a):
    shift = None
    if a < 0.5:
        shft = (np.arange(N) + int(np.fix(N / 2))) % N
        inv = np.argsort(shft)
        W = np.exp(2j * np.pi * np.outer(np.arange(N), np.arange(N)) / N) / math.sqrt(N)
        shift = W[inv, :][:, inv]
        a = a + 1.0
    alpha = a * math.pi / 2
    tana2, sina = math.tan(alpha / 2), math.sin(alpha)
    up = np.zeros((2 * N - 1, N))
    up[::2] = np.eye(N)
    kern = np.sinc(np.arange(-(2 * N - 3), 2 * N - 2) / 2.0)
    fi = np.stack([np.convolve(up[:, k], kern)[2 * N - 3:4 * N - 4] for k in range(N)], 1)
    fp = np.concatenate([np.zeros((N - 1, N)), fi, np.zeros((N - 1, N))], 0).astype(complex)
    n = np.arange(-2 * N + 2, 2 * N - 1).astype(float)
    chrp = np.exp(-1j * math.pi / N * tana2 / 4 * n ** 2)
    fp = chrp[:, None] * fp
    c = math.pi / N / sina / 4
    m = np.arange(-(4 * N - 4), 4 * N - 3).astype(float)
    kern = np.exp(1j * c * m ** 2)
    ret = np.stack([np.convolve(fp[:, k], kern)[4 * N - 4:8 * N - 7] for k in range(N)], 1) * math.sqrt(c / math.pi)
    ret = chrp[:, None] * ret
    M = np.exp(-1j * (1 - a) * math.pi / 4) * ret[N - 1:3 * N - 2:2]
    return M @ shift if shift is not None else M


def transforms():
    T, U = frft_matrix(S, 0.5), frft_matrix(S, -0.5)
    k = np.arange(S)
    turn = (np.outer(k, k) % S)
    cos, sin = np.round(np.cos(2 * np.pi * turn / S), 15), np.round(np.sin(2 * np.pi * turn / S), 15)
    d = np.zeros((128, D_N, 128))
    for img in range(2):
        r = slice(img * S, (img + 1) * S)
        d[r, D_S1F, :] = np.concatenate([T.real.T, T.imag.T], 1)
        d[r, D_S1R, 0:2 * KW] = np.concatenate([cos[:, 0:KW], -sin[:, 0:KW]], 1)
        for slot, a, b in ((D_S2F, T.real, T.imag), (D_S2R, cos, -sin), (D_S4F, U.real, U.imag)):
            d[r, slot, r], d[r, slot + 1, r], d[r, slot + 2, r] = a.T, b.T, -b.T
        c = np.full((KW, 1), 2.0 / S)
        c[0] = c[-1] = 1.0 / S
        d[img * S:img * S + KW, D_S4R, 0:S] = c * cos[0:KW]
        d[img * S:img * S + KW, D_S4R + 1, 0:S] = -c * sin[0:KW]
    for slot, a, b in ((D_S3F, U.real, U.imag), (D_S3R, cos / S, sin / S)):
        d[:, slot, :] = np.block([[a.T, b.T], [-b.T, a.T]])
    return (d + 0.0).astype(np.float32)


def masks():
    m = np.zeros((S, S), np.float32)
    m[H0:H0 + H1, H0:H0 + H1] = 1.0
    m = np.tile(m.reshape(8, 8, S), (CM, 1, 1))
    return np.stack([m, 1 - m], 1)


def spread(w, shift=0):
    m = np.zeros((CM, 8, CM, 8), w.dtype)
    for b in range(8):
        if 0 <= b + shift < 8:
            m[:, b, :, b + shift] = w.T
    return m.reshape(128, 128)


def mixing(mag_s_w, mag_f_w, mag_w, pha_w, conv_1_w):
    taps = [spread(mag_s_w[:, :, dy, dx]) for dy in range(3) for dx in range(3)]
    up = [spread(mag_s_w[:, :, 0, dx], 1) for dx in range(3)]
    down = [spread(mag_s_w[:, :, 2, dx], -1) for dx in range(3)]
    return np.ascontiguousarray(np.stack(taps + up + down + [spread(mag_f_w), spread(mag_w), spread(pha_w), spread(conv_1_w)], 1))


def biases(*b):
    return np.stack([np.repeat(x, 8) for x in b], 1)


def two_layers(nc, x, w0, b0, ident, group, imgsum, affine, conv1, conv2, c0w, c0b, mix, bias, mask, dft, out):
    B = x.shape[0]

    def scratch(name, shape):
        return nc.dram_tensor(name, shape, F32, kind="Internal").ap()

    y_d, bn_d = scratch("y_d", [B, C, HW]), scratch("bn_d", [TP, NT, 2])
    with ExitStack() as sems:
        layer0_conv(nc, sems, x, w0, b0, ident, group, imgsum, y_d, bn_d)
        layer1(nc, sems, x, y_d, bn_d, affine, group, conv1, conv2, c0w, c0b, mix, bias, mask, dft, out,
               scratch("v_d", [B, C1, HW]), scratch("f_d", [B, 2, CM, S, S]), scratch("r_d", [B, 2, CM, S, KW]),
               scratch("g_d", [B, 2, CM, S, S]), scratch("p_d", [B, 2, CM, S, KW]), scratch("z_d", [B, 2 * CM, S, S]))


def kernel(**inputs):
    import concourse.bacc as _bacc
    from concourse.bass_utils import run_bass_kernel_spmd as _run

    a = {k.replace("L0_conv_", "").replace("L1_conv_", ""): np.asarray(v) for k, v in inputs.items()}

    def by_tile(v):
        return v.reshape(NT, TP).T

    ins = {
        "x": a["x"],
        "w0": a["conv_w"].T.reshape(2 * NT, TP, C).transpose(1, 0, 2),
        "b0": by_tile(a["conv_b"]),
        "ident": np.eye(128, dtype=np.float32),
        "group": np.kron(np.eye(TP // 6), np.full((6, 6), 1 / 6)).astype(np.float32),
        "imgsum": np.kron(np.eye(2), np.full((S, S), 2.0 / HW)).astype(np.float32),
        "affine": np.stack([by_tile(a["bn_gamma"]), by_tile(a["bn_beta"])], 1),
        "conv1": a["conv1_w"].T.reshape(NT, TP, C1).transpose(1, 0, 2),
        "conv2": a["conv2_w"].T,
        "c0w": a["conv_0_w"],
        "c0b": a["conv_0_b"][:, None],
        "mix": mixing(a["mag_s_w"], a["mag_f_w"], a["mag_w"], a["pha_w"], a["conv_1_w"]),
        "bias": biases(a["mag_s_b"], a["mag_f_b"], a["mag_b"], a["pha_b"], a["conv_1_b"]),
        "mask": masks(),
        "dft": transforms(),
    }
    nc = _bacc.Bacc("TRN2", target_bir_lowering=False, num_devices=1)
    arrays, args = {}, []
    for name, v in ins.items():
        arrays[f"in_{name}_dram"] = np.ascontiguousarray(v)
        args.append(nc.dram_tensor(f"in_{name}_dram", v.shape, mybir.dt.from_np(v.dtype), kind="ExternalInput").ap())
    args.append(nc.dram_tensor("out_0_dram", a["x"].shape, F32, kind="ExternalOutput").ap())
    two_layers(nc, *args)
    r = _run(nc, [arrays], core_ids=[0])
    return r.results[0]["out_0_dram"]
```

```python
import math

import numpy as np
import concourse.bass as bass
from concourse import mybir
from contextlib import ExitStack

F32 = mybir.dt.float32
ALU = mybir.AluOpType
ACT = mybir.ActivationFunctionType
AX = mybir.AxisListType

TP = 96
NT = 2
C = TP * NT
S = 64
HW = S * S
K = 8
NP = S // K
ROW = HW // NP
BIG = 1.0e30


def pairs_of_line():
    a = [(p, p + s) for s in (1, 2) for p in range(NP - s)]
    b = [(p, p + s) for s in range(3, NP) for p in range(NP - s)]
    return a, b


def layer0_conv(nc, sems, x, w0_d, b0_d, ident_d, group_d, imgsum_d, y_d, bn_d):
    B = x.shape[0]
    PAIRS = B // 2
    PA, PB = pairs_of_line()
    NA, NB = len(PA), len(PB)
    NL = 2 * NP
    xv = x.rearrange("b (t p) h w -> p b t (h w)", p=TP)
    yv = y_d.rearrange("b (t p) n -> p b t n", p=TP)

    with ExitStack() as ctx:
        def sb(name, shape):
            return ctx.enter_context(nc.sbuf_tensor(name, shape, F32))

        def ps(name, shape):
            return ctx.enter_context(nc.psum_tensor(name, shape, F32))

        def sem(name):
            return sems.enter_context(nc.semaphore(name))

        xraw = sb("xraw", [TP, NT, ROW])
        xc = sb("xc", [TP, NT, NP, NP, 2, K * K])
        xp = sb("xp", [128, NP * NP, C])
        best = sb("best", [128, NP * NP, C])
        diff = sb("diff", [128, NA + NB, C])
        xjc = sb("xjc", [TP, NT, NP, 2, S])
        ysb = sb("ysb", [TP, 2, NT, ROW])
        xlast = diff[0:TP, NA:, :].rearrange("p u c -> p (u c)")[:, 0:2 * NT * ROW].rearrange("p (i t n) -> p i t n", i=2, t=NT)
        w0 = sb("w0", [TP, 4, C])
        b0 = sb("b0", [TP, NT])
        ident = sb("ident", [128, 128])
        group = sb("group", [TP, TP])
        imgsum = sb("imgsum", [128, 128])
        xsum = sb("xsum", [TP, 2 * NT, 2])
        xacc = sb("xacc", [TP, 2 * NT, 2])
        yst = sb("yst", [TP, NT, 2 * NP, 6])
        mv = sb("mv", [TP, 2 * NT, 2])
        gst = sb("gst", [TP, 2 * NT, 2])
        gtmp = sb("gtmp", [TP, 2 * NT])
        gstd = sb("gstd", [TP, 2 * NT])
        rstd = sb("rstd", [TP, 2 * NT])
        nbias = sb("nbias", [TP, 2 * NT])
        eps = sb("eps", [TP, 1])
        ymv = sb("ymv", [TP, NT, 3])
        yagg = sb("yagg", [TP, NT, PAIRS, 3])
        ybn = sb("ybn", [TP, NT, 2])
        dist_e = sb("dist_e", [128, NP * NP // 2])
        esum = sb("esum", [128, 1])
        emean = sb("emean", [128, 1])
        esq = sb("esq", [128, 1])
        estd = sb("estd", [128, 1])
        thresh = sb("thresh", [128, 1])
        dist = sb("dist", [128, NA + NB])
        pen = sb("pen", [128, NA + NB])

        tps = [ps(f"tps{n}", [128, 2, 512]) for n in range(2)]
        YB = 3
        yps = [ps(f"yps{n}", [TP, 512]) for n in range(YB)]
        sps = ps("sps", [128, 16])

        const_loaded = sem("const_loaded")
        eps_set = sem("eps_set")
        stat_loaded = sem("stat_loaded")
        x_loaded = sem("x_loaded")
        xlast_loaded = sem("xlast_loaded")
        x_grouped = sem("x_grouped")
        xstat_done = sem("xstat_done")
        xstat_added = sem("xstat_added")
        xsum_read = sem("xsum_read")
        stat_step = sem("stat_step")
        chan_stats = sem("chan_stats")
        group_sums = sem("group_sums")
        group_var = sem("group_var")
        group_std = sem("group_std")
        norm_ready = sem("norm_ready")
        tp_filled = sem("tp_filled")
        evac_act = sem("evac_act")
        edist_part = sem("edist_part")
        edist_mean = sem("edist_mean")
        edist_sq = sem("edist_sq")
        edist_diff = sem("edist_diff")
        edist_step = sem("edist_step")
        edist_var = sem("edist_var")
        edist_std = sem("edist_std")
        diff_a = sem("diff_a")
        diff_b = sem("diff_b")
        dist_a = sem("dist_a")
        dist_b = sem("dist_b")
        pen_a = sem("pen_a")
        pen_b = sem("pen_b")
        best_a = sem("best_a")
        best_b = sem("best_b")
        xj_done = sem("xj_done")
        y_filled = sem("y_filled")
        y_copied = sem("y_copied")
        y_counted = sem("y_counted")
        y_stored = [sem(f"y_stored{n}") for n in range(2)]
        bn_step = sem("bn_step")
        bn_ready = sem("bn_ready")
        bn_stored = sem("bn_stored")
        passed = sem("passed_rows")

        block = ctx.enter_context(nc.Block())

        def by_column(t):
            return t[:, :, :].rearrange("p (a b) c -> p a b c", b=NP)

        def line_of(t, along_rows, line, p0, n):
            v = by_column(t)
            if along_rows:
                return v[:, bass.ds(line, 1), p0:p0 + n, :].rearrange("p l n c -> p (l n) c")
            return v[:, p0:p0 + n, bass.ds(line, 1), :].rearrange("p n l c -> p n (l c)")

        GSTEPS, ESTEPS = 3, 3
        FILLS = 4 * NP

        def first_fill(i):
            return i * FILLS + 2 * NP

        def fill_back(r, more):
            return 4 * r - 2 if more and r else 2 * r

        def fill_next(r):
            return 4 * r + 4 if r < NP - 1 else FILLS - 2

        def pairs_of(eng, body):
            if PAIRS > 1:
                body(0, True)
            if PAIRS > 2:
                with eng.Fori(1, PAIRS - 1) as i:
                    body(i, True)
            body(PAIRS - 1, False)

        @block.sync
        def _(sp):
            def load_stat(i, a):
                n, ny = sp.snap((i * NP + a) * 2 * NT), sp.snap(2 * i)
                sp.wait_ge(xstat_done, n)
                sp.dma_start(ysb[:, :, :, :], xv[:, bass.ds(ny, 2), :, a * ROW:(a + 1) * ROW]).then_inc(stat_loaded, 16)

            def load_row(i, a, img):
                n, ni = sp.snap((i * NP + a) * 4 + 2 * img), sp.snap(2 * i + img)
                src = xv[:, bass.ds(ni, 1), :, a * ROW:(a + 1) * ROW].rearrange("p b t n -> p (b t) n")
                if a < NP - 1:
                    sp.wait_ge(x_grouped, n)
                    sp.dma_start(xraw[:, :, :], src).then_inc(x_loaded, 16)
                else:
                    sp.dma_start(xlast[:, img, :, :], src).then_inc(xlast_loaded, 16)

            def pair(i, more):
                if more:
                    stored, counted = sp.snap(i * (16 * NP)), sp.snap(i * (4 * NP))
                    for s, n in ((y_stored[0], stored), (y_stored[1], stored), (y_counted, counted)):
                        sp.wait_ge(s, n)
                        sp.sem_inc(passed, 1)
                    for a in range(NP):
                        load_stat(i + 1, a)
                    load_row(i + 1, 0, 0)
                for a in range(NP):
                    for img in range(2):
                        ni = sp.snap(2 * i + img)
                        sp.wait_ge(y_copied, i * (4 * NP) + 4 * a + 2 * (img + 1))
                        sp.dma_start(yv[:, bass.ds(ni, 1), :, a * ROW:(a + 1) * ROW].rearrange("p b t n -> p (b t) n"),
                                     ysb[:, img, :, :]).then_inc(y_stored[img], 16)
                    if more and a < NP - 1:
                        load_row(i + 1, a, 1)
                        if a < NP - 2:
                            load_row(i + 1, a + 1, 0)
                        if a == NP - 3:
                            nd = sp.snap(i * NL + NL)
                            sp.wait_ge(dist_b, nd)
                            sp.sem_inc(passed, 1)
                            for img in range(2):
                                load_row(i + 1, NP - 1, img)

            for dst, src in ((w0[:, :, :], w0_d), (b0[:, :], b0_d), (ident[:, :], ident_d),
                             (group[:, :], group_d), (imgsum[:, :], imgsum_d)):
                sp.dma_start(dst, src).then_inc(const_loaded, 16)
            for a in range(NP):
                load_stat(0, a)
            for a in range(NP):
                for img in range(2):
                    load_row(0, a, img)
            pairs_of(sp, pair)
            sp.wait_ge(bn_ready, 1)
            sp.dma_start(bn_d, ybn[:, :, :]).then_inc(bn_stored, 16)
            for n in range(2):
                sp.wait_ge(y_stored[n], 16 * NP * PAIRS)
            sp.wait_ge(bn_stored, 16)

        @block.gpsimd
        def _(pool):
            pool.memset(eps[:, :], 1e-5).then_inc(eps_set, 1)

            def line(i, along_rows, l, begun=False):
                n = pool.snap(i * NL + (NP if along_rows else 0) + l)
                for half, s0, s1, ready, used, at in ((0, 1, 2, diff_a, dist_a, 0), (1, 3, 7, diff_b, dist_b, NA)):
                    pool.wait_ge(used, n)
                    for s in range(s0, s1 + 1):
                        m = NP - s
                        p0 = m - 1 if begun and half == 0 else 0
                        ins = pool.tensor_tensor(diff[:, at + p0:at + m, :], line_of(xp, along_rows, l, s + p0, m - p0),
                                                 line_of(xp, along_rows, l, p0, m - p0), ALU.subtract)
                        at += m
                    ins.then_inc(ready, 1)

            def begin(i):
                pool.wait_ge(dist_a, i * NL)
                pool.wait_ge(evac_act, first_fill(i) - FILLS + fill_next(NP - 2) + 2)
                at = 0
                for s in (1, 2):
                    m = NP - s
                    pool.tensor_tensor(diff[:, at:at + m - 1, :], line_of(xp, False, 0, s, m - 1),
                                       line_of(xp, False, 0, 0, m - 1), ALU.subtract)
                    at += m

            def finish(i, a):
                pool.wait_ge(best_b, (i * NL + NP + a + 1) * 2 * NB)
                r = best[:, :, :].rearrange("p (a b) c -> p a (b c)", b=NP)[:, bass.ds(a, 1), :].rearrange("p a n -> p (a n)")
                q = xp[:, :, :].rearrange("p (a b) c -> p a (b c)", b=NP)[:, bass.ds(a, 1), :].rearrange("p a n -> p (a n)")
                pool.tensor_tensor(r, r, q, ALU.subtract).then_inc(xj_done, 1)

            def pair(i, more):
                pool.wait_ge(evac_act, first_fill(i))
                line(i, False, 0, not isinstance(i, int) or i > 0)
                with pool.Fori(1, NP) as l:
                    line(i, False, l)
                line(i, True, 0)
                with pool.Fori(1, NP) as l:
                    line(i, True, l)
                    finish(i, l - 1)
                finish(i, NP - 1)
                if more:
                    begin(i + 1)

            pairs_of(pool, pair)

        @block.scalar
        def _(act):
            act.wait_ge(eps_set, 1)
            act.wait_ge(const_loaded, 16 * 5)

            def distances(i, along_rows, l, halves=(0, 1)):
                n = act.snap(i * NL + (NP if along_rows else 0) + l)
                for half in halves:
                    u0, m, ready, done, used = ((0, NA, diff_a, dist_a, pen_a), (NA, NB, diff_b, dist_b, pen_b))[half]
                    act.wait_ge(ready, n + 1)
                    act.wait_ge(used, n)
                    for u in range(u0, u0 + m):
                        ins = act.activation(diff[:, u, :], diff[:, u, :], ACT.Abs, accum_out=dist[:, u:u + 1])
                    ins.then_inc(done, 1)

            def row(i, r, more):
                base = act.snap(i * (4 * NP) + 4 * r)
                if more and r == 0:
                    act.wait_ge(xstat_done, (i + 2) * (2 * NT * NP))
                for t in range(NT):
                    act.wait_ge(tp_filled, first_fill(i) + fill_back(r, more) + t + 1)
                    act.wait_ge(y_filled, base)
                    act.activation(xjc[:, t, :, :, :].rearrange("p b i n -> p (b i n)"),
                                   tps[t][0:TP, :, :].rearrange("p a n -> p (a n)"), ACT.Identity).then_inc(evac_act, 1)
                if r + 2 < NP:
                    distances(i, True, r + 2, (0,))
                if more and r > 0:
                    regroup(i + 1, r - 1, 1)
                rows = act.snap(i * NP + r)
                for g in range(4):
                    img, o = divmod(g, NT)
                    if more and r > 0 and g == 2:
                        fill_xp(first_fill(i) + fill_next(r - 1), r - 1)
                    if g == 0 and r + 2 < NP:
                        distances(i, True, r + 2, (1,))
                    if o == 0:
                        act.wait_ge(y_stored[img], rows * 16)
                        act.wait_ge(y_counted, base + (g - 2 if r else 0))
                    act.wait_ge(y_filled, base + g + 1)
                    act.activation(ysb[:, img, o, :].rearrange("p (i b j) -> p b i j", i=K, b=NP),
                                   yps[(4 * r + g) % YB][:, :].rearrange("p (b i j) -> p b i j", b=NP, i=K),
                                   ACT.Identity, bias=b0[:, o:o + 1]).then_inc(y_copied, 1)
                if more:
                    if r == 0:
                        act.wait_ge(norm_ready, i + 2)
                    regroup(i + 1, r, 0)

            def fill_xp(at, r):
                for n in range(2):
                    act.wait_ge(tp_filled, at + n + 1)
                    act.activation(xp[:, NP * r + 4 * n:NP * r + 4 * n + 4, :].rearrange("p (k g) c -> p k (g c)", k=2),
                                   tps[n][:, :, 0:2 * C], ACT.Identity).then_inc(evac_act, 1)

            def regroup(i, a, img):
                if a < NP - 1:
                    act.wait_ge(x_loaded, (i * (NP - 1) + a) * 32 + 16 * (img + 1))
                else:
                    act.wait_ge(xlast_loaded, i * 32 + 32)
                for t in range(NT):
                    k = img * NT + t
                    src = xraw[:, t, :] if a < NP - 1 else xlast[:, img, t, :]
                    act.activation(xc[:, t, a, :, img, :].rearrange("p b (i j) -> p b i j", i=K),
                                   src.rearrange("p (i b j) -> p b i j", i=K, b=NP),
                                   ACT.Identity, scale=rstd[:, k:k + 1], bias=nbias[:, k:k + 1]).then_inc(x_grouped, 1)

            def count_x(i, row):
                act.wait_ge(stat_loaded, (i * NP + row) * 16 + 16)
                act.wait_ge(xstat_added, i * NP + row)
                for k in range(2 * NT):
                    v = ysb[:, k // NT, k % NT, :]
                    act.activation(xjc[:, :, :, :, :].rearrange("p t b i n -> p (t b i n)")[:, k * ROW:(k + 1) * ROW], v,
                                   ACT.Identity, accum_out=xsum[:, k, 0:1]).then_inc(xsum_read, 1)
                    act.wait_ge(xsum_read, (i * NP + row) * (2 * NT) + k + 1)
                    act.activation(v, v, ACT.Square, accum_out=xsum[:, k, 1:2]).then_inc(xstat_done, 1)

            def group_root(i):
                act.wait_ge(group_var, i + 1)
                act.activation(gstd[:, :], gst[:, :, 1], ACT.Sqrt, bias=eps[:, 0:1]).then_inc(group_std, 1)

            def pair(i, more):
                distances(i, False, 0, (0,))
                act.wait_ge(edist_var, i + 1)
                act.activation(estd[:, :], sps[:, 9:10], ACT.Sqrt, scale=HW / (HW - 1)).then_inc(edist_std, 1)
                distances(i, False, 0, (1,))
                if more:
                    count_x(i + 1, 0)
                with act.Fori(1, NP) as l:
                    distances(i, False, l)
                    if more:
                        count_x(i + 1, l)
                distances(i, True, 0)
                distances(i, True, 1, (0,))
                if more:
                    group_root(i + 1)
                distances(i, True, 1, (1,))
                for r in range(NP):
                    row(i, r, more)
                if more:
                    regroup(i + 1, NP - 1, 1)
                    fill_xp(first_fill(i) + fill_next(NP - 1), NP - 1)

            for a in range(NP):
                count_x(0, a)
            group_root(0)
            act.wait_ge(norm_ready, 1)
            for a in range(NP):
                for img in range(2):
                    regroup(0, a, img)
                if a > 0:
                    fill_xp(2 * (a - 1), a - 1)
            fill_xp(2 * (NP - 1), NP - 1)
            pairs_of(act, pair)

        @block.vector
        def _(dve):
            def line(i, along_rows, l, between=None):
                n = dve.snap(i * NL + (NP if along_rows else 0) + l)
                last = {}
                for half, us, off, made, done, known in ((0, PA, 0, pen_a, best_a, dist_a), (1, PB, NA, pen_b, best_b, dist_b)):
                    m = len(us)
                    if half == 1 and between:
                        between()
                    dve.wait_ge(known, n + 1)
                    dve.wait_ge(done, n * 2 * m)
                    dve.tensor_scalar(pen[:, off:off + m], dist[:, off:off + m], thresh[:, 0:1], -BIG,
                                      ALU.is_ge, ALU.mult).then_inc(made, 1)
                    dve.wait_ge(made, n + 1)
                    at = dve.snap(n * 2 * m)
                    count = 0
                    todo = []
                    for s in sorted({q - p for p, q in us}):
                        todo += [(u, p, q) for u, (p, q) in enumerate(us) if q - p == s]
                        todo += [(u, q, p) for u, (p, q) in enumerate(us) if q - p == s]
                    for u, p, q in todo:
                        dst, cand = line_of(best, along_rows, l, p, 1), line_of(xp, along_rows, l, q, 1)
                        own = dst
                        if p in last:
                            sm, base, c = last[p]
                            dve.wait_ge(sm, base + c)
                        elif not along_rows:
                            own = line_of(xp, along_rows, l, p, 1)
                        dve.scalar_tensor_tensor(dst, cand, pen[:, off + u:off + u + 1], own,
                                                 ALU.add, ALU.max).then_inc(done, 1)
                        count += 1
                        last[p] = (done, at, count)

            def count_y(i, r, img):
                base = dve.snap(i * (4 * NP) + 4 * r)
                dve.wait_ge(y_copied, base + 2 * (img + 1))
                for o in range(NT):
                    dve.bn_stats(yst[:, o, bass.ds(2 * r + img, 1), :].rearrange("p a s -> p (a s)"),
                                 ysb[:, img, o, :]).then_inc(y_counted, 1)

            def link(ins, s, value):
                ins.then_inc(s, 1)
                dve.wait_ge(s, value)

            def add_x(i, row, first=False):
                dve.wait_ge(xstat_done, (i * NP + row + 1) * (2 * NT))
                if first:
                    dve.tensor_copy(xacc[:, :, :], xsum[:, :, :]).then_inc(xstat_added, 1)
                else:
                    dve.wait_ge(xstat_added, i * NP + row)
                    dve.tensor_tensor(xacc[:, :, :], xacc[:, :, :], xsum[:, :, :], ALU.add).then_inc(xstat_added, 1)

            def channel_stats(i):
                dve.wait_ge(xstat_added, (i + 1) * NP)
                dve.tensor_scalar(mv[:, :, :], xacc[:, :, :], 1.0 / HW, None, ALU.mult).then_inc(chan_stats, 1)

            def group_variance(i, first=False):
                dve.wait_ge(group_sums, i + 1)
                if not first:
                    dve.wait_ge(x_grouped, i * (4 * NP))
                link(dve.tensor_copy(gst[:, :, :].rearrange("p k s -> p (k s)"), sps[0:TP, 0:4 * NT]), stat_step, i * GSTEPS + 1)
                link(dve.tensor_tensor(gtmp[:, :], gst[:, :, 0], gst[:, :, 0], ALU.mult), stat_step, i * GSTEPS + 2)
                dve.tensor_tensor(gst[:, :, 1], gst[:, :, 1], gtmp[:, :], ALU.subtract).then_inc(group_var, 1)

            def group_scale(i):
                dve.wait_ge(group_std, i + 1)
                link(dve.reciprocal(rstd[:, :], gstd[:, :]), stat_step, i * GSTEPS + 3)
                dve.scalar_tensor_tensor(nbias[:, :], gst[:, :, 0], -1.0, rstd[:, :], ALU.mult, ALU.mult).then_inc(norm_ready, 1)

            def half_roll(i, a):
                h = NP // 2
                dve.wait_ge(evac_act, first_fill(i) - FILLS + fill_next(a + h) + 2)
                for b in (0, h):
                    ins = dve.tensor_tensor(best[:, a * NP + b:a * NP + b + h, :],
                                            xp[:, (a + h) * NP + h - b:(a + h) * NP + 2 * h - b, :],
                                            xp[:, a * NP + b:a * NP + b + h, :], ALU.subtract)
                link(ins, edist_diff, i * h + a + 1)
                return dve.tensor_reduce(dist_e[:, a * NP:(a + 1) * NP], best[:, a * NP:(a + 1) * NP, :], AX.X, ALU.add,
                                         apply_absolute_value=True)

            def threshold(i):
                ins = half_roll(i, NP // 2 - 1)
                link(ins, edist_step, i * ESTEPS + 1)
                dve.tensor_reduce(esum[:, :], dist_e[:, :], AX.X, ALU.add).then_inc(edist_part, 1)
                dve.wait_ge(edist_mean, i + 1)
                link(dve.tensor_copy(emean[:, :], sps[:, 8:9]), edist_step, i * ESTEPS + 2)
                link(dve.tensor_scalar(dist_e[:, :], dist_e[:, :], emean[:, 0:1], None, ALU.subtract), edist_step, i * ESTEPS + 3)
                dve.tensor_tensor_reduce(out=dist_e[:, :], in0=dist_e[:, :], in1=dist_e[:, :], scale=1.0, scalar=0.0,
                                         op0=ALU.mult, op1=ALU.add, accum_out=esq[:, :]).then_inc(edist_sq, 1)
                dve.wait_ge(edist_std, i + 1)
                dve.tensor_tensor(thresh[:, :], emean[:, :], estd[:, :], ALU.subtract).then_inc(edist_part, 1)
                dve.wait_ge(edist_part, 2 * i + 2)

            def pair(i, more):
                threshold(i)
                line(i, False, 0)
                if more:
                    add_x(i + 1, 0, True)
                with dve.Fori(1, NP) as l:
                    line(i, False, l)
                    if more:
                        add_x(i + 1, l)
                dve.wait_ge(best_b, (i * NL + NP) * 2 * NB)
                if more:
                    channel_stats(i + 1)
                line(i, True, 0, (lambda: group_variance(i + 1)) if more else None)
                if more:
                    group_scale(i + 1)
                line(i, True, 1)
                with dve.Fori(2, NP) as l:
                    line(i, True, l, lambda: count_y(i, l - 2, 0))
                    count_y(i, l - 2, 1)
                count_y(i, NP - 2, 0)
                if more:
                    half_roll(i + 1, 0)
                count_y(i, NP - 2, 1)
                if more:
                    half_roll(i + 1, 1)
                count_y(i, NP - 1, 0)
                if more:
                    half_roll(i + 1, 2)
                count_y(i, NP - 1, 1)
                dve.wait_ge(y_counted, (i + 1) * (4 * NP))
                dve.memset(ymv[:, :, 0], float(2 * HW))
                for o in range(NT):
                    ins = dve.bn_aggr(ymv[:, o, 1:3], yst[:, o, :, :].rearrange("p a s -> p (a s)"))
                ins.then_inc(bn_step, 1)
                dve.wait_ge(bn_step, 1 + 2 * i)
                dve.tensor_copy(yagg[:, :, bass.ds(i, 1), 0:2].rearrange("p o a s -> p o (a s)"), ymv[:, :, 0:2])
                dve.tensor_scalar(yagg[:, :, bass.ds(i, 1), 2].rearrange("p o a -> p (o a)"), ymv[:, :, 2],
                                  float(2 * HW), None, ALU.mult).then_inc(bn_step, 1)
                dve.wait_ge(bn_step, 2 + 2 * i)
            dve.wait_ge(const_loaded, 16 * 5)
            for a in range(NP):
                add_x(0, a, a == 0)
            channel_stats(0)
            group_variance(0, True)
            group_scale(0)
            dve.wait_ge(evac_act, 2 * NP)
            for a in range(3):
                half_roll(0, a)
            pairs_of(dve, pair)
            for o in range(NT):
                ins = dve.bn_aggr(ybn[:, o, :], yagg[:, o, :, :].rearrange("p a s -> p (a s)"))
            ins.then_inc(bn_ready, 1)

        @block.tensor
        def _(pe):
            pe.wait_ge(const_loaded, 16 * 5)

            def group_average(i):
                pe.wait_ge(chan_stats, i + 1)
                pe.matmul(sps[0:TP, 0:4 * NT], group[:, :], mv[:, :, :].rearrange("p k s -> p (k s)"),
                          start=True, stop=True).then_inc(group_sums, 1)

            def to_pixels(at, i, a):
                pe.wait_ge(x_grouped, (i * NP + a) * 4 + 4)
                for n in range(2):
                    if not isinstance(at, int) or at + n > 1:
                        pe.wait_ge(evac_act, at + n - 1)
                    for g in range(4):
                        for t in range(NT):
                            src = xc[:, t, a, 4 * n + g, :, :].rearrange("p k n -> p (k n)")
                            ins = pe.transpose(tps[n][:, g // 2, (g % 2) * C + t * TP:(g % 2) * C + (t + 1) * TP],
                                               src, ident[0:TP, 0:TP])
                    ins.then_inc(tp_filled, 1)

            def pair(i, more):
                pe.wait_ge(edist_part, i * 2 + 1)
                pe.matmul(sps[:, 8:9], imgsum[:, :], esum[:, :], start=True, stop=True).then_inc(edist_mean, 1)
                pe.wait_ge(edist_sq, i + 1)
                pe.matmul(sps[:, 9:10], imgsum[:, :], esq[:, :], start=True, stop=True).then_inc(edist_var, 1)
                if more:
                    group_average(i + 1)
                for a in range(NP):
                    pe.wait_ge(xj_done, i * NP + a + 1)
                    for t in range(NT):
                        pe.wait_ge(evac_act, first_fill(i) + fill_back(a, more) + t - 1)
                        for b in range(NP):
                            ins = pe.transpose(tps[t][0:TP, b // 4, (b % 4) * 128:(b % 4 + 1) * 128],
                                               best[:, a * NP + b, t * TP:(t + 1) * TP], ident[:, :])
                        ins.then_inc(tp_filled, 1)
                    for g in range(4):
                        img, o = divmod(g, NT)
                        if more and a > 0 and g == 2:
                            to_pixels(first_fill(i) + fill_next(a - 1), i + 1, a - 1)
                        n = 4 * a + g
                        pe.wait_ge(y_copied, i * (4 * NP) + (n + 1 - YB if n >= YB else 0))
                        if g == 0:
                            pe.wait_ge(evac_act, first_fill(i) + fill_back(a, more) + 2)
                        for k in range(2 * NT):
                            t = k % NT
                            if k < NT:
                                rhs = xc[:, t, a, :, img, :]
                            else:
                                rhs = xjc[:, t, :, img, :]
                            ins = pe.matmul(yps[n % YB][:, :], w0[:, k, o * TP:(o + 1) * TP], rhs,
                                            start=(k == 0), stop=(k == 2 * NT - 1))
                        ins.then_inc(y_filled, 1)
                if more:
                    to_pixels(first_fill(i) + fill_next(NP - 1), i + 1, NP - 1)

            group_average(0)
            for a in range(NP):
                to_pixels(2 * a, 0, a)
            pairs_of(pe, pair)


CM = 16
C1 = 3 * CM
KW = S // 2 + 1
CH = HW // 8
NCH = HW // CH
H1 = int(S * math.cos(math.pi / 4))
H0 = (S - H1) // 2
FR = CM * S
RF = CM * KW
EW = FR + RF
BR = 8 * KW
BW = CH + BR
F32R, I32 = mybir.dt.float32r, mybir.dt.int32
HIGH = -4096
TWO_PI = 2 * math.pi
TWO_PI_HI = 6.28125
ROUND = 12582912.0
PIX = 2 * NT * NCH

FILLS = ([(n, c, "act") for n in ("s1f", "s1r") for c in range(4)]
         + [(n + p, c, e) for n in ("s2f", "s2r") for c in range(2) for p, e in (("_re", "act"), ("_im", "dve"))]
         + [("outer", 0, "dve"), ("inner", 0, "dve"), ("phase", 0, "act"), ("rmod", 0, "act"), ("rang", 0, "act"),
            ("outer", 1, "dve"), ("inner", 1, "dve"), ("mod", 0, "act"),
            ("phase", 1, "act"), ("rmod", 1, "act"), ("rang", 1, "act"), ("mod", 1, "act")]
         + [("s3f", c, "act" if c % 2 else "dve") for c in range(4)] + [("s3r", c, "act" if c % 2 else "dve") for c in range(4)]
         + [("s4f" + p, c, "act") for c in range(2) for p in ("_re", "_im")] + [("s4r", c, "dve") for c in range(2)])
NF = len(FILLS)
INDEX = {(n, c): k for k, (n, c, _) in enumerate(FILLS)}
TAKES = {e: sum(x == e for _, _, x in FILLS) for e in ("act", "dve")}
GA, GM, SA = 8, 4, 26


def takes(e, name, c):
    return sum(x == e for _, _, x in FILLS[:INDEX[name, c] + 1])


D_S1F, D_S1R, D_S2F, D_S2R, D_S3F, D_S3R, D_S4F, D_S4R, D_N = 0, 1, 2, 5, 8, 9, 10, 13, 15
M_TAP, M_UP, M_DOWN, M_OUTER, M_MOD, M_PHASE, M_REAL, M_N = 0, 9, 12, 15, 16, 17, 18, 19


def layer1(nc, sems, x, y_d, bn_d, affine_d, group_d, conv1_d, conv2_d, c0w_d, c0b_d, mix_d, bias_d, mask_d, dft_d, out,
           v_d, f_d, r_d, g_d, p_d, z_d, w_d):
    B = x.shape[0]
    PAIRS = B // 2
    xv = x.rearrange("b (t p) h w -> p b t (h w)", p=TP)
    ov = out.rearrange("b (t p) h w -> p b t (h w)", p=TP)
    yv = y_d.rearrange("b (t p) n -> p b t n", p=TP)

    ZC = 2 * CH
    with ExitStack() as ctx:
        def sb(name, shape):
            return ctx.enter_context(nc.sbuf_tensor(name, shape, F32))

        def ps(name, shape):
            return ctx.enter_context(nc.psum_tensor(name, shape, F32))

        def sem(name):
            return sems.enter_context(nc.semaphore("l1_" + name))

        x1 = [sb(f"x1_{n}", [TP, 2, NT, HW]) for n in range(2)]
        ra, rb = sb("ra", [128, 2 * EW]), sb("rb", [128, 6 * CH + 4 * BR])
        with ExitStack() as shared:
            ring = shared.enter_context(nc.sbuf_tensor("ring", [TP, 4, CH], F32))
            rc = shared.enter_context(nc.sbuf_tensor("rc", [128, 2 * EW], F32))
        zin = sb("zin", [2 * C1, 4 * CH + 2 * EW])
        xw = ra[:, 0:2 * FR].rearrange("p (c h) -> p c h", h=S)
        x0, x0_hi = ra[:, 2 * FR:3 * FR], ra[:, 0:FR]
        mod, ang = ra[:, 0:EW], ra[:, EW:2 * EW]
        im2, re2 = ra[:, 0:2 * BW], ra[:, 2 * BW:4 * BW]
        zt = ra[:, 0:2 * FR].rearrange("p (c h) -> p c h", h=S)
        a1f = rb[:, 0:2 * FR].rearrange("p (c r n) -> p c r n", r=2, n=S)
        a1r = rb[:, 2 * FR:2 * FR + 2 * RF].rearrange("p (c r n) -> p c r n", r=2, n=KW)
        magb = rb[:, 0:2 * CH].rearrange("p (i n) -> p i n", i=2)
        magi = rb[:, 2 * CH:4 * CH].rearrange("p (i n) -> p i n", i=2)
        mixu = rb[:, 0:2 * CH].rearrange("p (i r n) -> p i r n", i=2, r=8)
        mixt = rb[:, 2 * CH:4 * CH].rearrange("p (i m) -> p i m", i=2)[:, :, 0:8 * H1].rearrange("p i (r n) -> p i r n", r=8)
        angb = rb[:, 4 * CH:6 * CH].rearrange("p (i n) -> p i n", i=2)
        rblk = rb[:, 6 * CH:6 * CH + 4 * BR].rearrange("p (i s n) -> p i s n", i=2, s=2)
        h1f = rb[:, 0:2 * FR].rearrange("p (c r n) -> p c r n", r=2, n=S)
        h1r = rb[:, 2 * FR:4 * FR].rearrange("p (c r n) -> p c r n", r=2, n=S)
        vch = rb[0:C1, 0:8 * CH].rearrange("p (k n) -> p k n", k=8)
        re, im = rc[:, 0:EW], rc[:, EW:2 * EW]
        mo = rc[:, 0:2 * BW].rearrange("p (i n) -> p i n", i=2)
        ph = rc[:, 2 * BW:4 * BW].rearrange("p (i n) -> p i n", i=2)
        gt = rc[:, 0:2 * FR].rearrange("p (i c n) -> p i c n", i=2, n=S)
        pt = rc[:, 2 * FR:2 * FR + 2 * RF].rearrange("p (i c n) -> p i c n", i=2, n=KW)
        sq = rc[:, 0:2 * FR].rearrange("p (r n) -> p r n", r=2)
        zch = [zin[:, 4 * CH + n * ZC:4 * CH + (n + 1) * ZC] for n in range(3)] + [zin[:, 0:ZC]]
        z_hi = (rc[:, 2 * FR:3 * FR], ra[:, 2 * FR:3 * FR])

        group = sb("l1_group", [TP, TP])
        conv1 = sb("conv1", [TP, NT, C1])
        conv1s = sb("conv1s", [TP, 2 * NT, C1])
        conv2 = sb("conv2", [C1, C])
        conv2_hi = sb("conv2_hi", [C1, C])
        conv2s = sb("conv2s", [2 * C1, 2, C])
        conv2a = sb("conv2a", [CM, C])
        c0w, c0b = sb("c0w", [CM, CM]), sb("c0b", [CM, 1])
        mix = sb("mix", [128, M_N, 128])
        bias = sb("bias", [128, 5])
        mask = sb("mask", [128, 2, 8, S])
        dft = sb("dft", [128, D_N, 128])
        bnp = sb("bnp", [TP, NT, 2])
        affine = sb("affine", [TP, 2, NT])
        bns = sb("bns", [TP, NT, 2])
        cbias = sb("cbias", [TP, NT])
        eps = sb("l1_eps", [TP, 1])
        half_pi = sb("half_pi", [128, 1])
        st = sb("st", [TP, 2 * NT, NCH, 6])
        mv = sb("l1_mv", [TP, 2 * NT, 2])
        gst = sb("l1_gst", [TP, 2 * NT, 2])
        gtmp = sb("l1_gtmp", [TP, 2 * NT])
        gstd = sb("l1_gstd", [TP, 2 * NT])
        rstd = sb("l1_rstd", [TP, 2 * NT])
        vbias = sb("vbias", [C1, 2])

        cps = [ps(f"cps{n}", [TP, CH]) for n in range(4)]
        stage = [ps(f"stage{n}", [128, 512]) for n in range(3)]
        gps = ps("gps", [128, 512])

        const_loaded, eps_set, set_up, setup_sum = sem("const_loaded"), sem("eps_set"), sem("set_up"), sem("setup_sum")
        setup_step = sem("setup_step")
        x_loaded = [sem(f"x_loaded{n}") for n in range(2)]
        y_loaded = [sem(f"y_loaded{n}") for n in range(4)]
        gelu_done, x1_done, x1_counted, stat_step = sem("gelu_done"), sem("x1_done"), sem("x1_counted"), sem("stat_step")
        chan_stats, group_sums, group_var, group_std = sem("chan_stats"), sem("group_sums"), sem("group_var"), sem("group_std")
        w_scaled, vbias_sum, vbias_done = sem("w_scaled"), sem("vbias_sum"), sem("vbias_done")
        v_filled, v_copied = sem("v_filled"), sem("v_copied")
        v_stored = [sem(f"v_stored{n}") for n in range(4)]
        xw_loaded, filled = sem("xw_loaded"), sem("filled")
        taken = {"act": sem("taken_act"), "dve": sem("taken_dve")}
        squared, sq_summed, mod_done, ratio_done, atan_done = sem("squared"), sem("sq_summed"), sem("mod_done"), sem("ratio_done"), sem("atan_done")
        ew_step, re_abs, ang_done, masked = sem("ew_step"), sem("re_abs"), sem("ang_done"), sem("masked")
        fmod_stored, rmod_stored, ang_stored = sem("fmod_stored"), sem("rmod_stored"), sem("ang_stored")
        fmod_loaded, rmod_loaded, ang_loaded = sem("fmod_loaded"), sem("rmod_loaded"), sem("ang_loaded")
        mixed, turn_done, abs_done, sin_done, g_done = sem("mixed"), sem("turn_done"), sem("abs_done"), sem("sin_done"), sem("g_done")
        g_stored, g_loaded, z_summed, z_abs = sem("g_stored"), sem("g_loaded"), sem("z_summed"), sem("z_abs")
        x0_loaded, x0_split, x0_stored, z_split = sem("x0_loaded"), sem("x0_split"), sem("x0_stored"), sem("z_split")
        w2_split, w2_stored, w2_loaded, split_step = sem("w2_split"), sem("w2_stored"), sem("w2_loaded"), sem("split_step")
        z_stored = sem("z_stored")
        z_loaded = [sem(f"z_loaded{n}") for n in range(4)]
        o_filled, o_added = sem("o_filled"), sem("o_added")
        o_stored = [sem(f"o_stored{n}") for n in range(2)]

        passed = {e: sem("passed_" + e) for e in ("sp", "pe")}

        block = ctx.enter_context(nc.Block())
        NCONST = 12

        def wait_fill(eng, i, k):
            eng.wait_ge(filled, i * NF + k + 1)

        def place(k):
            return k // (NT * NCH), (k // NCH) % NT, k % NCH

        def pairs_of(eng, body):
            if PAIRS > 2:
                body(0, 0, True)
                body(1, 1, True)
            if PAIRS > 4:
                with eng.Fori(1, PAIRS // 2 - 1) as j:
                    body(eng.snap(2 * j), 0, True)
                    body(eng.snap(2 * j + 1), 1, True)
            body(PAIRS - 2, 0, True)
            body(PAIRS - 1, 1, False)

        @block.sync
        def _(sp):
            def wait(semaphore, value):
                value = sp.snap(value)
                sp.wait_ge(semaphore, value)
                sp.sem_inc(passed["sp"], 1)

            def load_x(i, slot, img):
                ni = sp.snap(2 * i + img)
                if not isinstance(i, int) or i >= 2:
                    wait(o_stored[img], 16 * (i - 1))
                sp.dma_start(x1[slot][:, img, :, :], xv[:, bass.ds(ni, 1), :, :].rearrange("p b t n -> p (b t) n")
                             ).then_inc(x_loaded[img], 16)

            def store_out(i, slot, img):
                ni = sp.snap(2 * i + img)
                wait(o_added, i * PIX + 16 * (img + 1))
                sp.dma_start(ov[:, bass.ds(ni, 1), :, :].rearrange("p b t n -> p (b t) n"), x1[slot][:, img, :, :]
                             ).then_inc(o_stored[img], 16)

            def store_v(i, d):
                img, q = divmod(2 * d, NCH)
                ni = sp.snap(2 * i + img)
                wait(v_copied, i * (2 * NCH) + 2 * d + 2)
                sp.dma_start(v_d[bass.ds(ni, 1), :, q * CH:(q + 2) * CH].rearrange("b c n -> (b c) n"),
                             vch[:, 2 * (d % 4):2 * (d % 4) + 2, :].rearrange("p k n -> p (k n)")).then_inc(v_stored[d % 4], 16)

            def load_xw(i):
                for n in range(4):
                    wait(v_stored[n], i * 32 + 32)
                for img in range(2):
                    ni = sp.snap(2 * i + img)
                    sp.dma_start(xw[img * S:(img + 1) * S, :, :], v_d[bass.ds(ni, 1), CM:C1, :].rearrange("b c (w h) -> w (b c) h", h=S)
                                 ).then_inc(xw_loaded, 16)
                for img in range(2):
                    ni = sp.snap(2 * i + img)
                    sp.dma_start(x0[img * S:(img + 1) * S, :].rearrange("p (c h) -> p c h", h=S),
                                 v_d[bass.ds(ni, 1), 0:CM, :].rearrange("b c (w h) -> w (b c) h", h=S)).then_inc(x0_loaded, 16)

            def store_z(b, branch, hi, lo, done):
                for img in range(2):
                    for n, part in enumerate((hi, lo)):
                        sp.dma_start(z_d[bass.ds(b[img], 1), n, branch * CM:(branch + 1) * CM, :, :].rearrange("b c w h -> (b w) c h"),
                                     part[img * S:(img + 1) * S, :].rearrange("p (c h) -> p c h", h=S)).then_inc(done, 16)

            def load_z(b, m):
                img, q = divmod(m, 4)
                sp.dma_start(zch[m % 4], z_d[bass.ds(b[img], 1), :, :, 16 * q:16 * q + 16, :].rearrange("b s c w h -> (b s c) (w h)")
                             ).then_inc(z_loaded[m % 4], 16)

            def chain(i, slot, more):
                b = [sp.snap(2 * i + img) for img in range(2)]
                rows = [slice(img * S, (img + 1) * S) for img in range(2)]
                wait(x0_split, 2 * i + 2)
                store_z(b, 0, x0_hi, x0, x0_stored)

                def store_f(s, part, img, n):
                    sp.dma_start(f_d[bass.ds(b[img], 1), s, :, :, :].rearrange("b c h w -> (b h) c w"),
                                 part[rows[img], 0:FR].rearrange("p (c n) -> p c n", n=S)).then_inc(n, 16)

                def store_r(s, part, img, n):
                    sp.dma_start(r_d[bass.ds(b[img], 1), s, :, :, :].rearrange("b c h w -> (b h) c w"),
                                 part[rows[img], FR:EW].rearrange("p (c n) -> p c n", n=KW)).then_inc(n, 16)

                def load_f(s, dst, img, n):
                    sp.dma_start(dst[:, img, :], f_d[bass.ds(b[img], 1), s, :, :, :].rearrange("b c (k r) w -> (b c k) (r w)", r=8)
                                 ).then_inc(n, 16)

                def load_r(s, img, n):
                    sp.dma_start(rblk[:, img, s, :], r_d[bass.ds(b[img], 1), s, :, :, :].rearrange("b c (k r) w -> (b c k) (r w)", r=8)
                                 ).then_inc(n, 16)

                wait(mod_done, 2 * i + 1)
                for img in range(2):
                    store_f(0, mod, img, fmod_stored)
                wait(mod_done, 2 * i + 2)
                for img in range(2):
                    store_r(0, mod, img, rmod_stored)
                wait(fmod_stored, 32 * i + 32)
                for img in range(2):
                    load_f(0, magb, img, fmod_loaded)
                wait(rmod_stored, 32 * i + 32)
                for img in range(2):
                    load_r(0, img, rmod_loaded)
                if not isinstance(i, int) or i > 0:
                    store_out(i - 1, 1 - slot, 1)
                wait(ang_done, 2 * i + 1)
                for img in range(2):
                    store_f(1, ang, img, ang_stored)
                wait(ang_done, 2 * i + 2)
                for img in range(2):
                    store_r(1, ang, img, ang_stored)
                wait(ang_stored, 64 * i + 64)
                for img in range(2):
                    load_f(1, angb, img, ang_loaded)
                    load_r(1, img, ang_loaded)
                if more:
                    load_x(i + 1, 1 - slot, 1)
                for img in range(2):
                    wait(g_done, 2 * i + img + 1)
                    for ri, part in ((0, re2), (1, im2)):
                        sp.dma_start(g_d[bass.ds(b[img], 1), ri, :, :, :].rearrange("b c (k r) w -> (b c k) (r w)", r=8),
                                     part[:, img * BW:img * BW + CH]).then_inc(g_stored, 16)
                        sp.dma_start(p_d[bass.ds(b[img], 1), ri, :, :, :].rearrange("b c (k r) w -> (b c k) (r w)", r=8),
                                     part[:, img * BW + CH:(img + 1) * BW]).then_inc(g_stored, 16)
                wait(g_stored, 128 * i + 128)
                for img in range(2):
                    for ri in range(2):
                        sp.dma_start(gt[rows[ri], img, :, :], g_d[bass.ds(b[img], 1), ri, :, :, :].rearrange("b c h w -> (b h) c w")
                                     ).then_inc(g_loaded, 16)
                for img in range(2):
                    for ri in range(2):
                        sp.dma_start(pt[rows[ri], img, :, :], p_d[bass.ds(b[img], 1), ri, :, :, :].rearrange("b c h w -> (b h) c w")
                                     ).then_inc(g_loaded, 16)
                zf = zt.rearrange("p c h -> p (c h)")
                wait(z_split, 2 * i + 1)
                store_z(b, 2, z_hi[1], zf[:, FR:2 * FR], z_stored)
                wait(z_split, 2 * i + 2)
                store_z(b, 1, z_hi[0], zf[:, 0:FR], z_stored)
                if more:
                    for d in range(3):
                        store_v(i + 1, d)
                wait(z_stored, 128 * i + 128)
                for m in range(4):
                    if m == 3:
                        wait(x1_done, (i + 2 if more else i + 1) * PIX)
                    load_z(b, m)
                if more:
                    for d in range(3, 8):
                        store_v(i + 1, d)
                    load_xw(i + 1)
                for m in range(4, 8):
                    wait(o_filled, i * PIX + 4 * (m - 3))
                    load_z(b, m)
                store_out(i, slot, 0)
                if not isinstance(i, int) or i + 2 < PAIRS:
                    load_x(i + 2, slot, 0)

            consts = [(group[:, :], group_d), (conv1[:, :, :], conv1_d), (conv2[:, :], conv2_d), (conv2a[:, :], conv2_d[0:CM, :]),
                      (c0w[:, :], c0w_d), (c0b[:, :], c0b_d), (mix[:, :, :], mix_d), (bias[:, :], bias_d),
                      (mask[:, :, :, :], mask_d), (dft[:, :, :], dft_d), (bnp[:, :, :], bn_d), (affine[:, :, :], affine_d)]
            for dst, src in consts:
                sp.dma_start(dst, src).then_inc(const_loaded, 16)
            assert len(consts) == NCONST
            for img in range(2):
                load_x(0, 0, img)
            for s, n in ((conv2_hi, 0), (conv2, 1)):
                wait(w2_split, n + 1)
                sp.dma_start(w_d[n], s[:, :]).then_inc(w2_stored, 16)
            wait(w2_stored, 32)
            for r in range(2):
                sp.dma_start(conv2s[r * C1:(r + 1) * C1, :, :], w_d.rearrange("s p c -> p s c")).then_inc(w2_loaded, 16)
            for d in range(8):
                store_v(0, d)
            load_xw(0)
            load_x(1, 1, 0)
            pairs_of(sp, chain)
            store_out(PAIRS - 1, 1, 1)
            for n in range(2):
                sp.wait_ge(o_stored[n], 16 * PAIRS)

        @block.gpsimd
        def _(pool):
            pool.memset(eps[:, :], 1e-5).then_inc(eps_set, 1)
            pool.memset(half_pi[:, :], math.pi / 2).then_inc(eps_set, 1)

            def add(i, slot):
                for k in range(PIX):
                    img, t, q = place(k)
                    if k % (PIX // 2) == 0:
                        pool.wait_ge(x_loaded[img], 16 * i + 16)
                    dst = x1[slot][:, img, t, q * CH:(q + 1) * CH]
                    pool.wait_ge(gelu_done, i * PIX + k + 1)
                    pool.tensor_tensor(dst, dst, ring[:, k % 4, :], ALU.add).then_inc(x1_done, 1)

            def chain(i, slot, more):
                pool.wait_ge(fmod_loaded, 32 * i + 32)
                for img in range(2):
                    pool.tensor_tensor(magi[:, img, :], magb[:, img, :], mask[:, 0, :, :].rearrange("p r n -> p (r n)"), ALU.mult
                                       ).then_inc(masked, 1)
                    pool.wait_ge(masked, 4 * i + 2 * img + 1)
                    pool.tensor_tensor(magb[:, img, :], magb[:, img, :], mask[:, 1, :, :].rearrange("p r n -> p (r n)"), ALU.mult
                                       ).then_inc(masked, 1)
                if more:
                    add(i + 1, 1 - slot)

            pool.wait_ge(const_loaded, 16 * NCONST)
            add(0, 0)
            pairs_of(pool, chain)

        @block.scalar
        def _(act):
            def take(i, k, out_ap, in_ap, func=ACT.Identity, **kw):
                wait_fill(act, i, k)
                act.activation(out_ap, in_ap, func, **kw).then_inc(taken["act"], 1)

            def load_y(i, k):
                img, t, q = place(k)
                ni, n = act.snap(2 * i + img), act.snap(i * PIX + max(k - 3, 0))
                act.wait_ge(x1_done, n)
                act.dma_start(ring[:, k % 4, :], yv[:, bass.ds(ni, 1), t, q * CH:(q + 1) * CH].rearrange("p b n -> p (b n)")
                              ).then_inc(y_loaded[k % 4], 16)

            def gelu(i, k0, k1):
                for k in range(k0, k1):
                    img, t, q = place(k)
                    act.wait_ge(y_loaded[k % 4], i * (4 * PIX) + 16 * (k // 4 + 1))
                    act.activation(ring[:, k % 4, :], ring[:, k % 4, :], ACT.Gelu, scale=bns[:, t, 0:1], bias=bns[:, t, 1:2]
                                   ).then_inc(gelu_done, 1)
                    if k + 2 < PIX:
                        load_y(i, k + 2)

            def copy_v(i):
                act.wait_ge(vbias_done, i + 1)
                for k in range(2 * NCH):
                    img, q = divmod(k, NCH)
                    act.wait_ge(v_filled, i * (2 * NCH) + k + 1)
                    if k >= 8 and k % 2 == 0:
                        act.wait_ge(v_stored[(k // 2) % 4], i * 32 + 16)
                    act.activation(vch[:, k % 8, :], cps[k % 4][0:C1, :], ACT.Identity, bias=vbias[:, img:img + 1]).then_inc(v_copied, 1)

            def group_root(i):
                act.wait_ge(group_var, i + 1)
                act.activation(gstd[:, :], gst[:, :, 1], ACT.Sqrt, bias=eps[:, 0:1]).then_inc(group_std, 1)

            def first_takes(i):
                for n, dst, w in (("s1f", a1f, 512), ("s1r", a1r, 8 * KW)):
                    for c in range(4):
                        k = INDEX[n, c]
                        take(i, k, dst[:, 4 * c:4 * c + 4, :, :].rearrange("p c r n -> p (c r n)"), stage[k % 3][:, 0:w])

            def chain(i, slot, more):
                if more:
                    act.wait_ge(o_filled, i * PIX)
                    for k in range(2):
                        load_y(i + 1, k)
                for h, (n, cols, w) in enumerate((("s2f", slice(0, FR), 512), ("s2r", slice(FR, EW), 8 * KW))):
                    for c in range(2):
                        k = INDEX[n + "_re", c]
                        at = cols.start + c * w
                        take(i, k, re[:, at:at + w], stage[k % 3][:, 0:w])
                    act.wait_ge(taken["act"], i * TAKES["act"] + takes("act", n + "_re", 1))
                    if h == 0:
                        act.wait_ge(x0_stored, 64 * i + 64)
                    act.activation(mod[:, cols], re[:, cols], ACT.Square).then_inc(squared, 1)
                    act.wait_ge(taken["dve"], i * TAKES["dve"] + takes("dve", n + "_im", 1))
                    act.activation(ang[:, cols], im[:, cols], ACT.Square).then_inc(squared, 1)
                for h, cols in enumerate((slice(0, FR), slice(FR, EW))):
                    act.wait_ge(sq_summed, 2 * i + h + 1)
                    act.activation(mod[:, cols], mod[:, cols], ACT.Sqrt).then_inc(mod_done, 1)
                    act.activation(ang[:, cols], re[:, cols], ACT.Abs).then_inc(re_abs, 1)
                for h, cols in enumerate((slice(0, FR), slice(FR, EW))):
                    act.wait_ge(ratio_done, 2 * i + h + 1)
                    act.activation(ang[:, cols], ang[:, cols], ACT.Arctan).then_inc(atan_done, 1)
                if more:
                    gelu(i + 1, 0, GA)
                for img in range(2):
                    part = slice(img * BW, (img + 1) * BW)

                    def mod_take():
                        k = INDEX["mod", img]
                        take(i, k, mo[:, img, 0:CH], stage[k % 3][:, :], bias=bias[:, 2:3])

                    for n, dst, w, kw in (("phase", ph[:, img, 0:CH], CH, dict(scale=2.0, bias=bias[:, 3:4])),
                                          ("rmod", mo[:, img, CH:BW], BR, dict(bias=bias[:, 4:5])),
                                          ("rang", ph[:, img, CH:BW], BR, dict(scale=2.0, bias=bias[:, 4:5]))):
                        k = INDEX[n, img]
                        take(i, k, dst, stage[k % 3][:, 0:w], **kw)
                    if more:
                        gelu(i + 1, GA + img * GM, GA + (img + 1) * GM)
                    if img:
                        mod_take()
                    act.wait_ge(turn_done, 2 * i + img + 1)
                    act.activation(re2[:, part], im2[:, part], ACT.Abs).then_inc(abs_done, 1)
                    act.wait_ge(abs_done, 2 * i + img + 1)
                    act.activation(re2[:, part], re2[:, part], ACT.Sin, scale=-1.0, bias=half_pi[:, 0:1]).then_inc(sin_done, 1)
                    act.activation(im2[:, part], im2[:, part], ACT.Sin).then_inc(sin_done, 1)
                    if not img:
                        mod_take()
                if more:
                    gelu(i + 1, GA + 2 * GM, PIX)
                for n, dst, p in (("s3f", h1f, 128), ("s3r", h1r, KW)):
                    for c in (1, 3):
                        k = INDEX[n, c]
                        wait_fill(act, i, k)
                        if p == 128:
                            act.activation(dst[:, 4 * c:4 * c + 4, :, :].rearrange("p c r n -> p (c r n)"), stage[k % 3][:, :],
                                           ACT.Identity).then_inc(taken["act"], 1)
                        else:
                            for img in range(2):
                                rows = slice(img * S, img * S + KW)
                                ins = act.activation(dst[rows, 4 * c:4 * c + 4, :, :].rearrange("p c r n -> p (c r n)"),
                                                     stage[k % 3][rows, :], ACT.Identity)
                            ins.then_inc(taken["act"], 1)
                for c in range(2):
                    for r, n in enumerate(("s4f_re", "s4f_im")):
                        k = INDEX[n, c]
                        take(i, k, sq[:, r, c * 512:(c + 1) * 512], stage[k % 3][:, :], ACT.Square)
                for c in range(2):
                    act.wait_ge(z_summed, 2 * i + c + 1)
                    act.activation(zt[:, 8 * c:8 * c + 8, :].rearrange("p c n -> p (c n)"), sq[:, 0, c * 512:(c + 1) * 512], ACT.Sqrt
                                   ).then_inc(z_abs, 1)
                if more:
                    group_root(i + 1)
                    copy_v(i + 1)
                    first_takes(i + 1)

            act.wait_ge(eps_set, 2)
            act.wait_ge(const_loaded, 16 * NCONST)
            act.activation(bns[:, :, 0], bnp[:, :, 1], ACT.Sqrt, bias=eps[:, 0:1]).then_inc(set_up, 1)
            act.wait_ge(set_up, 3)
            for k in range(2):
                load_y(0, k)
            gelu(0, 0, PIX)
            group_root(0)
            copy_v(0)
            first_takes(0)
            pairs_of(act, chain)

        @block.vector
        def _(dve):
            count = {"ew": 0, "stat": 0}
            EW_STEPS, STAT_STEPS = 17, 6

            def link(ins, i, what):
                count[what] += 1
                s, n = (ew_step, EW_STEPS) if what == "ew" else (stat_step, STAT_STEPS)
                ins.then_inc(s, 1)
                dve.wait_ge(s, i * n + count[what])

            def split(hi, v, s, n):
                dve.tensor_scalar(hi.bitcast(I32), v.bitcast(I32), HIGH, None, ALU.bitwise_and).then_inc(s, 1)
                dve.wait_ge(s, n + 1)
                dve.tensor_tensor(v, v, hi, ALU.subtract).then_inc(s, 1)

            def take(i, k, out_ap, in_ap):
                wait_fill(dve, i, k)
                dve.tensor_copy(out_ap, in_ap).then_inc(taken["dve"], 1)

            def stats(i, slot, k0, k1):
                for k in range(k0, k1):
                    img, t, q = place(k)
                    dve.wait_ge(x1_done, i * PIX + k + 1)
                    dve.bn_stats(st[:, img * NT + t, q, :], x1[slot][:, img, t, q * CH:(q + 1) * CH]).then_inc(x1_counted, 1)

            def group_stats(i):
                count["stat"] = 0
                dve.wait_ge(x1_counted, (i + 1) * PIX)
                dve.memset(gtmp[:, :], 0.0)
                for k in range(2 * NT):
                    ins = dve.bn_aggr(mv[:, k, :], st[:, k, :, :].rearrange("p a s -> p (a s)"))
                link(ins, i, "stat")
                link(dve.tensor_tensor(gtmp[:, :], mv[:, :, 0], mv[:, :, 0], ALU.mult), i, "stat")
                dve.tensor_tensor(mv[:, :, 1], mv[:, :, 1], gtmp[:, :], ALU.add).then_inc(chan_stats, 1)
                dve.wait_ge(group_sums, i + 1)
                link(dve.tensor_copy(gst[:, :, :].rearrange("p k s -> p (k s)"), gps[0:TP, 0:4 * NT]), i, "stat")
                link(dve.tensor_tensor(gtmp[:, :], gst[:, :, 0], gst[:, :, 0], ALU.mult), i, "stat")
                dve.tensor_tensor(gst[:, :, 1], gst[:, :, 1], gtmp[:, :], ALU.subtract).then_inc(group_var, 1)
                dve.wait_ge(group_std, i + 1)
                link(dve.reciprocal(rstd[:, :], gstd[:, :]), i, "stat")
                for k in range(2 * NT):
                    ins = dve.tensor_scalar(conv1s[:, k, :], conv1[:, k % NT, :], rstd[:, k:k + 1], None, ALU.mult)
                ins.then_inc(w_scaled, 1)
                dve.wait_ge(vbias_sum, i + 1)
                link(dve.tensor_scalar(vbias[:, :], gps[0:C1, 16:18], -1.0, None, ALU.mult), i, "stat")
                dve.tensor_copy(gtmp[:, 0:1], rstd[:, 0:1]).then_inc(vbias_done, 1)
                assert count["stat"] == STAT_STEPS

            def chain(i, slot, more):
                count["ew"] = 0
                dve.wait_ge(x0_loaded, 32 * i + 32)
                wait_fill(dve, i, INDEX["s1r", 3])
                split(x0_hi, x0, x0_split, 2 * i)
                halves = (slice(0, FR), slice(FR, EW))
                for n, off, w in (("s2f", 0, 512), ("s2r", FR, 8 * KW)):
                    for c in range(2):
                        k = INDEX[n + "_im", c]
                        take(i, k, im[:, off + c * w:off + (c + 1) * w], stage[k % 3][:, 0:w])
                for h, cols in enumerate(halves):
                    dve.wait_ge(squared, 4 * i + 2 * h + 2)
                    dve.tensor_tensor(mod[:, cols], mod[:, cols], ang[:, cols], ALU.add).then_inc(sq_summed, 1)
                for h, cols in enumerate(halves):
                    dve.wait_ge(mod_done, 2 * i + h + 1)
                    dve.wait_ge(re_abs, 2 * i + h + 1)
                    link(dve.scalar_tensor_tensor(ang[:, cols], ang[:, cols], 1e-30, mod[:, cols], ALU.max, ALU.add), i, "ew")
                    link(dve.reciprocal(ang[:, cols], ang[:, cols]), i, "ew")
                    dve.tensor_tensor(ang[:, cols], im[:, cols], ang[:, cols], ALU.mult).then_inc(ratio_done, 1)
                dve.wait_ge(ratio_done, 2 * i + 2)
                link(dve.tensor_scalar(im, im, 0.0, -0.5, ALU.is_ge, ALU.add), i, "ew")
                for h, cols in enumerate(halves):
                    dve.wait_ge(atan_done, 2 * i + h + 1)
                    link(dve.scalar_tensor_tensor(im[:, cols], ang[:, cols], -2.0 / math.pi, im[:, cols], ALU.mult, ALU.add), i, "ew")
                    link(dve.scalar_tensor_tensor(re[:, cols], re[:, cols], 0.0, im[:, cols], ALU.is_lt, ALU.mult), i, "ew")
                    dve.scalar_tensor_tensor(ang[:, cols], re[:, cols], math.pi, ang[:, cols], ALU.mult, ALU.add).then_inc(ang_done, 1)
                inner = slice(H0, H0 + H1)

                def masked_sum(img):
                    k = INDEX["outer", img]
                    wait_fill(dve, i, k)
                    dve.scalar_tensor_tensor(mixu[:, img, :, :].rearrange("p r n -> p (r n)"), stage[k % 3][:, :], bias[:, 1:2],
                                             mask[:, 1, :, :].rearrange("p r n -> p (r n)"), ALU.add, ALU.mult).then_inc(taken["dve"], 1)
                    k = INDEX["inner", img]
                    wait_fill(dve, i, k)
                    dve.scalar_tensor_tensor(mixt[:, img, :, :], stage[k % 3][:, 0:8 * H1].rearrange("p (r n) -> p r n", n=H1),
                                             bias[:, 0:1], mask[:, 0, :, inner], ALU.add, ALU.mult).then_inc(taken["dve"], 1)
                    dve.wait_ge(taken["dve"], i * TAKES["dve"] + takes("dve", "inner", img))
                    dve.tensor_tensor(mixu[:, img, :, inner], mixu[:, img, :, inner], mixt[:, img, :, :], ALU.add).then_inc(mixed, 1)

                def turn(img):
                    dve.wait_ge(taken["act"], i * TAKES["act"] + takes("act", "rang", img))
                    q, phase = slice(img * BW, (img + 1) * BW), ph[:, img, :]
                    link(dve.tensor_scalar(im2[:, q], phase, 1.0 / TWO_PI, ROUND, ALU.mult, ALU.add), i, "ew")
                    link(dve.tensor_scalar(im2[:, q], im2[:, q], ROUND, None, ALU.subtract), i, "ew")
                    link(dve.scalar_tensor_tensor(re2[:, q], im2[:, q], -TWO_PI_HI, phase, ALU.mult, ALU.add), i, "ew")
                    link(dve.scalar_tensor_tensor(im2[:, q], im2[:, q], -(TWO_PI - TWO_PI_HI), re2[:, q], ALU.mult, ALU.add), i, "ew")
                    dve.tensor_scalar(im2[:, q], im2[:, q], 3.1415925, -3.1415925, ALU.min, ALU.max).then_inc(turn_done, 1)

                def parts(img):
                    dve.wait_ge(taken["act"], i * TAKES["act"] + takes("act", "mod", img))
                    q = slice(img * BW, (img + 1) * BW)
                    for n, part in enumerate((re2, im2)):
                        dve.wait_ge(sin_done, 4 * i + 2 * img + n + 1)
                        ins = dve.tensor_tensor(part[:, q], part[:, q], mo[:, img, :], ALU.mult)
                    ins.then_inc(g_done, 1)

                masked_sum(0)
                turn(0)
                masked_sum(1)
                parts(0)
                turn(1)
                parts(1)
                if more:
                    stats(i + 1, 1 - slot, 0, SA)
                for n, dst, p in (("s3f", h1f, 128), ("s3r", h1r, KW)):
                    for c in (0, 2):
                        k = INDEX[n, c]
                        wait_fill(dve, i, k)
                        if p == 128:
                            dve.tensor_copy(dst[:, 4 * c:4 * c + 4, :, :].rearrange("p c r n -> p (c r n)"), stage[k % 3][:, :]
                                            ).then_inc(taken["dve"], 1)
                        else:
                            for img in range(2):
                                rows = slice(img * S, img * S + KW)
                                ins = dve.tensor_copy(dst[rows, 4 * c:4 * c + 4, :, :].rearrange("p c r n -> p (c r n)"),
                                                      stage[k % 3][rows, :])
                            ins.then_inc(taken["dve"], 1)
                for c in range(2):
                    dve.wait_ge(taken["act"], i * TAKES["act"] + takes("act", "s4f_im", c))
                    cols = slice(c * 512, (c + 1) * 512)
                    dve.tensor_tensor(sq[:, 0, cols], sq[:, 0, cols], sq[:, 1, cols], ALU.add).then_inc(z_summed, 1)
                for c in range(2):
                    k = INDEX["s4r", c]
                    wait_fill(dve, i, k)
                    dve.tensor_copy(zt[:, CM + 8 * c:CM + 8 * c + 8, :].rearrange("p c n -> p (c n)"), stage[k % 3][:, :]
                                    ).then_inc(taken["dve"], 1)
                dve.wait_ge(taken["dve"], (i + 1) * TAKES["dve"])
                zf = zt.rearrange("p c h -> p (c h)")
                for n, (hi, v) in enumerate(((z_hi[1], zf[:, FR:2 * FR]), (z_hi[0], zf[:, 0:FR]))):
                    if n:
                        dve.wait_ge(z_abs, 2 * i + 2)
                    dve.tensor_scalar(hi.bitcast(I32), v.bitcast(I32), HIGH, None, ALU.bitwise_and).then_inc(split_step, 1)
                    dve.wait_ge(split_step, 2 * i + n + 1)
                    dve.tensor_tensor(v, v, hi, ALU.subtract).then_inc(z_split, 1)
                if more:
                    stats(i + 1, 1 - slot, SA, PIX)
                    group_stats(i + 1)
                for j in range(2 * NCH):
                    img, q = divmod(j, NCH)
                    for t in range(NT):
                        dve.wait_ge(o_filled, i * PIX + 2 * j + t + 1)
                        dst = x1[slot][:, img, t, :].rearrange("p (h w) -> p w h", w=S)[:, 8 * q:8 * q + 8, :]
                        dve.scalar_tensor_tensor(dst, cps[(2 * j + t) % 4][:, :].rearrange("p (w h) -> p w h", h=S), cbias[:, t:t + 1], dst,
                                                 ALU.add, ALU.add).then_inc(o_added, 1)
                assert count["ew"] == EW_STEPS

            dve.wait_ge(set_up, 1)
            dve.reciprocal(bns[:, :, 0], bns[:, :, 0]).then_inc(setup_step, 1)
            dve.wait_ge(setup_step, 1)
            dve.tensor_tensor(bns[:, :, 0], bns[:, :, 0], affine[:, 0, :], ALU.mult).then_inc(setup_step, 1)
            dve.wait_ge(setup_step, 2)
            dve.tensor_tensor(bns[:, :, 1], bns[:, :, 0], bnp[:, :, 0], ALU.mult).then_inc(setup_step, 1)
            dve.wait_ge(setup_step, 3)
            dve.tensor_tensor(bns[:, :, 1], affine[:, 1, :], bns[:, :, 1], ALU.subtract).then_inc(set_up, 1)
            dve.wait_ge(setup_sum, 1)
            dve.tensor_copy(conv2[0:CM, :], gps[0:CM, 32:32 + C])
            dve.tensor_copy(cbias[:, :], gps[0:TP, 20:22]).then_inc(set_up, 1)
            dve.wait_ge(set_up, 3)
            split(conv2_hi[:, :], conv2[:, :], w2_split, 0)
            stats(0, 0, 0, PIX)
            group_stats(0)
            pairs_of(dve, chain)

        @block.tensor
        def _(pe):
            def fill(i, k, products):
                before = k - 3
                if before >= 0:
                    e = FILLS[before][2]
                    pe.wait_ge(taken[e], i * TAKES[e] + sum(x == e for _, _, x in FILLS[:before + 1]))
                else:
                    e = FILLS[before][2]
                    pe.wait_ge(taken[e], i * TAKES[e])
                if products[0][1].shape[0] <= S and products[0][0].shape[0] <= S:
                    pe.sem_inc(passed["pe"], 1)
                for args in products:
                    ins = pe.matmul(*args[:3], start=args[3], stop=args[4])
                ins.then_inc(filled, 1)

            def conv_first(i, slot):
                pe.wait_ge(chan_stats, i + 1)
                pe.matmul(gps[0:TP, 0:4 * NT], group[:, :], mv[:, :, :].rearrange("p k s -> p (k s)"), start=True, stop=True
                          ).then_inc(group_sums, 1)
                pe.wait_ge(w_scaled, i + 1)
                for img in range(2):
                    for t in range(NT):
                        ins = pe.matmul(gps[0:C1, 16 + img:17 + img], conv1s[:, img * NT + t, :], gst[:, img * NT + t, 0:1],
                                        start=(t == 0), stop=(t == NT - 1))
                ins.then_inc(vbias_sum, 1)
                for k in range(2 * NCH):
                    img, q = divmod(k, NCH)
                    if k < 4:
                        if not isinstance(i, int) or i >= 2:
                            pe.wait_ge(o_added, (i - 1) * PIX)
                    else:
                        pe.wait_ge(v_copied, i * (2 * NCH) + k - 3)
                    for t in range(NT):
                        rhs = x1[slot][:, img, t, :].rearrange("p (h w) -> p w h", w=S)[:, 8 * q:8 * q + 8, :]
                        ins = pe.matmul(cps[k % 4][0:C1, :], conv1s[:, img * NT + t, :], rhs, start=(t == 0), stop=(t == NT - 1))
                    ins.then_inc(v_filled, 1)

            def first_step(i, n):
                if n == 0:
                    pe.wait_ge(xw_loaded, 32 * i + 32)
                name, w, c0, d = (("s1f", 128, 0, D_S1F), ("s1r", 2 * KW, CM, D_S1R))[n // 4]
                c = n % 4
                k = INDEX[name, c]
                fill(i, k, [(stage[k % 3][img * S:(img + 1) * S, w * g:w * (g + 1)], xw[img * S:(img + 1) * S, c0 + 4 * c + g, :],
                                     dft[img * S:(img + 1) * S, d, 0:w], True, True) for g in range(4) for img in range(2)])

            def chain(i, slot, more):
                pe.wait_ge(taken["act"], i * TAKES["act"] + takes("act", "s1r", 3))
                for name, src, d, w in (("s2f", a1f, D_S2F, S), ("s2r", a1r, D_S2R, KW)):
                    for c in range(2):
                        r, m = src[:, 8 * c:8 * c + 8, 0, :], src[:, 8 * c:8 * c + 8, 1, :]
                        for part, terms in (("_re", ((d, r), (d + 2, m))), ("_im", ((d + 1, r), (d, m)))):
                            k = INDEX[name + part, c]
                            fill(i, k, [(stage[k % 3][:, 0:8 * w], dft[:, dd, :], rhs, n == 0, n == 1) for n, (dd, rhs) in enumerate(terms)])
                def outer_inner(img):
                    pe.wait_ge(masked, 4 * i + 2 * img + 2)
                    k = INDEX["outer", img]
                    fill(i, k, [(stage[k % 3][:, :], mix[:, M_OUTER, :], magb[:, img, :], True, True)])
                    k = INDEX["inner", img]
                    o = stage[k % 3][:, 0:8 * H1].rearrange("p (r n) -> p r n", n=H1)
                    src = magi[:, img, :].rearrange("p (r n) -> p r n", n=S)

                    def cols(dx):
                        return slice(H0 + dx - 1, H0 + dx - 1 + H1)

                    prods = [(o, mix[:, M_TAP + 3 + dx, :], src[:, :, cols(dx)], dx == 0, False) for dx in range(3)]
                    prods += [(o[:, 1:8, :], mix[:, M_TAP + dx, :], src[:, 0:7, cols(dx)], False, False) for dx in range(3)]
                    prods += [(o[:, 0:7, :], mix[:, M_TAP + 6 + dx, :], src[:, 1:8, cols(dx)], False, False) for dx in range(3)]
                    prods += [(o[:, 0, :], mix[:, M_UP + dx, :], src[:, 7, cols(dx)], False, False) for dx in range(3)]
                    prods += [(o[:, 7, :], mix[:, M_DOWN + dx, :], src[:, 0, cols(dx)], False, dx == 2) for dx in range(3)]
                    fill(i, k, prods)

                def channels(img):
                    for name, m, rhs, w, loaded in (("phase", M_PHASE, angb[:, img, :], CH, (ang_loaded, 64)),
                                                    ("rmod", M_REAL, rblk[:, img, 0, :], BR, (rmod_loaded, 32)),
                                                    ("rang", M_REAL, rblk[:, img, 1, :], BR, (ang_loaded, 64))):
                        k = INDEX[name, img]
                        pe.wait_ge(loaded[0], (i + 1) * loaded[1])
                        fill(i, k, [(stage[k % 3][:, 0:w], mix[:, m, :], rhs, True, True)])

                def modulus(img):
                    k = INDEX["mod", img]
                    pe.wait_ge(mixed, 2 * i + img + 1)
                    fill(i, k, [(stage[k % 3][:, :], mix[:, M_MOD, :], mixu[:, img, :, :].rearrange("p r n -> p (r n)"), True, True)])

                outer_inner(0)
                channels(0)
                outer_inner(1)
                modulus(0)
                channels(1)
                modulus(1)
                pe.wait_ge(g_loaded, (i + 1) * 128)
                for name, src, n, d in (("s3f", gt, S, D_S3F), ("s3r", pt, KW, D_S3R)):
                    for c in range(4):
                        k = INDEX[name, c]
                        fill(i, k, [(stage[k % 3][img * S:img * S + n, 128 * g:128 * (g + 1)], src[:, img, 4 * c + g, :], dft[:, d, :], True, True)
                                    for g in range(4) for img in range(2)])
                for e, c in (("act", 3), ("dve", 2)):
                    pe.wait_ge(taken[e], i * TAKES[e] + takes(e, "s3r", c))
                for c in range(2):
                    r, m = h1f[:, 8 * c:8 * c + 8, 0, :], h1f[:, 8 * c:8 * c + 8, 1, :]
                    for part, terms in (("_re", ((D_S4F, r), (D_S4F + 2, m))), ("_im", ((D_S4F + 1, r), (D_S4F, m)))):
                        k = INDEX["s4f" + part, c]
                        fill(i, k, [(stage[k % 3][:, :], dft[:, dd, :], rhs, n == 0, n == 1) for n, (dd, rhs) in enumerate(terms)])
                for c in range(2):
                    k = INDEX["s4r", c]
                    fill(i, k, [(stage[k % 3][img * S:(img + 1) * S, :], dft[img * S:img * S + KW, D_S4R + r, 0:S],
                                 h1r[img * S:img * S + KW, 8 * c:8 * c + 8, r, :], r == 0, r == 1) for img in range(2) for r in range(2)])
                if more:
                    conv_first(i + 1, 1 - slot)
                pe.wait_ge(w2_loaded, 32)
                for m in range(8):
                    if more and 3 <= m < 7:
                        for n in range(2):
                            first_step(i + 1, 2 * (m - 3) + n)
                    pe.wait_ge(z_loaded[m % 4], i * 32 + 16 * (m // 4 + 1))
                    for n in range(4 * m, 4 * m + 4):
                        t = n % 2
                        if n < 4:
                            pe.wait_ge(v_copied, (i + 2 if more else i + 1) * (2 * NCH))
                            if not more:
                                pe.wait_ge(o_added, i * PIX)
                        else:
                            pe.wait_ge(o_added, i * PIX + n - 3)
                        half = (n // 2) % 2
                        for part in range(2):
                            ins = pe.matmul(cps[n % 4][:, :], conv2s[:, part, t * TP:(t + 1) * TP].bitcast(F32R),
                                            zch[m % 4][:, half * CH:(half + 1) * CH].bitcast(F32R), start=part == 0, stop=part == 1)
                        ins.then_inc(o_filled, 1)

            pe.wait_ge(const_loaded, 16 * NCONST)
            pe.matmul(gps[0:CM, 32:32 + C], c0w[:, :], conv2a[:, :], start=True, stop=True)
            for t in range(NT):
                ins = pe.matmul(gps[0:TP, 20 + t:21 + t], conv2a[:, t * TP:(t + 1) * TP], c0b[:, :], start=True, stop=True)
            ins.then_inc(setup_sum, 1)
            conv_first(0, 0)
            for n in range(8):
                first_step(0, n)
            pairs_of(pe, chain)


def frft_matrix(N, a):
    shift = None
    if a < 0.5:
        shft = (np.arange(N) + int(np.fix(N / 2))) % N
        inv = np.argsort(shft)
        W = np.exp(2j * np.pi * np.outer(np.arange(N), np.arange(N)) / N) / math.sqrt(N)
        shift = W[inv, :][:, inv]
        a = a + 1.0
    alpha = a * math.pi / 2
    tana2, sina = math.tan(alpha / 2), math.sin(alpha)
    up = np.zeros((2 * N - 1, N))
    up[::2] = np.eye(N)
    kern = np.sinc(np.arange(-(2 * N - 3), 2 * N - 2) / 2.0)
    fi = np.stack([np.convolve(up[:, k], kern)[2 * N - 3:4 * N - 4] for k in range(N)], 1)
    fp = np.concatenate([np.zeros((N - 1, N)), fi, np.zeros((N - 1, N))], 0).astype(complex)
    n = np.arange(-2 * N + 2, 2 * N - 1).astype(float)
    chrp = np.exp(-1j * math.pi / N * tana2 / 4 * n ** 2)
    fp = chrp[:, None] * fp
    c = math.pi / N / sina / 4
    m = np.arange(-(4 * N - 4), 4 * N - 3).astype(float)
    kern = np.exp(1j * c * m ** 2)
    ret = np.stack([np.convolve(fp[:, k], kern)[4 * N - 4:8 * N - 7] for k in range(N)], 1) * math.sqrt(c / math.pi)
    ret = chrp[:, None] * ret
    M = np.exp(-1j * (1 - a) * math.pi / 4) * ret[N - 1:3 * N - 2:2]
    return M @ shift if shift is not None else M


def transforms():
    T, U = frft_matrix(S, 0.5), frft_matrix(S, -0.5)
    k = np.arange(S)
    turn = (np.outer(k, k) % S)
    cos, sin = np.round(np.cos(2 * np.pi * turn / S), 15), np.round(np.sin(2 * np.pi * turn / S), 15)
    d = np.zeros((128, D_N, 128))
    for img in range(2):
        r = slice(img * S, (img + 1) * S)
        d[r, D_S1F, :] = np.concatenate([T.real.T, T.imag.T], 1)
        d[r, D_S1R, 0:2 * KW] = np.concatenate([cos[:, 0:KW], -sin[:, 0:KW]], 1)
        for slot, a, b in ((D_S2F, T.real, T.imag), (D_S2R, cos, -sin), (D_S4F, U.real, U.imag)):
            d[r, slot, r], d[r, slot + 1, r], d[r, slot + 2, r] = a.T, b.T, -b.T
        c = np.full((KW, 1), 2.0 / S)
        c[0] = c[-1] = 1.0 / S
        d[img * S:img * S + KW, D_S4R, 0:S] = c * cos[0:KW]
        d[img * S:img * S + KW, D_S4R + 1, 0:S] = -c * sin[0:KW]
    for slot, a, b in ((D_S3F, U.real, U.imag), (D_S3R, cos / S, sin / S)):
        d[:, slot, :] = np.block([[a.T, b.T], [-b.T, a.T]])
    return (d + 0.0).astype(np.float32)


def masks():
    m = np.zeros((S, S), np.float32)
    m[H0:H0 + H1, H0:H0 + H1] = 1.0
    m = np.tile(m.reshape(8, 8, S), (CM, 1, 1))
    return np.stack([m, 1 - m], 1)


def spread(w, shift=0):
    m = np.zeros((CM, 8, CM, 8), w.dtype)
    for b in range(8):
        if 0 <= b + shift < 8:
            m[:, b, :, b + shift] = w.T
    return m.reshape(128, 128)


def mixing(mag_s_w, mag_f_w, mag_w, pha_w, conv_1_w):
    taps = [spread(mag_s_w[:, :, dy, dx]) for dy in range(3) for dx in range(3)]
    up = [spread(mag_s_w[:, :, 0, dx], 1) for dx in range(3)]
    down = [spread(mag_s_w[:, :, 2, dx], -1) for dx in range(3)]
    return np.ascontiguousarray(np.stack(taps + up + down + [spread(mag_f_w), spread(mag_w), spread(pha_w), spread(conv_1_w)], 1))


def biases(*b):
    return np.stack([np.repeat(x, 8) for x in b], 1)


def two_layers(nc, x, w0, b0, ident, group, imgsum, affine, conv1, conv2, c0w, c0b, mix, bias, mask, dft, out):
    B = x.shape[0]

    def scratch(name, shape):
        return nc.dram_tensor(name, shape, F32, kind="Internal").ap()

    y_d, bn_d = scratch("y_d", [B, C, HW]), scratch("bn_d", [TP, NT, 2])
    with ExitStack() as sems:
        layer0_conv(nc, sems, x, w0, b0, ident, group, imgsum, y_d, bn_d)
        layer1(nc, sems, x, y_d, bn_d, affine, group, conv1, conv2, c0w, c0b, mix, bias, mask, dft, out,
               scratch("v_d", [B, C1, HW]), scratch("f_d", [B, 2, CM, S, S]), scratch("r_d", [B, 2, CM, S, KW]),
               scratch("g_d", [B, 2, CM, S, S]), scratch("p_d", [B, 2, CM, S, KW]), scratch("z_d", [B, 2, C1, S, S]),
               scratch("w_d", [2, C1, C]))


def kernel(**inputs):
    import concourse.bacc as _bacc
    from concourse.bass_utils import run_bass_kernel_spmd as _run

    a = {k.replace("L0_conv_", "").replace("L1_conv_", ""): np.asarray(v) for k, v in inputs.items()}

    def by_tile(v):
        return v.reshape(NT, TP).T

    ins = {
        "x": a["x"],
        "w0": a["conv_w"].T.reshape(2 * NT, TP, C).transpose(1, 0, 2),
        "b0": by_tile(a["conv_b"]),
        "ident": np.eye(128, dtype=np.float32),
        "group": np.kron(np.eye(TP // 6), np.full((6, 6), 1 / 6)).astype(np.float32),
        "imgsum": np.kron(np.eye(2), np.full((S, S), 2.0 / HW)).astype(np.float32),
        "affine": np.stack([by_tile(a["bn_gamma"]), by_tile(a["bn_beta"])], 1),
        "conv1": a["conv1_w"].T.reshape(NT, TP, C1).transpose(1, 0, 2),
        "conv2": a["conv2_w"].T,
        "c0w": a["conv_0_w"],
        "c0b": a["conv_0_b"][:, None],
        "mix": mixing(a["mag_s_w"], a["mag_f_w"], a["mag_w"], a["pha_w"], a["conv_1_w"]),
        "bias": biases(a["mag_s_b"], a["mag_f_b"], a["mag_b"], a["pha_b"], a["conv_1_b"]),
        "mask": masks(),
        "dft": transforms(),
    }
    nc = _bacc.Bacc("TRN2", target_bir_lowering=False, num_devices=1)
    arrays, args = {}, []
    for name, v in ins.items():
        arrays[f"in_{name}_dram"] = np.ascontiguousarray(v)
        args.append(nc.dram_tensor(f"in_{name}_dram", v.shape, mybir.dt.from_np(v.dtype), kind="ExternalInput").ap())
    args.append(nc.dram_tensor("out_0_dram", a["x"].shape, F32, kind="ExternalOutput").ap())
    two_layers(nc, *args)
    r = _run(nc, [arrays], core_ids=[0])
    return r.results[0]["out_0_dram"]
```
